# Optimizing a Trainium2 kernel written in Bass

```python
import numpy as np
import jax
import jax.numpy as jnp

def _softmax(x, axis=-1):
    return jax.nn.softmax(x, axis=axis)

def _gelu(x):
    return jax.nn.gelu(x, approximate=True)

def _silu(x):
    return jax.nn.silu(x)

def _sigmoid(x):
    return jax.nn.sigmoid(x)

def _layernorm(x, axis=-1, eps=1e-05):
    m = jnp.mean(x, axis=axis, keepdims=True)
    v = jnp.var(x, axis=axis, keepdims=True)
    return (x - m) / jnp.sqrt(v + eps)

def _scatter_add(tgt, idx, src, axis=0):
    return tgt.at[idx].add(src)

def _segment_sum(src, seg, n):
    return jax.ops.segment_sum(src, seg, n)
kernel_name = 'mk_sandwich_d1_jaxref_r4_2e5e98'

def setup_inputs(seed: int=0):
    np.random.seed(seed)
    _w = jnp.asarray

    def _L0_attn_setup():
        import jax, jax.numpy as jnp
        import numpy as np
        D = 256
        H = 16
        KVH = 4
        HD = D // H
        LAT = 64
        WIN = 64
        B, S = (1, 512)
        BASE_G, BASE_L = (1000000.0, 10000.0)
        EPS = 1e-06

        def rmsnorm(x, w):
            return x * jax.lax.rsqrt(jnp.mean(x * x, axis=-1, keepdims=True) + EPS) * w

        def qk_norm(x):
            return x * jax.lax.rsqrt(jnp.mean(x * x, axis=-1, keepdims=True) + EPS)

        def rope(x, base):
            s, hd = (x.shape[-2], x.shape[-1])
            inv_freq = 1.0 / base ** (jnp.arange(0, hd, 2, dtype=jnp.float32) / hd)
            freqs = jnp.arange(s, dtype=jnp.float32)[:, None] * inv_freq[None, :]
            cos, sin = (jnp.cos(freqs), jnp.sin(freqs))
            xe, xo = (x[..., ::2], x[..., 1::2])
            out = jnp.stack([xe * cos - xo * sin, xe * sin + xo * cos], axis=-1)
            return out.reshape(x.shape)

        def split_heads(x, n_heads):
            b, s, _ = x.shape
            return x.reshape(b, s, n_heads, HD).transpose(0, 2, 1, 3)

        def repeat_kv(x):
            return jnp.repeat(x, H // KVH, axis=1)

        def sdpa(q, k, v, mask):
            scores = jnp.einsum('bhqd,bhkd->bhqk', q, k) / np.sqrt(HD).astype(np.float32)
            scores = jnp.where(mask, scores, jnp.float32(-1e+30))
            probs = jax.nn.softmax(scores, axis=-1)
            return jnp.einsum('bhqk,bhkd->bhqd', probs, v)

        def merge_heads(x):
            b, h, s, hd = x.shape
            return x.transpose(0, 2, 1, 3).reshape(b, s, h * hd)

        def global_latent_attn(x, wq, w_kv_down, w_k_up, w_v_up, wo):
            q = split_heads(x @ wq, H)
            latent = x @ w_kv_down
            k = split_heads(latent @ w_k_up, KVH)
            v = split_heads(latent @ w_v_up, KVH)
            q, k = (rope(q, BASE_G), rope(k, BASE_G))
            q, k = (qk_norm(q), qk_norm(k))
            k, v = (repeat_kv(k), repeat_kv(v))
            i = jnp.arange(x.shape[1])
            causal = i[:, None] >= i[None, :]
            return merge_heads(sdpa(q, k, v, causal)) @ wo

        def local_gqa_attn(x, wq, wk, wv, wo):
            q = split_heads(x @ wq, H)
            k = split_heads(x @ wk, KVH)
            v = split_heads(x @ wv, KVH)
            q, k = (rope(q, BASE_L), rope(k, BASE_L))
            q, k = (qk_norm(q), qk_norm(k))
            k, v = (repeat_kv(k), repeat_kv(v))
            i = jnp.arange(x.shape[1])
            diff = i[:, None] - i[None, :]
            mask = (diff >= 0) & (diff < WIN)
            return merge_heads(sdpa(q, k, v, mask)) @ wo
        key = jax.random.key(seed)
        ks = jax.random.split(key, 12)
        std = 0.02
        return {'hidden': jax.random.normal(ks[0], (B, S, D), dtype=jnp.float32), 'norm1_w': jnp.ones((D,), jnp.float32), 'norm2_w': jnp.ones((D,), jnp.float32), 'g_wq': jax.random.normal(ks[1], (D, H * HD), jnp.float32) * std, 'g_kv_down': jax.random.normal(ks[2], (D, LAT), jnp.float32) * std, 'g_k_up': jax.random.normal(ks[3], (LAT, KVH * HD), jnp.float32) * std, 'g_v_up': jax.random.normal(ks[4], (LAT, KVH * HD), jnp.float32) * std, 'g_wo': jax.random.normal(ks[5], (D, D), jnp.float32) * std, 'l_wq': jax.random.normal(ks[6], (D, H * HD), jnp.float32) * std, 'l_wk': jax.random.normal(ks[7], (D, KVH * HD), jnp.float32) * std, 'l_wv': jax.random.normal(ks[8], (D, KVH * HD), jnp.float32) * std, 'l_wo': jax.random.normal(ks[9], (D, D), jnp.float32) * std}
    _L0_attn_in = _L0_attn_setup()

    def _L0_ffn_setup():
        import jax, jax.numpy as jnp
        import numpy as np
        E = 8
        K = 2
        D = 256
        F = 1024
        key = jax.random.key(seed)
        k1, k2, k3, k4, k5 = jax.random.split(key, 5)
        s = 0.02
        return {'x': jax.random.normal(k1, (2, 512, D), dtype=jnp.float32), 'gate_w': jax.random.normal(k2, (D, E), dtype=jnp.float32) * s, 'w1': jax.random.normal(k3, (E, D, F), dtype=jnp.float32) * s, 'w2': jax.random.normal(k4, (E, F, D), dtype=jnp.float32) * s, 'w3': jax.random.normal(k5, (E, D, F), dtype=jnp.float32) * s}
    _L0_ffn_in = _L0_ffn_setup()
    _d = {'L0_attn_hidden': _L0_attn_in['hidden'], 'L0_attn_norm1_w': _L0_attn_in['norm1_w'], 'L0_attn_norm2_w': _L0_attn_in['norm2_w'], 'L0_attn_g_wq': _L0_attn_in['g_wq'], 'L0_attn_g_kv_down': _L0_attn_in['g_kv_down'], 'L0_attn_g_k_up': _L0_attn_in['g_k_up'], 'L0_attn_g_v_up': _L0_attn_in['g_v_up'], 'L0_attn_g_wo': _L0_attn_in['g_wo'], 'L0_attn_l_wq': _L0_attn_in['l_wq'], 'L0_attn_l_wk': _L0_attn_in['l_wk'], 'L0_attn_l_wv': _L0_attn_in['l_wv'], 'L0_attn_l_wo': _L0_attn_in['l_wo'], 'L0_ffn_gate_w': _L0_ffn_in['gate_w'], 'L0_ffn_w1': _L0_ffn_in['w1'], 'L0_ffn_w2': _L0_ffn_in['w2'], 'L0_ffn_w3': _L0_ffn_in['w3']}
    _x0 = _d['L0_attn_hidden']
    _d['L0_attn_hidden'] = jax.random.normal(jax.random.fold_in(jax.random.key(seed), 1), (8, 512, 256), dtype=_x0.dtype)
    del _x0
    return _d

def reference(L0_attn_hidden, L0_attn_norm1_w, L0_attn_norm2_w, L0_attn_g_wq, L0_attn_g_kv_down, L0_attn_g_k_up, L0_attn_g_v_up, L0_attn_g_wo, L0_attn_l_wq, L0_attn_l_wk, L0_attn_l_wv, L0_attn_l_wo, L0_ffn_gate_w, L0_ffn_w1, L0_ffn_w2, L0_ffn_w3):

    def _L0_attn_ref(hidden, norm1_w, norm2_w, g_wq, g_kv_down, g_k_up, g_v_up, g_wo, l_wq, l_wk, l_wv, l_wo):
        import jax, jax.numpy as jnp
        import numpy as np
        D = 256
        H = 16
        KVH = 4
        HD = D // H
        LAT = 64
        WIN = 64
        B, S = (1, 512)
        BASE_G, BASE_L = (1000000.0, 10000.0)
        EPS = 1e-06

        def rmsnorm(x, w):
            return x * jax.lax.rsqrt(jnp.mean(x * x, axis=-1, keepdims=True) + EPS) * w

        def qk_norm(x):
            return x * jax.lax.rsqrt(jnp.mean(x * x, axis=-1, keepdims=True) + EPS)

        def rope(x, base):
            s, hd = (x.shape[-2], x.shape[-1])
            inv_freq = 1.0 / base ** (jnp.arange(0, hd, 2, dtype=jnp.float32) / hd)
            freqs = jnp.arange(s, dtype=jnp.float32)[:, None] * inv_freq[None, :]
            cos, sin = (jnp.cos(freqs), jnp.sin(freqs))
            xe, xo = (x[..., ::2], x[..., 1::2])
            out = jnp.stack([xe * cos - xo * sin, xe * sin + xo * cos], axis=-1)
            return out.reshape(x.shape)

        def split_heads(x, n_heads):
            b, s, _ = x.shape
            return x.reshape(b, s, n_heads, HD).transpose(0, 2, 1, 3)

        def repeat_kv(x):
            return jnp.repeat(x, H // KVH, axis=1)

        def sdpa(q, k, v, mask):
            scores = jnp.einsum('bhqd,bhkd->bhqk', q, k) / np.sqrt(HD).astype(np.float32)
            scores = jnp.where(mask, scores, jnp.float32(-1e+30))
            probs = jax.nn.softmax(scores, axis=-1)
            return jnp.einsum('bhqk,bhkd->bhqd', probs, v)

        def merge_heads(x):
            b, h, s, hd = x.shape
            return x.transpose(0, 2, 1, 3).reshape(b, s, h * hd)

        def global_latent_attn(x, wq, w_kv_down, w_k_up, w_v_up, wo):
            q = split_heads(x @ wq, H)
            latent = x @ w_kv_down
            k = split_heads(latent @ w_k_up, KVH)
            v = split_heads(latent @ w_v_up, KVH)
            q, k = (rope(q, BASE_G), rope(k, BASE_G))
            q, k = (qk_norm(q), qk_norm(k))
            k, v = (repeat_kv(k), repeat_kv(v))
            i = jnp.arange(x.shape[1])
            causal = i[:, None] >= i[None, :]
            return merge_heads(sdpa(q, k, v, causal)) @ wo

        def local_gqa_attn(x, wq, wk, wv, wo):
            q = split_heads(x @ wq, H)
            k = split_heads(x @ wk, KVH)
            v = split_heads(x @ wv, KVH)
            q, k = (rope(q, BASE_L), rope(k, BASE_L))
            q, k = (qk_norm(q), qk_norm(k))
            k, v = (repeat_kv(k), repeat_kv(v))
            i = jnp.arange(x.shape[1])
            diff = i[:, None] - i[None, :]
            mask = (diff >= 0) & (diff < WIN)
            return merge_heads(sdpa(q, k, v, mask)) @ wo
        x = hidden
        x = x + global_latent_attn(rmsnorm(x, norm1_w), g_wq, g_kv_down, g_k_up, g_v_up, g_wo)
        x = x + local_gqa_attn(rmsnorm(x, norm2_w), l_wq, l_wk, l_wv, l_wo)
        return x

    def _L0_ffn_ref(x, gate_w, w1, w2, w3):
        import jax, jax.numpy as jnp
        import numpy as np
        E = 8
        K = 2
        D = 256
        F = 1024
        xs = x.reshape(-1, x.shape[-1])
        gate_logits = xs @ gate_w
        topw, sel = jax.lax.top_k(gate_logits, K)
        topw = jax.nn.softmax(topw.astype(jnp.float32), axis=-1).astype(x.dtype)
        comb = (jax.nn.one_hot(sel, E, dtype=x.dtype) * topw[..., None]).sum(axis=1)
        out = jnp.zeros_like(xs)
        for i in range(E):
            h = jax.nn.silu(xs @ w1[i]) * (xs @ w3[i])
            out = out + comb[:, i:i + 1] * (h @ w2[i])
        return out.reshape(x.shape)
    x = L0_attn_hidden
    x = x + _layernorm(_L0_attn_ref(_layernorm(x, axis=-1), L0_attn_norm1_w, L0_attn_norm2_w, L0_attn_g_wq, L0_attn_g_kv_down, L0_attn_g_k_up, L0_attn_g_v_up, L0_attn_g_wo, L0_attn_l_wq, L0_attn_l_wk, L0_attn_l_wv, L0_attn_l_wo), axis=-1)
    x = x + _layernorm(_L0_ffn_ref(_layernorm(x, axis=-1), L0_ffn_gate_w, L0_ffn_w1, L0_ffn_w2, L0_ffn_w3), axis=-1)
    return x

_drawn_inputs = setup_inputs


def setup_inputs(seed=0):
    import zlib

    import numpy as np

    out = dict(_drawn_inputs(seed))
    spreads = {'L0_attn_norm1_w': (1.0, 0.6), 'L0_attn_norm2_w': (1.0, 0.582)}
    factors = {'L0_attn_g_wq': 5.176,
     'L0_attn_g_kv_down': 4.21,
     'L0_attn_g_k_up': 4.135,
     'L0_attn_g_v_up': 3.898,
     'L0_attn_g_wo': 4.508}
    for name, (base, spread) in spreads.items():
        noise = np.random.default_rng([zlib.crc32(name.encode()), seed]).standard_normal(out[name].shape)
        drawn = base * np.exp(spread * noise) if base else spread * noise
        out[name] = jnp.asarray(drawn.astype(out[name].dtype))
    for name, factor in factors.items():
        out[name] = (out[name] * factor).astype(out[name].dtype)
    return out
```

```python
from contextlib import ExitStack

import concourse.bass as bass
from concourse import mybir
import numpy as np

F32 = mybir.dt.float32
F32R = mybir.dt.float32r
BF16 = mybir.dt.bfloat16
U32 = mybir.dt.uint32
I32 = mybir.dt.int32
ALU = mybir.AluOpType
ACT = mybir.ActivationFunctionType
AX = mybir.AxisListType

P = 128
B, S, D = 8, 512, 256
H, KVH, HD, LAT = 16, 4, 16, 64
WIN = 64
E, F = 8, 1024
TT = S // P
DH = D // P
HPG = H // KVH
NQK = (H + KVH) * HD
NPROJ = NQK + KVH * HD
NTOK = B * S
MT = 256
REG = NTOK + MT
NTILES = 2 * NTOK // MT + E - 1
ROWS = E * REG + E * MT
EPS_LN, EPS_RMS = 1e-5, 1e-6
NEG = -1e30
SCALE = HD ** -0.5

CONST = {}
_at = 0
for _name, _n in (("ident", P), ("before", P), ("ones", P), ("mask0", P), ("mask1", P + WIN),
                  ("cos0", TT * HD), ("sin0", TT * HD), ("cos1", TT * HD), ("sin1", TT * HD),
                  ("expert", E), ("region", E), ("tile", NTILES + 2)):
    CONST[_name] = (_at, _n)
    _at += _n
NCONST = _at

CHUNKS = [[(0, 0, 2, 1), (0, 2, 2, 1), (1, 0, 2, 1), (1, 2, 2, 1), (2, 0, 4, 2), (3, 0, 4, 4)],
          [(0, 0, 4, 2), (1, 0, 4, 2), (2, 0, 4, 2), (3, 0, 4, 4)]]


def width(l, kt):
    return S - kt * P if l == 0 else min(S - kt * P, P + WIN)


NCH = [KVH * len(c) for c in CHUNKS]
UNITS = KVH * TT


def chunks_of(l, u):
    g, kt = divmod(u, TT)
    return [(g * len(CHUNKS[l]) + n, c) for n, c in enumerate(CHUNKS[l]) if c[0] == kt]


def unit_of(l, n):
    g, c = divmod(n, len(CHUNKS[l]))
    return g * TT + CHUNKS[l][c][0]


def order(l, b):
    if l == 0:
        return 0 if isinstance(b, int) and b == 0 else 2 * b - 1
    return 2 * B - 1 if isinstance(b, int) and b == B - 1 else 2 * b + 2


def first_chunk(l, b):
    if l == 0:
        return 0 if isinstance(b, int) and b == 0 else (b - 1) * sum(NCH) + NCH[0]
    if isinstance(b, int) and b == B - 1:
        return NCH[0] + (B - 1) * sum(NCH)
    return b * sum(NCH) + 2 * NCH[0]


class Steps:

    def __init__(self, eng, sem, per_batch, b):
        self.eng, self.sem, self.per_batch = eng, sem, per_batch
        self.base, self.n = b * per_batch, 0

    def did(self, ins):
        ins.then_inc(self.sem, 1)
        self.n += 1
        assert self.n <= self.per_batch
        return ins

    def settle(self):
        self.eng.wait_ge(self.sem, self.base + self.n)

    def end(self):
        assert self.n == self.per_batch, (self.n, self.per_batch)


def spread(ap, dims):
    return bass.AP(ap.tensor, ap.offset, [list(ap.ap[0])] + dims)


def attend(nc, A, dram):
    with ExitStack() as ctx:
        def sb(name, shape, dt=F32):
            return ctx.enter_context(nc.sbuf_tensor(name, shape, dt))

        def pb(name, shape, dt=F32):
            return ctx.enter_context(nc.psum_tensor(name, shape, dt))

        def sem(name):
            return ctx.enter_context(nc.semaphore(name))

        const, eps_ln, eps_rms = A["const"], A["eps_ln"], A["eps_rms"]
        counts, slot_f, top2 = A["counts"], A["slot_f"], A["top2"]

        def K(name, rows=P):
            at, n = CONST[name]
            return const[0:rows, at:at + n]

        ident = K("ident")
        ident_b = sb("ident_b", [P, P], BF16)
        before_b = sb("before_b", [P, P], BF16)
        ones_b = sb("ones_b", [P, P], BF16)
        zeros_b = sb("zeros_b", [P, P], BF16)
        mask_b = [sb(f"mask_b{l}", [P, CONST[f"mask{l}"][1]], BF16) for l in range(2)]
        W = [sb(f"W{l}", [P, DH, NPROJ]) for l in range(2)]
        WO = [sb(f"WO{l}", [P, KVH, D]) for l in range(2)]
        gate = sb("gate", [P, DH, E])
        normw = sb("normw", [P, 2, DH])
        down = sb("down", [P, DH, LAT])
        up = sb("up", [LAT, 2 * KVH * HD])
        downT = sb("downT", [LAT, DH, P])

        Xin = sb("Xin", [P, TT, D])
        Hs = sb("Hs", [P, 4 * TT * D])
        xn = sb("xn", [P, TT, D])
        xT = sb("xT", [P, DH, S])
        R = sb("R", [P, TT, NQK])
        T2 = sb("T2", [P, 2, NQK])
        SQ = sb("SQ", [P, 2, NQK])
        SS = sb("SS", [P, TT, H + KVH])
        RL = sb("RL", [P, TT, H + KVH])
        RS = sb("RS", [P, TT, H + KVH])
        hi_q = sb("hi_q", [P, 2, S], F32R)
        lo_q = sb("lo_q", [P, 2, S], F32R)
        hi_k = sb("hi_k", [KVH * HD, S], F32R)
        lo_k = sb("lo_k", [KVH * HD, S], F32R)
        QS = [sb(f"QS{l}", [P, 2, HPG * S], F32R) for l in range(2)]
        KS = [sb(f"KS{l}", [P, KVH, S], F32R) for l in range(2)]
        VA = [sb(f"VA{l}", [P, TT, KVH, 2 * HD]) for l in range(2)]
        probs = sb("probs", [P, 4, 1024])
        turned = sb("turned", [P, S])
        inv = sb("inv", [P, S // 32])
        OT = [sb(f"OT{l}", [P, KVH, S]) for l in range(2)]
        st = sb("st", [P, TT, 6])
        mv = sb("mv", [P, TT, 2])
        vv = sb("vv", [P, TT])
        lnv = sb("lnv", [P, TT])
        rr = sb("rr", [P, TT])
        Xres = sb("Xres", [P, TT, D])
        Ff = sb("Ff", [P, TT, D])
        FT = sb("FT", [P, DH, S])
        st2 = sb("st2", [P, TT, 6])
        mv2 = sb("mv2", [P, TT, 2])
        lnv2 = sb("lnv2", [P, TT])
        rr2 = sb("rr2", [P, TT])
        lg = sb("lg", [P, TT, E])
        mx = sb("mx", [P, TT, 8])
        ix = sb("ix", [P, TT, 8], U32)
        ixf = sb("ixf", [P, TT, 2])
        oh = sb("oh", [P, 2, TT, E])
        ohb = sb("ohb", [P, TT, E], BF16)
        pos = sb("pos", [P, TT, E])
        slot_u = sb("slot_u", [P, TT * 2], U32)
        base = sb("base", [P, E])

        SC = [pb(f"SC{n}", [P, 1024]) for n in range(2)]
        OP = pb("OP", [P, 512])
        PR = [pb(f"PR{n}", [P, 512]) for n in range(3)]

        q_stack = [nc.dram_tensor(f"q_stack{l}", [KVH, 2, HD, HPG, S], F32, kind="Internal").ap()
                   for l in range(2)]
        k_stack = [nc.dram_tensor(f"k_stack{l}", [2, KVH * HD, S], F32, kind="Internal").ap()
                   for l in range(2)]

        two = range(2)
        UNSTACK, STACK = 16 * 10, 16 * 3
        wts_in = sem("wts_in")
        ups_in = sem("ups_in")
        nw_in = sem("nw_in")
        setup_v = sem("setup_v")
        setup_g = sem("setup_g")
        setup_pe = sem("setup_pe")
        x_in, x_used = sem("x_in"), sem("x_used")
        norm_v = [sem(f"norm_v{l}") for l in two]
        var_ready = [sem(f"var_ready{l}") for l in two]
        ln_done = [sem(f"ln_done{l}") for l in two]
        rstd_ready = [sem(f"rstd_ready{l}") for l in two]
        xn_ready = [sem(f"xn_ready{l}") for l in two]
        xt_psum = [sem(f"xt_psum{l}") for l in two]
        xt_act = [sem(f"xt_act{l}") for l in two]
        xt_dve = [sem(f"xt_dve{l}") for l in two]
        proj_done = [sem(f"proj_done{l}") for l in two]
        roped = [sem(f"roped{l}") for l in two]
        squared = [sem(f"squared{l}") for l in two]
        summed = [sem(f"summed{l}") for l in two]
        rot_ready = [sem(f"rot_ready{l}") for l in two]
        qk_ln = [sem(f"qk_ln{l}") for l in two]
        qk_rstd = [sem(f"qk_rstd{l}") for l in two]
        qk_ready = [sem(f"qk_ready{l}") for l in two]
        qkt_psum = [sem(f"qkt_psum{l}") for l in two]
        hi_done = [sem(f"hi_done{l}") for l in two]
        lo_done = [sem(f"lo_done{l}") for l in two]
        unstacked = [sem(f"unstacked{l}") for l in two]
        stacked = [[sem(f"stacked{l}_{g}") for g in range(KVH)] for l in two]
        scored, exped = sem("scored"), sem("exped")
        pv_done = sem("pv_done")
        op_read, sums_inv, scaled, ot_done = sem("op_read"), sem("sums_inv"), sem("scaled"), sem("ot_done")
        wo_done = [sem(f"wo_done{l}") for l in two]
        resid = [sem(f"resid{l}") for l in two]
        xres_in = sem("xres_in")
        tail_v = sem("tail_v")
        var2_ready, ln2_done, rstd2_ready = sem("var2_ready"), sem("ln2_done"), sem("rstd2_ready")
        x1_ready, x1_out = sem("x1_ready"), sem("x1_out")
        f_ready, ft_psum, ft_act, ft_dve = sem("f_ready"), sem("ft_psum"), sem("ft_act"), sem("ft_dve")
        logits_done, picks_ready, pos_done = sem("logits_done"), sem("picks_ready"), sem("pos_done")
        slots_ready, scattered = sem("slots_ready"), sem("scattered")
        f_free = sem("f_free")
        passed_v, passed_g = sem("passed_v"), sem("passed_g")

        block = ctx.enter_context(nc.Block())

        def alone(eng, passed):
            eng.sem_inc(passed, 1)

        def program(eng, half, finish_only_wo):
            half(att=None, prep=(0, 0), wo=None, tail=None, prev=None)
            half(att=(0, 0), prep=None, wo=None, tail=None, prev=None)
            half(att=None, prep=(0, 1), wo=(0, 0), tail=None, prev=None)
            half(att=(0, 1), prep=(1, 0), wo=None, tail=None, prev=0)
            half(att=(1, 0), prep=(0, 2), wo=(0, 1), tail=None, prev=0)
            with eng.Fori(2, B - 1) as i:
                half(att=(0, i), prep=(1, i - 1), wo=(1, i - 2), tail=None, prev=1)
                half(att=(1, i - 1), prep=(0, i + 1), wo=(0, i), tail=i - 2, prev=0)
            half(att=(0, B - 1), prep=(1, B - 2), wo=(1, B - 3), tail=None, prev=1)
            half(att=(1, B - 2), prep=None, wo=(0, B - 1), tail=B - 3, prev=0)
            half(att=None, prep=(1, B - 1), wo=(1, B - 2), tail=None, prev=None)
            half(att=(1, B - 1), prep=None, wo=None, tail=B - 2, prev=1)
            finish_only_wo(1, B - 1)
            half(att=None, prep=None, wo=None, tail=B - 1, prev=None)

        def hs(b, t0=0, n=TT):
            return Hs[:, bass.ds((b % 4) * (TT * D) + t0 * D, n * D)]

        AT_TR, AT_PROJ, AT_QKT, AT_WO = 4, (6, 7, 8, 9), 11, (13, 14)
        AT_FT, AT_LOGITS, AT_POS = (12, 13), 14, 15

        @block.sync
        def _(sp):
            sp.dma_start(const[:, :], dram["const"]).then_inc(A["const_in"], 16)
            for l, w in enumerate(("norm1_w", "norm2_w")):
                sp.dma_start(normw[:, l, :], dram[w].rearrange("(a p) -> p a", p=P),
                             allow_slow_non_contiguous=True).then_inc(nw_in, 16)
            sp.dma_start(down[:, :, :], dram["g_kv_down"].rearrange("(a p) n -> p a n", p=P)).then_inc(ups_in, 16)
            sp.dma_start(up[:, 0:KVH * HD], dram["g_k_up"]).then_inc(ups_in, 16)
            sp.dma_start(up[:, KVH * HD:], dram["g_v_up"]).then_inc(ups_in, 16)
            sp.dma_start(W[0][:, :, 0:D], dram["g_wq"].rearrange("(a p) n -> p a n", p=P)).then_inc(wts_in, 16)
            for w, at in (("l_wq", 0), ("l_wk", D), ("l_wv", NQK)):
                v = dram[w].rearrange("(a p) n -> p a n", p=P)
                sp.dma_start(W[1][:, :, at:at + v.shape[2]], v).then_inc(wts_in, 16)
            sp.dma_start(gate[:, :, :], dram["gate_w"].rearrange("(a p) n -> p a n", p=P)).then_inc(wts_in, 16)
            sp.wait_ge(setup_g, 2)
            for l, w in enumerate(("g_wo", "l_wo")):
                v = dram[w].rearrange("(g h d) n -> h d g n", g=KVH, h=HPG)
                for h in range(HPG):
                    sp.dma_start(WO[l][32 * h:32 * h + HD, :, :], v[h]).then_inc(wts_in, 16)

            def load_x(b):
                sp.dma_start(Xin[:, :, :], dram["x"][bass.ds(b * S, S), :].rearrange("(t p) n -> p t n", p=P)
                             ).then_inc(x_in, 16)

            def half(att, prep, wo, tail, prev):
                if prep is not None:
                    l, b = prep
                    if l == 0:
                        if not (isinstance(b, int) and b == 0):
                            sp.wait_ge(x_used, b)
                        load_x(b)
                if tail is not None:
                    sp.wait_ge(x1_out, tail * 16 + 1)
                    sp.wait_ge(f_ready, tail + 1)
                    sp.dma_start(Xres[:, :, :], dram["x"][bass.ds(tail * S, S), :].rearrange("(t p) n -> p t n", p=P)
                                 ).then_inc(xres_in, 16)
                    sp.wait_ge(x1_ready, tail + 1)
                    sp.dma_start(dram["x1"][bass.ds(tail * S, S), :].rearrange("(t p) n -> p t n", p=P),
                                 Xres[:, :, :]).then_inc(x1_out, 16)
                if prep is not None:
                    l, b = prep
                    if not (isinstance(b, int) and b == 0):
                        for g in range(KVH):
                            sp.wait_ge(stacked[l][g], STACK * b)
                    for n in range(3):
                        for part, done, q, k in ((0, hi_done, hi_q, hi_k), (1, lo_done, lo_q, lo_k)):
                            sp.wait_ge(done[l], 3 * b + n + 1)
                            if n == 2:
                                sp.dma_start(k_stack[l][part], k[:, :].bitcast(F32)).then_inc(unstacked[l], 16)
                                continue
                            for g in range(2):
                                sp.dma_start(q_stack[l][2 * n + g, part].rearrange("d h s -> h d s"),
                                             q[64 * g:64 * (g + 1), n, :].bitcast(F32)).then_inc(unstacked[l], 16)
                    sp.wait_ge(unstacked[l], UNSTACK * (b + 1))
                    if not (isinstance(b, int) and b == 0):
                        sp.wait_ge(exped, first_chunk(l, b - 1) + NCH[l])
                    for g in range(KVH):
                        row = 64 * (g % 2)
                        q = q_stack[l][g]
                        sp.dma_start(QS[l][row:row + 64, g // 2, :].bitcast(F32),
                                     bass.AP(q.tensor, q.offset, [[0, 2], [HPG * S, 2 * HD], [1, HPG * S]])
                                     ).then_inc(stacked[l][g], 16)
                        for part in range(2):
                            k = k_stack[l][part, HD * g:HD * (g + 1)]
                            sp.dma_start(KS[l][row + 32 * part:row + 32 * part + 32, g, :].bitcast(F32),
                                         bass.AP(k.tensor, k.offset, [[0, 2], [S, HD], [1, S]])
                                         ).then_inc(stacked[l][g], 16)

            sp.sem_inc(x1_out, 1)
            program(sp, half, lambda l, b: None)
            sp.wait_ge(x1_out, 16 * B + 1)

        @block.gpsimd
        def _(pool):
            for l in two:
                nc.gpsimd.memset(WO[l][:, :, :], 0.0).then_inc(setup_g, 1)
            for l in two:
                nc.gpsimd.memset(VA[l][:, :, :, :], 1.0).then_inc(setup_g, 1)
                nc.gpsimd.memset(KS[l][:, :, :].bitcast(F32), 0.0).then_inc(setup_g, 1)

            def half(att, prep, wo, tail, prev):
                if prep is not None:
                    l, b = prep
                    for t in range(TT):
                        pool.wait_ge(roped[l], 4 * b + t + 1)
                        nc.gpsimd.tensor_tensor(R[:, t, :], R[:, t, :], T2[:, t % 2, :], ALU.add
                                                ).then_inc(rot_ready[l], 1)
                if tail is not None:
                    pool.wait_ge(slots_ready, tail + 1)
                    alone(pool, passed_g)
                    for t in range(TT):
                        for k in range(2):
                            c = 2 * t + k
                            nc.gpsimd.indirect_dma_start(
                                dram["xs"], bass.IndirectOffsetOnAxis(ap=slot_u[:, c:c + 1], axis=0),
                                Ff[:, t, :], None).then_inc(scattered, 16)
                    pool.wait_ge(scattered, 16 * 2 * TT * (tail + 1))
                    pool.sem_inc(f_free, 1)

            pool.sem_inc(f_free, 1)
            program(pool, half, lambda l, b: None)

        @block.tensor
        def _(pe):
            mm, tr = nc.tensor.matmul, nc.tensor.transpose
            pe.wait_ge(A["const_in"], 16)
            pe.wait_ge(ups_in, 48)
            for a in range(DH):
                tr(PR[a][0:LAT, 0:P], down[:, a, :], ident).then_inc(setup_pe, 1)
            pe.wait_ge(setup_v, 1)
            for a in range(DH):
                mm(PR[2][:, P * a:P * (a + 1)], downT[:, a, :], up[:, :], start=True, stop=True
                   ).then_inc(setup_pe, 1)

            def score_unit(l, b, u, chunk0):
                g, kt = divmod(u, TT)
                w = width(l, kt)
                mw = CONST[f"mask{l}"][1] if l == 1 and w > P else P
                if kt == 0 and g % 2 == 0:
                    pe.wait_ge(stacked[l][g], STACK * (b + 1))
                    pe.wait_ge(stacked[l][g + 1], STACK * (b + 1))
                for n, (_, h0, nh, per) in chunks_of(l, u):
                    if not (isinstance(chunk0, int) and chunk0 + n < 2):
                        pe.wait_ge(exped, chunk0 + n - 1)
                    sc = SC[n % 2]
                    for j in range(0, nh, per):
                        out = spread(sc[:, 512 * (j // per):512 * (j // per) + 1], [[w, per], [1, w]])
                        q = QS[l][:, g // 2, (h0 + j) * S + kt * P:(h0 + j) * S + kt * P + 1]
                        mm(out, KS[l][:, g, kt * P:(kt + 1) * P], spread(q, [[S, per], [1, w]]),
                           start=True, stop=False)
                        out = spread(sc[:, 512 * (j // per):512 * (j // per) + 1], [[w, per], [1, mw]])
                        last = mm(out, ident_b[:, :], spread(mask_b[l][:, 0:1], [[0, per], [1, mw]]),
                                  start=False, stop=True)
                    last.then_inc(scored, 1)

            def pv_unit(l, b, a, u, chunk0):
                g, kt = divmod(u, TT)
                w = width(l, kt)
                mine = chunks_of(l, u)
                pe.wait_ge(exped, chunk0 + mine[-1][0] + 1)
                if kt == 0 and not (isinstance(a, int) and a == 0 and g == 0):
                    pe.wait_ge(op_read, 4 * a + g)
                if kt == 0 and l == 1:
                    mm(OP[:, :], zeros_b[:, :], spread(ones_b[:, 0:1], [[0, S]]), start=True, stop=False)
                for n, (_, h0, nh, per) in mine:
                    for j in range(nh):
                        h = h0 + j
                        at = 512 * (j // per) + w * (j % per)
                        last = mm(OP[32 * h:32 * h + 32, kt * P:kt * P + w], VA[l][:, kt, g, :],
                                  probs[:, n % 4, at:at + w], start=(kt == 0 and l == 0), stop=(kt == TT - 1),
                                  tile_position=(0, 32 * h))
                last.then_inc(pv_done, 1)

            def project_out(l, b, u):
                pe.wait_ge(ot_done, 4 * (order(l, b) + 1))
                if l == 0 and not (isinstance(b, int) and b < 2):
                    pe.wait_ge(resid[1], 2 * (b - 1))
                if l == 1:
                    pe.wait_ge(resid[0], 2 * min(b + 2, B) if isinstance(b, int) else 2 * (b + 2))
                for j in range(2):
                    for g in range(KVH):
                        last = mm(PR[u][:, D * j:D * (j + 1)], OT[l][:, g, (2 * u + j) * P:(2 * u + j + 1) * P],
                                  WO[l][:, g, :], start=(g == 0), stop=(g == KVH - 1))
                last.then_inc(wo_done[l], 1)

            def half(att, prep, wo, tail, prev):
                for u in range(UNITS):
                    if att is not None:
                        la, ba = att
                        chunk0, a = first_chunk(la, ba), order(la, ba)
                        score_unit(la, ba, u, chunk0)
                        if u > 0:
                            pv_unit(la, ba, a, u - 1, chunk0)
                    if prep is not None:
                        l, b = prep
                        if u == AT_TR:
                            pe.wait_ge(xn_ready[l], b + 1)
                            for f in range(DH):
                                for t in range(TT):
                                    last = tr(PR[f][:, t * P:(t + 1) * P], xn[:, t, f * P:(f + 1) * P], ident)
                                last.then_inc(xt_psum[l], 1)
                        if u in AT_PROJ:
                            t = AT_PROJ.index(u)
                            if isinstance(b, int) and b == 0 and t == 0:
                                pe.wait_ge(setup_v, 2)
                            if t == 0:
                                pe.wait_ge(xt_act[l], b + 1)
                                pe.wait_ge(xt_dve[l], b + 1)
                            if t == 3:
                                pe.wait_ge(roped[l], 4 * b + 1)
                            bank = PR[(2, 0, 1, 2)[t]]
                            for f in range(DH):
                                last = mm(bank[:, 0:NPROJ], xT[:, f, t * P:(t + 1) * P], W[l][:, f, :],
                                          start=(f == 0), stop=(f == DH - 1))
                            last.then_inc(proj_done[l], 1)
                        if u == AT_QKT:
                            pe.wait_ge(qk_ready[l], 4 * (b + 1))
                            for n in range(3):
                                m = P if n < 2 else KVH * HD
                                for t in range(TT):
                                    last = tr(PR[n][0:m, t * P:(t + 1) * P], R[:, t, n * P:n * P + m], ident)
                                last.then_inc(qkt_psum[l], 1)
                    if wo is not None and u in AT_WO:
                        n = AT_WO.index(u)
                        if prep is not None:
                            pe.wait_ge(lo_done[prep[0]], 3 * prep[1] + n + 1)
                        project_out(*wo, n)
                    if tail is not None:
                        b = tail
                        if u in AT_FT:
                            f = AT_FT.index(u)
                            if f == 0:
                                pe.wait_ge(f_ready, b + 2)
                                if prep is not None:
                                    pe.wait_ge(lo_done[prep[0]], 3 * (prep[1] + 1))
                            else:
                                pe.wait_ge(ft_act, b + 1)
                            for t in range(TT):
                                last = tr(PR[2][:, t * P:(t + 1) * P], Ff[:, t, f * P:(f + 1) * P], ident)
                            last.then_inc(ft_psum, 1)
                        if u == AT_LOGITS:
                            pe.wait_ge(ft_dve, b + 1)
                            for t in range(TT):
                                for f in range(DH):
                                    last = mm(PR[2][:, t * E:(t + 1) * E], FT[:, f, t * P:(t + 1) * P],
                                              gate[:, f, :], start=(f == 0), stop=(f == DH - 1))
                            last.then_inc(logits_done, 1)
                        if u == AT_POS:
                            pe.wait_ge(picks_ready, b + 1)
                            for t in range(TT + 1):
                                out = PR[2][:, t * E:(t + 1) * E]
                                for s in range(min(t, TT)):
                                    last = mm(out, ones_b[:, :], ohb[:, s, :], start=(s == 0), stop=(t == TT and s == TT - 1))
                                if t < TT:
                                    last = mm(out, before_b[:, :], ohb[:, t, :], start=(t == 0), stop=True)
                            last.then_inc(pos_done, 1)
                if att is not None:
                    pv_unit(la, ba, a, UNITS - 1, chunk0)

            def finish(l, b):
                for n in range(2):
                    project_out(l, b, n)

            program(pe, half, finish)

        @block.scalar
        def _(act):
            act.wait_ge(A["eps_set"], 2)
            nc.scalar.preload_act_table_set("natural_log_exp_and_others")

            def exp_unit(l, b, a, u, chunk0, prev):
                for n, (kt, h0, nh, per) in chunks_of(l, u):
                    act.wait_ge(scored, chunk0 + n + 1)
                    if n >= 4:
                        act.wait_ge(pv_done, UNITS * a + unit_of(l, n - 4) + 1)
                    elif prev is not None:
                        act.wait_ge(pv_done, UNITS * (a - 1) + unit_of(prev, NCH[prev] + n - 4) + 1)
                    cols = per * width(l, kt)
                    nb = nh // per
                    nc.scalar.activation(spread(probs[:, n % 4, 0:1], [[512, nb], [1, cols]]),
                                         spread(SC[n % 2][:, 0:1], [[512, nb], [1, cols]]),
                                         ACT.Exp, scale=SCALE).then_inc(exped, 1)

            def rsqrt(out, tmp, in_, eps, scale, wait, waited, mid, midv, done):
                act.wait_ge(wait, waited)
                nc.scalar.activation(tmp, in_, ACT.Ln, bias=eps, scale=scale).then_inc(mid, 1)
                act.wait_ge(mid, midv)
                nc.scalar.activation(out, tmp, ACT.Exp, scale=-0.5).then_inc(done, 1)

            def half(att, prep, wo, tail, prev):
                for u in range(UNITS):
                    if att is not None:
                        la, ba = att
                        exp_unit(la, ba, order(la, ba), u, first_chunk(la, ba), prev)
                    if prep is not None:
                        l, b = prep
                        if l == 0 and u < 2:
                            rsqrt(rr[:, :], lnv[:, :], vv[:, :], (eps_ln, eps_rms)[u][:, :], 1.0,
                                  var_ready[0], 2 * b + u + 1, ln_done[0], 2 * b + u + 1, rstd_ready[0])
                        if l == 1 and u == 0:
                            rsqrt(rr[:, :], lnv[:, :], vv[:, :], eps_rms[:, :], 1.0,
                                  var_ready[1], b + 1, ln_done[1], b + 1, rstd_ready[1])
                        if u == AT_TR:
                            act.wait_ge(xt_psum[l], 2 * b + 1)
                            nc.scalar.activation(xT[:, 0, :], PR[0][:, :], ACT.Copy).then_inc(xt_act[l], 1)
                        if u in AT_PROJ:
                            t = AT_PROJ.index(u)
                            if isinstance(b, int) and b == 0 and t == 0:
                                act.wait_ge(setup_g, 6)
                            act.wait_ge(proj_done[l], 4 * b + t + 1)
                            nc.scalar.activation(VA[l][:, t, :, 0:HD],
                                                 PR[(2, 0, 1, 2)[t]][:, NQK:NPROJ].rearrange("p (g d) -> p g d", g=KVH),
                                                 ACT.Copy)
                            if t >= 2:
                                act.wait_ge(summed[l], 4 * b + t - 1)
                            nc.scalar.activation(SQ[:, t % 2, :], PR[(2, 0, 1, 2)[t]][:, 0:NQK], ACT.Square
                                                 ).then_inc(squared[l], 1)
                        if u == AT_PROJ[-1] + 1:
                            rsqrt(RS[:, :, :], RL[:, :, :], SS[:, :, :], eps_rms[:, :], 1.0 / HD,
                                  summed[l], 4 * (b + 1), qk_ln[l], b + 1, qk_rstd[l])
                        if u == AT_QKT:
                            if l == 1:
                                act.wait_ge(unstacked[0], UNSTACK * min(b + 2, B) if isinstance(b, int) else UNSTACK * (b + 2))
                            elif isinstance(b, int) and b <= 1:
                                if b == 1:
                                    act.wait_ge(unstacked[0], UNSTACK)
                            else:
                                act.wait_ge(unstacked[1], UNSTACK * (b - 1))
                            for n in range(3):
                                act.wait_ge(qkt_psum[l], 3 * b + n + 1)
                                o = hi_q[:, n, :] if n < 2 else hi_k[:, :]
                                i = PR[n][:, :] if n < 2 else PR[n][0:KVH * HD, :]
                                nc.scalar.activation(o, i, ACT.Copy).then_inc(hi_done[l], 1)
                    if tail is not None:
                        if u in (2, 5):
                            n = (2, 5).index(u)
                            rsqrt(rr2[:, :], lnv2[:, :], mv2[:, :, 1], eps_ln[:, :], 1.0,
                                  var2_ready, 2 * tail + n + 1, ln2_done, 2 * tail + n + 1, rstd2_ready)
                        if u == AT_FT[0]:
                            act.wait_ge(ft_psum, 2 * tail + 1)
                            nc.scalar.activation(FT[:, 0, :], PR[2][:, :], ACT.Copy).then_inc(ft_act, 1)

            program(act, half, lambda l, b: None)

        @block.vector
        def _(dve):
            v = nc.vector
            v.memset(eps_ln[:, :], EPS_LN).then_inc(A["eps_set"], 1)
            v.memset(eps_rms[:, :], EPS_RMS).then_inc(A["eps_set"], 1)
            dve.wait_ge(A["const_in"], 16)
            for o, i in ((ident_b, "ident"), (before_b, "before"), (ones_b, "ones"), (mask_b[0], "mask0"), (mask_b[1], "mask1")):
                v.tensor_copy(o[:, :], K(i))
            v.memset(zeros_b[:, :], 0.0)
            v.tensor_copy(base[:, :], K("region"))
            dve.wait_ge(setup_pe, DH)
            v.tensor_copy(downT[:, 0, :], PR[0][0:LAT, 0:P])
            v.tensor_copy(downT[:, 1, :], PR[1][0:LAT, 0:P]).then_inc(setup_v, 1)
            dve.wait_ge(nw_in, 32)
            dve.wait_ge(wts_in, 16 * (5 + 2 * HPG))
            dve.wait_ge(setup_pe, 2 * DH)
            for a in range(DH):
                v.tensor_scalar(W[0][:, a, 0:D], W[0][:, a, 0:D], normw[:, 0, a:a + 1], None, ALU.mult)
                v.tensor_scalar(W[0][:, a, D:NPROJ], PR[2][:, P * a:P * (a + 1)], normw[:, 0, a:a + 1], None, ALU.mult)
            for a in range(DH):
                last = v.tensor_scalar(W[1][:, a, :], W[1][:, a, :], normw[:, 1, a:a + 1], None, ALU.mult)
            last.then_inc(setup_v, 1)

            NORM = [6, 4]

            def norm_stats(l, b, s):
                if l == 0:
                    dve.wait_ge(x_in, 16 * (b + 1))
                    src = Xin[:, :, :]
                else:
                    dve.wait_ge(resid[0], 2 * (b + 1))
                    src = hs(b).rearrange("p (t n) -> p t n", t=TT)
                alone(dve, passed_v)
                for t in range(TT):
                    last = v.bn_stats(st[:, t, :], src[:, t, :])
                s.did(last)
                s.settle()
                alone(dve, passed_v)
                for t in range(TT):
                    last = v.bn_aggr(mv[:, t, :], st[:, t, :])
                s.did(last)
                s.settle()
                if l == 0:
                    v.tensor_copy(vv[:, :], mv[:, :, 1]).then_inc(var_ready[0], 1)
                else:
                    s.did(v.tensor_tensor(vv[:, :], mv[:, :, 0], mv[:, :, 0], ALU.mult))
                    s.settle()
                    v.tensor_tensor(vv[:, :], vv[:, :], mv[:, :, 1], ALU.add).then_inc(var_ready[1], 1)

            def layer_norm_h(b, s):
                dve.wait_ge(rstd_ready[0], 2 * b + 1)
                s.did(v.tensor_tensor(vv[:, :], mv[:, :, 1], rr[:, :], ALU.mult))
                s.settle()
                s.did(v.tensor_tensor(vv[:, :], vv[:, :], rr[:, :], ALU.mult))
                for t in range(TT):
                    last = v.tensor_scalar(hs(b, t, 1), Xin[:, t, :], mv[:, t, 0:1], rr[:, t:t + 1],
                                           ALU.subtract, ALU.mult)
                s.did(last)
                s.settle()
                dve.sem_inc(x_used, 1)
                dve.sem_inc(var_ready[0], 1)

            def rms_x(l, b, s):
                dve.wait_ge(rstd_ready[l], 2 * b + 2 if l == 0 else b + 1)
                for t in range(TT):
                    last = v.tensor_scalar(xn[:, t, :], hs(b, t, 1), rr[:, t:t + 1], None, ALU.mult)
                s.did(last)
                s.settle()
                dve.sem_inc(xn_ready[l], 1)

            def rope(l, b, t):
                dve.wait_ge(squared[l], 4 * b + t + 1)
                if t >= 2:
                    dve.wait_ge(rot_ready[l], 4 * b + t - 1)
                qk = PR[(2, 0, 1, 2)[t]][:, 0:NQK]
                tab = [CONST[f"{n}{l}"][0] + t * HD for n in ("cos", "sin")]
                heads = [[HD, H + KVH], [2, HD // 2], [1, 2]]
                over = [[0, H + KVH], [2, HD // 2], [1, 2]]
                v.tensor_tensor(R[:, t, :].rearrange("p (h i two) -> p h i two", i=HD // 2, two=2),
                                spread(qk, heads), spread(const[:, tab[0]:tab[0] + 1], over), ALU.mult)
                swapped = spread(PR[(2, 0, 1, 2)[t]][:, 1:2], [[HD, H + KVH], [2, HD // 2], [-1, 2]])
                v.tensor_tensor(T2[:, t % 2, :].rearrange("p (h i two) -> p h i two", i=HD // 2, two=2),
                                swapped, spread(const[:, tab[1]:tab[1] + 1], over), ALU.mult
                                ).then_inc(roped[l], 1)
                v.tensor_reduce(SS[:, t, :], SQ[:, t % 2, :].rearrange("p (h d) -> p h d", d=HD), AX.X, ALU.add
                                ).then_inc(summed[l], 1)

            def qk_norm(l, b):
                dve.wait_ge(qk_rstd[l], b + 1)
                for t in range(TT):
                    dve.wait_ge(rot_ready[l], 4 * b + t + 1)
                    r = R[:, t, :].rearrange("p (h d) -> p h d", d=HD)
                    v.tensor_tensor(r, r, spread(RS[:, t, 0:1], [[1, H + KVH], [0, HD]]), ALU.mult
                                    ).then_inc(qk_ready[l], 1)

            def low_parts(l, b):
                if l == 1:
                    dve.wait_ge(unstacked[0], UNSTACK * min(b + 2, B) if isinstance(b, int) else UNSTACK * (b + 2))
                elif isinstance(b, int) and b <= 1:
                    if b == 1:
                        dve.wait_ge(unstacked[0], UNSTACK)
                else:
                    dve.wait_ge(unstacked[1], UNSTACK * (b - 1))
                for n in range(3):
                    dve.wait_ge(hi_done[l], 3 * b + n + 1)
                    o, h = (lo_q[:, n, :], hi_q[:, n, :]) if n < 2 else (lo_k[:, :], hi_k[:, :])
                    i = PR[n][:, :] if n < 2 else PR[n][0:KVH * HD, :]
                    v.tensor_tensor(o, i, h.bitcast(F32), ALU.subtract).then_inc(lo_done[l], 1)

            def normalise(l, a, g):
                if not (isinstance(a, int) and 4 * a + g == 0):
                    dve.wait_ge(ot_done, 4 * a + g)
                dve.wait_ge(pv_done, UNITS * a + TT * (g + 1))
                v.transpose(turned[:, :], OP[:, :]).then_inc(op_read, 1)
                dve.wait_ge(op_read, 4 * a + g + 1)
                blocks = turned[:, :].rearrange("p (q i) -> p q i", i=32)
                v.reciprocal(inv[:, :], blocks[:, :, HD]).then_inc(sums_inv, 1)
                dve.wait_ge(sums_inv, 4 * a + g + 1)
                v.tensor_tensor(blocks[:, :, 0:HD], blocks[:, :, 0:HD], spread(inv[:, 0:1], [[1, S // 32], [0, HD]]),
                                ALU.mult).then_inc(scaled, 1)
                dve.wait_ge(scaled, 4 * a + g + 1)
                v.transpose(OT[l][:, g, :], turned[:, :]).then_inc(ot_done, 1)

            def residual(l, b, u):
                dve.wait_ge(wo_done[l], 2 * b + u + 1)
                h = hs(b, 2 * u, 2)
                v.tensor_tensor(h, h, PR[u][:, :], ALU.add).then_inc(resid[l], 1)

            TAIL = 13

            def stats2(b, src, s):
                alone(dve, passed_v)
                for t in range(TT):
                    last = v.bn_stats(st2[:, t, :], src[:, t, :])
                s.did(last)
                s.settle()
                alone(dve, passed_v)
                for t in range(TT):
                    last = v.bn_aggr(mv2[:, t, :], st2[:, t, :])
                last.then_inc(var2_ready, 1)

            def tail_1(b, s):
                dve.wait_ge(resid[1], 2 * (b + 1))
                stats2(b, hs(b).rearrange("p (t n) -> p t n", t=TT), s)

            def tail_2(b, s):
                dve.wait_ge(rstd2_ready, 2 * b + 1)
                dve.wait_ge(xres_in, 16 * (b + 1))
                dve.wait_ge(f_free, b + 1)
                for t in range(TT):
                    last = v.tensor_scalar(Ff[:, t, :], hs(b, t, 1), mv2[:, t, 0:1], rr2[:, t:t + 1],
                                           ALU.subtract, ALU.mult)
                s.did(last)
                s.settle()
                s.did(v.tensor_tensor(Xres[:, :, :], Xres[:, :, :], Ff[:, :, :], ALU.add))
                s.settle()
                dve.sem_inc(x1_ready, 1)
                stats2(b, Xres[:, :, :], s)

            def tail_3(b, s):
                dve.wait_ge(rstd2_ready, 2 * b + 2)
                for t in range(TT):
                    last = v.tensor_scalar(Ff[:, t, :], Xres[:, t, :], mv2[:, t, 0:1], rr2[:, t:t + 1],
                                           ALU.subtract, ALU.mult)
                last.then_inc(f_ready, 1)

            def tail_4(b, s):
                dve.wait_ge(ft_psum, 2 * b + 2)
                v.tensor_copy(FT[:, 1, :], PR[2][:, :]).then_inc(ft_dve, 1)

            def tail_5(b, s):
                dve.wait_ge(logits_done, b + 1)
                s.did(v.tensor_copy(lg[:, :, :], PR[2][:, 0:TT * E].rearrange("p (t e) -> p t e", t=TT)))
                s.settle()
                alone(dve, passed_v)
                for t in range(TT):
                    last = v.max(mx[:, t, :], lg[:, t, :])
                s.did(last)
                s.settle()
                alone(dve, passed_v)
                for t in range(TT):
                    last = v.max_index(ix[:, t, :], mx[:, t, :], lg[:, t, :])
                s.did(last)
                s.settle()
                alone(dve, passed_v)
                v.tensor_copy(top2[:, bass.ds(b * (2 * TT), 2 * TT)].rearrange("p (t k) -> p t k", k=2), mx[:, :, 0:2])
                s.did(v.tensor_copy(ixf[:, :, :], ix[:, :, 0:2]))
                s.settle()
                for k in range(2):
                    last = v.tensor_tensor(oh[:, k, :, :], spread(K("expert"), [[0, TT], [1, E]]),
                                           spread(ixf[:, 0, k:k + 1], [[2, TT], [0, E]]), ALU.is_equal)
                s.did(last)
                s.settle()
                v.tensor_tensor(ohb[:, :, :], oh[:, 0, :, :], oh[:, 1, :, :], ALU.add).then_inc(picks_ready, 1)

            def tail_6(b, s):
                dve.wait_ge(pos_done, b + 1)
                s.did(v.tensor_tensor(pos[:, :, :], PR[2][:, 0:TT * E].rearrange("p (t e) -> p t e", t=TT),
                                      spread(base[:, 0:1], [[0, TT], [1, E]]), ALU.add))
                s.settle()
                s.did(v.tensor_tensor(base[:, :], base[:, :], PR[2][:, TT * E:(TT + 1) * E], ALU.add))
                for k in range(2):
                    last = v.tensor_tensor(oh[:, k, :, :], oh[:, k, :, :], pos[:, :, :], ALU.mult)
                s.did(last)
                s.settle()
                rows = slot_f[:, bass.ds(b * (2 * TT), 2 * TT)].rearrange("p (t k) -> p t k", k=2)
                for k in range(2):
                    last = v.tensor_reduce(rows[:, :, k], oh[:, k, :, :], AX.X, ALU.add)
                s.did(last)
                s.settle()
                alone(dve, passed_v)
                v.tensor_copy(slot_u[:, :], slot_f[:, bass.ds(b * (2 * TT), 2 * TT)]).then_inc(slots_ready, 1)

            def half(att, prep, wo, tail, prev):
                if att is not None:
                    la, a = att[0], order(*att)
                if prep is not None:
                    l, b = prep
                    s = Steps(dve, norm_v[l], NORM[l], b)
                    norm_stats(l, b, s)
                if tail is not None:
                    ts = Steps(dve, tail_v, TAIL, tail)
                for u in range(UNITS):
                    if prep is not None:
                        if u == 0 and l == 0:
                            layer_norm_h(b, s)
                        if u == 1:
                            rms_x(l, b, s)
                            s.end()
                        if u == AT_TR:
                            dve.wait_ge(xt_psum[l], 2 * b + 2)
                            v.tensor_copy(xT[:, 1, :], PR[1][:, :]).then_inc(xt_dve[l], 1)
                        if u in AT_PROJ:
                            rope(l, b, AT_PROJ.index(u))
                        if u == AT_PROJ[-1] + 1:
                            qk_norm(l, b)
                        if u == AT_QKT:
                            low_parts(l, b)
                    if tail is not None:
                        if u == 1:
                            tail_1(tail, ts)
                        if u == 3:
                            tail_2(tail, ts)
                        if u == 5:
                            tail_3(tail, ts)
                        if u == AT_FT[1]:
                            tail_4(tail, ts)
                        if u == AT_LOGITS:
                            tail_5(tail, ts)
                    if wo is not None and u in AT_WO:
                        residual(*wo, AT_WO.index(u))
                    if att is not None and u % TT == 0 and u > 0:
                        normalise(la, a, u // TT - 1)
                    if tail is not None and u == AT_POS:
                        tail_6(tail, ts)
                        ts.end()
                if att is not None:
                    normalise(la, a, KVH - 1)

            def finish(l, b):
                for u in range(2):
                    residual(l, b, u)

            dve.sem_inc(f_ready, 1)
            program(dve, half, finish)
            v.tensor_tensor(counts[:, :], base[:, :], K("region"), ALU.subtract)


NQ, FC = 4, F // P
UNROLL = 3
HP, LP, RING = 256, 3, 4


def experts(nc, A, dram):
    with ExitStack() as ctx:
        def sb(name, shape, dt=F32):
            return ctx.enter_context(nc.sbuf_tensor(name, shape, dt))

        def pb(name, shape, dt=F32):
            return ctx.enter_context(nc.psum_tensor(name, shape, dt))

        def sem(name):
            return ctx.enter_context(nc.semaphore(name))

        const, counts, slot_f = A["const"], A["counts"], A["slot_f"]

        def K(name):
            at, n = CONST[name]
            return const[:, at:at + n]

        ident = K("ident")
        NT1 = NTILES + 2
        cnt_i = sb("cnt_i", [P, E], I32)
        nt_i = sb("nt_i", [P, E], I32)
        nt = sb("nt", [P, E])
        ends = sb("ends", [P, E])
        past = sb("past", [P, NT1, E])
        of_past = sb("of_past", [P, NT1, E])
        expert_f = sb("expert_f", [P, NT1])
        first_f = sb("first_f", [P, NT1])
        row_f = sb("row_f", [P, NT1])
        row_i = sb("row_i", [P, NT1], I32)
        expert_i = sb("expert_i", [P, NT1], I32)
        fresh_f = sb("fresh_f", [P, NT1])
        fresh_i = sb("fresh_i", [P, NT1], I32)
        pad_f = sb("pad_f", [P, E])
        pad_i = sb("pad_i", [P, E], I32)
        NSLOT = 2 * TT * B
        move, step = sb("move", [P, E]), sb("step", [P, E - 1])
        beyond, moved = sb("beyond", [P, NSLOT, E - 1]), sb("moved", [P, NSLOT])
        zeros = sb("zeros", [P, MT // P, D])
        raw1, raw3 = sb("raw1", [P, DH, F]), sb("raw3", [P, DH, F])
        raw2 = sb("raw2", [P, FC, D])
        hi1, lo1 = sb("hi1", [P, DH, F], F32R), sb("lo1", [P, DH, F], F32R)
        hi3, lo3 = sb("hi3", [P, DH, F], F32R), sb("lo3", [P, DH, F], F32R)
        hi2, lo2 = sb("hi2", [P, FC, D], F32R), sb("lo2", [P, FC, D], F32R)
        xg = sb("xg", [P, UNROLL, MT // P, D])
        hx, lx = sb("hx", [P, UNROLL, DH, MT], F32R), sb("lx", [P, UNROLL, DH, MT], F32R)
        gate_s = sb("gate_s", [P, RING, MT])
        prod = sb("prod", [P, RING, MT])
        hh, lh = sb("hh", [P, RING, MT], F32R), sb("lh", [P, RING, MT], F32R)
        ys = sb("ysb", [P, UNROLL, MT // P, D])

        HB = [pb(f"HB{n}", [P, 2 * MT]) for n in range(RING)]
        XB = pb("XB", [P, DH * MT])
        YB = [pb(f"YB{n}", [P, MT // P, D]) for n in range(UNROLL)]

        table_v, table_ready = sem("table_v"), sem("table_ready")
        zeroed = sem("zeroed")
        x_in = [sem(f"xg_in{n}") for n in range(UNROLL)]
        y_out = [sem(f"y_out{n}") for n in range(UNROLL)]
        raw_in = [sem(f"raw_in{q}") for q in range(NQ)]
        x_psum, x_hi, x_lo = sem("x_psum"), sem("x_hi"), sem("x_lo")
        w_hi, w_lo = sem("w_hi"), sem("w_lo")
        h_psum, silu_done, gated, h_hi, h_lo = (sem("h_psum"), sem("silu_done"), sem("gated"), sem("h_hi"), sem("h_lo"))
        l2_done, y_read = sem("l2_done"), sem("y_read")
        passed = sem("epassed")

        block = ctx.enter_context(nc.Block())

        def tiles(eng, tile):
            for s in range(UNROLL):
                tile(s, 0, s)
            with eng.Fori(1, NTILES // UNROLL) as r:
                for s in range(UNROLL):
                    tile(r * UNROLL + s, r, s)

        def where_fresh(eng, j, work, otherwise):
            if isinstance(j, int) and j == 0:
                work()
                return
            fresh = eng.value_load(fresh_i[0:1, bass.ds(j, 1)], min_val=0, max_val=1)
            with eng.If(fresh):
                work()
            with eng.Else():
                otherwise()

        def quarter(q):
            c, n = slice(HP * q, HP * (q + 1)), slice(HP // P * q, HP // P * (q + 1))
            return ((raw1[:, :, c], hi1[:, :, c], lo1[:, :, c]), (raw3[:, :, c], hi3[:, :, c], lo3[:, :, c]),
                    (raw2[:, n, :], hi2[:, n, :], lo2[:, n, :]))

        @block.sync
        def _(sp):
            sp.wait_ge(table_ready, 1)
            for e in range(E):
                at = sp.value_load(pad_i[0:1, e:e + 1], min_val=0, max_val=ROWS - MT)
                sp.dma_start(dram["xs"][bass.ds(at, MT), :].rearrange("(m p) n -> p m n", p=P), zeros[:, :, :]
                             ).then_inc(zeroed, 16)
            for m in range(E):
                r0 = E * REG + m * MT
                sp.dma_start(dram["xs"][r0:r0 + MT, :].rearrange("(m p) n -> p m n", p=P), zeros[:, :, :]
                             ).then_inc(zeroed, 16)

            def load_weights(j):
                for q in range(NQ):
                    c, n = slice(HP * q, HP * (q + 1)), slice(HP // P * q, HP // P * (q + 1))
                    if not (isinstance(j, int) and j == 0):
                        sp.wait_ge(w_lo, NQ * (j - 1) + q + 1)
                    sp.sem_inc(passed, 1)

                    def load():
                        e = sp.value_load(expert_i[0:1, bass.ds(j, 1)], min_val=0, max_val=E - 1)
                        for w, raw in (("w1", raw1), ("w3", raw3)):
                            sp.dma_start(raw[:, :, c], dram[w][bass.ds(e * D, D), c].rearrange("(a p) n -> p a n", p=P)
                                         ).then_inc(raw_in[q], 16)
                        sp.dma_start(raw2[:, n, :], dram["w2"][bass.ds(e * F + HP * q, HP), :]
                                     .rearrange("(a p) n -> p a n", p=P)).then_inc(raw_in[q], 16)

                    where_fresh(sp, j, load, lambda: sp.sem_inc(raw_in[q], 48))

            def load_x(j, r, s):
                if not (isinstance(r, int) and r == 0):
                    sp.wait_ge(x_psum, j - UNROLL + 1)
                sp.sem_inc(passed, 1)
                at = sp.value_load(row_i[0:1, bass.ds(j, 1)], min_val=0, max_val=ROWS - MT)
                sp.dma_start(xg[:, s, :, :], dram["xs"][bass.ds(at, MT), :].rearrange("(m p) n -> p m n", p=P)
                             ).then_inc(x_in[s], 16)

            def store_y(j, r, s):
                sp.wait_ge(y_read, j + 1)
                sp.dma_start(dram["ys"][bass.ds(j * MT, MT), :].rearrange("(m p) n -> p m n", p=P), ys[:, s, :, :]
                             ).then_inc(y_out[s], 16)

            load_weights(0)
            sp.wait_ge(zeroed, 16 * 2 * E)
            load_x(0, 0, 0)
            load_x(1, 0, 1)

            def tile(j, r, s):
                ahead = (s + 2) % UNROLL
                load_x(j + 2, r if s == 0 else r + 1, ahead)
                load_weights(j + 1)
                if not (isinstance(j, int) and j == 0):
                    store_y(j - 1, r if s else r - 1, (s - 1) % UNROLL)

            tiles(sp, tile)
            store_y(NTILES - 1, NTILES // UNROLL - 1, UNROLL - 1)
            for s in range(UNROLL):
                sp.wait_ge(y_out[s], 16 * (NTILES // UNROLL))
            for s in range(2):
                sp.wait_ge(x_in[s], 16 * (NTILES // UNROLL + 1))
            for q in range(NQ):
                sp.wait_ge(raw_in[q], 48 * (NTILES + 1))

        @block.gpsimd
        def _(pool):
            nc.gpsimd.memset(zeros[:, :, :], 0.0).then_inc(table_v, 1)

        @block.tensor
        def _(pe):
            mm = nc.tensor.matmul

            def turn_x(j, r, s):
                pe.wait_ge(x_in[s], 16 * (r + 1))
                if not (isinstance(j, int) and j == 0):
                    pe.wait_ge(x_lo, j)
                for m in range(MT // P):
                    for a in range(DH):
                        last = nc.tensor.transpose(XB[:, a * MT + m * P:a * MT + (m + 1) * P],
                                                   xg[:, s, m, a * P:(a + 1) * P], ident)
                last.then_inc(x_psum, 1)

            def first(j, s, f):
                n, k, c = FC * j + f, f % RING, slice(f * P, (f + 1) * P)
                if f % 2 == 0:
                    pe.wait_ge(w_lo, NQ * j + f // 2 + 1)
                if f == 0:
                    pe.wait_ge(x_lo, j + 1)
                if not (isinstance(n, int) and n < RING):
                    pe.wait_ge(gated, n - RING + 1)
                for i, (hi, lo) in enumerate(((hi1, lo1), (hi3, lo3))):
                    out = HB[k][:, i * MT:(i + 1) * MT]
                    for a in range(DH):
                        for p, (w, x) in enumerate(((hi, hx), (hi, lx), (lo, hx))):
                            last = mm(out, w[:, a, c], x[:, s, a, :], start=(a == 0 and p == 0),
                                      stop=(a == DH - 1 and p == 2))
                last.then_inc(h_psum, 1)

            def second(j, s, f):
                n, k = FC * j + f, f % RING
                pe.wait_ge(h_lo, n + 1)
                for m in range(MT // P):
                    for p, (h, w) in enumerate(((hh, hi2), (hh, lo2), (lh, hi2))):
                        last = mm(YB[s][:, m, :], h[:, k, m * P:(m + 1) * P], w[:, f, :],
                                  start=(f == 0 and m == 0 and p == 0),
                                  stop=(f == FC - 1 and m == MT // P - 1 and p == 2))
                last.then_inc(l2_done, 1)

            turn_x(0, 0, 0)

            def tile(j, r, s):
                for f in range(FC):
                    first(j, s, f)
                    if f >= LP:
                        if f == LP and not (isinstance(r, int) and r == 0):
                            pe.wait_ge(y_read, j - UNROLL + 1)
                        second(j, s, f - LP)
                    elif not (isinstance(j, int) and j == 0):
                        second(j - 1, (s - 1) % UNROLL, FC - LP + f)
                    if f == 4:
                        nxt = (s + 1) % UNROLL
                        turn_x(j + 1, r if nxt else r + 1, nxt)

            tiles(pe, tile)
            for f in range(FC - LP, FC):
                second(NTILES - 1, (NTILES - 1) % UNROLL, f)

        SPLIT = {4: (0, 1), 6: (1, 1), 0: (2, 0), 2: (3, 0)}

        @block.scalar
        def _(act):
            nc.scalar.preload_act_table(ACT.Silu)

            def split(j, q):
                def high():
                    act.wait_ge(raw_in[q], 48 * (j + 1))
                    if not (isinstance(j, int) and j == 0):
                        act.wait_ge(l2_done, FC * (j - 1) + 2 * q + 2)
                    for raw, hi, _ in quarter(q):
                        last = nc.scalar.activation(hi, raw, ACT.Copy)
                    last.then_inc(w_hi, 1)

                def otherwise():
                    act.wait_ge(w_hi, NQ * j + q)
                    act.sem_inc(w_hi, 1)

                where_fresh(act, j, high, otherwise)

            def x_high(j, s):
                act.wait_ge(x_psum, j + 1)
                nc.scalar.activation(hx[:, s, :, :], XB[:, :].rearrange("p (a n) -> p a n", a=DH), ACT.Copy
                                     ).then_inc(x_hi, 1)

            def evacuate(j, r, s):
                act.wait_ge(l2_done, FC * (j + 1))
                if not (isinstance(r, int) and r == 0):
                    act.wait_ge(y_out[s], 16 * r)
                nc.scalar.activation(ys[:, s, :, :], YB[s][:, :, :], ACT.Copy).then_inc(y_read, 1)

            x_high(0, 0)
            split(0, 0)
            split(0, 1)

            def tile(j, r, s):
                for f in range(FC):
                    n, k = FC * j + f, f % RING
                    if f in SPLIT:
                        q, ahead = SPLIT[f]
                        split(j + ahead, q)
                    act.wait_ge(h_psum, n + 1)
                    if not (isinstance(n, int) and n < RING):
                        act.wait_ge(gated, n - RING + 1)
                    nc.scalar.activation(gate_s[:, k, :], HB[k][:, 0:MT], ACT.Silu).then_inc(silu_done, 1)
                    if f == LP and not (isinstance(j, int) and j == 0):
                        evacuate(j - 1, r if s else r - 1, (s - 1) % UNROLL)
                    if f == 4:
                        x_high(j + 1, (s + 1) % UNROLL)

            tiles(act, tile)
            evacuate(NTILES - 1, NTILES // UNROLL - 1, UNROLL - 1)

        @block.vector
        def _(dve):
            v = nc.vector
            steps = Steps(dve, table_v, 0, 0)
            steps.n, steps.per_batch = 1, 99

            def did(ins):
                steps.did(ins)
                steps.settle()

            did(v.tensor_scalar(cnt_i[:, :], counts[:, :], float(MT - 1), None, ALU.add))
            did(v.tensor_scalar(nt_i[:, :], cnt_i[:, :], MT.bit_length() - 1, None, ALU.arith_shift_right))
            did(v.tensor_copy(nt[:, :], nt_i[:, :]))
            did(v.tensor_copy(ends[:, 0:1], nt[:, 0:1]))
            for e in range(1, E):
                did(v.tensor_tensor(ends[:, e:e + 1], ends[:, e - 1:e], nt[:, e:e + 1], ALU.add))
            tile_no = K("tile")
            did(v.tensor_tensor(past[:, :, :], spread(tile_no[:, 0:1], [[1, NT1], [0, E]]),
                                spread(ends[:, 0:1], [[0, NT1], [1, E]]), ALU.is_ge))
            did(v.tensor_tensor(of_past[:, :, :], past[:, :, :], spread(nt[:, 0:1], [[0, NT1], [1, E]]), ALU.mult))
            did(v.tensor_reduce(expert_f[:, :], past[:, :, :], AX.X, ALU.add))
            did(v.tensor_reduce(first_f[:, :], of_past[:, :, :], AX.X, ALU.add))
            did(v.tensor_tensor(row_f[:, :], tile_no[:, 0:NT1], first_f[:, :], ALU.subtract))
            did(v.tensor_scalar(row_f[:, :], row_f[:, :], float(MT), None, ALU.mult))
            did(v.scalar_tensor_tensor(row_f[:, :], expert_f[:, :], float(REG), row_f[:, :], ALU.mult, ALU.add))
            did(v.tensor_copy(row_i[:, :], row_f[:, :]))
            did(v.tensor_scalar(expert_f[:, :], expert_f[:, :], float(E - 1), None, ALU.min))
            did(v.tensor_copy(expert_i[:, :], expert_f[:, :]))
            did(v.tensor_tensor(fresh_f[:, 1:NT1], expert_f[:, 1:NT1], expert_f[:, 0:NT1 - 1], ALU.not_equal))
            did(v.tensor_copy(fresh_i[:, 1:NT1], fresh_f[:, 1:NT1]))
            did(v.tensor_tensor(pad_f[:, :], counts[:, :], K("region"), ALU.add))
            did(v.tensor_copy(pad_i[:, :], pad_f[:, :]))
            dve.sem_inc(table_ready, 1)
            did(v.tensor_tensor(move[:, :], ends[:, :], nt[:, :], ALU.subtract))
            did(v.tensor_scalar(move[:, :], move[:, :], float(MT), None, ALU.mult))
            did(v.tensor_tensor(move[:, :], move[:, :], K("region"), ALU.subtract))
            did(v.tensor_tensor(step[:, :], move[:, 1:E], move[:, 0:E - 1], ALU.subtract))
            did(v.tensor_tensor(beyond[:, :, :], spread(slot_f[:, 0:1], [[1, NSLOT], [0, E - 1]]),
                                spread(K("region")[:, 1:2], [[0, NSLOT], [1, E - 1]]), ALU.is_ge))
            did(v.tensor_tensor(beyond[:, :, :], beyond[:, :, :], spread(step[:, 0:1], [[0, NSLOT], [1, E - 1]]), ALU.mult))
            did(v.tensor_reduce(moved[:, :], beyond[:, :, :], AX.X, ALU.add))
            did(v.tensor_tensor(slot_f[:, :], slot_f[:, :], moved[:, :], ALU.add))

            def split(j, q):
                def low():
                    dve.wait_ge(w_hi, NQ * j + q + 1)
                    for raw, hi, lo in quarter(q):
                        last = v.tensor_tensor(lo, raw, hi.bitcast(F32), ALU.subtract)
                    last.then_inc(w_lo, 1)

                def otherwise():
                    dve.wait_ge(w_lo, NQ * j + q)
                    dve.sem_inc(w_lo, 1)

                where_fresh(dve, j, low, otherwise)

            def x_low(j, s):
                dve.wait_ge(x_hi, j + 1)
                v.tensor_tensor(lx[:, s, :, :], XB[:, :].rearrange("p (a n) -> p a n", a=DH),
                                hx[:, s, :, :].bitcast(F32), ALU.subtract).then_inc(x_lo, 1)

            x_low(0, 0)
            split(0, 0)
            split(0, 1)

            def tile(j, r, s):
                for f in range(FC):
                    n, k = FC * j + f, f % RING
                    if f in SPLIT:
                        q, ahead = SPLIT[f]
                        split(j + ahead, q)
                    dve.wait_ge(silu_done, n + 1)
                    if not (isinstance(n, int) and n < RING):
                        dve.wait_ge(l2_done, n - RING + 1)
                    v.tensor_tensor(prod[:, k, :], gate_s[:, k, :], HB[k][:, MT:2 * MT], ALU.mult).then_inc(gated, 1)
                    dve.wait_ge(gated, n + 1)
                    v.tensor_copy(hh[:, k, :], prod[:, k, :]).then_inc(h_hi, 1)
                    dve.wait_ge(h_hi, n + 1)
                    v.tensor_tensor(lh[:, k, :], prod[:, k, :], hh[:, k, :].bitcast(F32), ALU.subtract
                                    ).then_inc(h_lo, 1)
                    if f == 4:
                        x_low(j + 1, (s + 1) % UNROLL)

            tiles(dve, tile)


def combine(nc, A, dram):
    with ExitStack() as ctx:
        def sb(name, shape, dt=F32):
            return ctx.enter_context(nc.sbuf_tensor(name, shape, dt))

        def sem(name):
            return ctx.enter_context(nc.semaphore(name))

        slot_f, top2, eps_ln = A["slot_f"], A["top2"], A["eps_ln"]
        RB = 2
        NG = 2 * TT
        slots = sb("slots", [P, B * NG], U32)
        stage = sb("stage", [P, RB, NG], U32)
        diff = sb("diff", [P, B * TT])
        expd = sb("expd", [P, B * TT])
        den = sb("den", [P, B * TT])
        wt = sb("wt", [P, B * TT, 2])
        got = sb("got", [P, RB, NG, D])
        x1 = sb("x1s", [P, RB, TT, D])
        z = sb("z", [P, RB, TT, D])
        res = sb("res", [P, RB, TT, D])
        wts = sb("wts", [P, RB, NG])
        st = sb("cst", [P, RB, TT, 6])
        mv = sb("cmv", [P, RB, TT, 2])
        lnv = sb("clnv", [P, RB, TT])
        rr = sb("crr", [P, RB, TT])

        setup_v, exp_done = sem("csetup_v"), sem("cexp_done")
        staged = sem("staged")
        gathered = [sem(f"gathered{n}") for n in range(RB)]
        x1_in = [sem(f"x1_in{n}") for n in range(RB)]
        out_done = [sem(f"out_done{n}") for n in range(RB)]
        summed, var_ready, ln_done, rstd_ready, res_ready = (
            sem("csummed"), sem("cvar_ready"), sem("cln_done"), sem("crstd_ready"), sem("res_ready"))
        chain, passed = sem("cchain"), sem("cpassed")

        block = ctx.enter_context(nc.Block())

        def batches(eng, batch):
            for n in range(RB):
                batch(n, 0, n)
            with eng.Fori(1, B // RB) as r:
                for n in range(RB):
                    batch(r * RB + n, r, n)

        def rows(name, b):
            return dram[name][bass.ds(b * S, S), :].rearrange("(t p) n -> p t n", p=P)

        @block.sync
        def _(sp):
            def batch(b, r, n):
                if not (isinstance(r, int) and r == 0):
                    sp.wait_ge(res_ready, b - 1)
                sp.dma_start(x1[:, n, :, :], rows("x1", b)).then_inc(x1_in[n], 16)

            batches(sp, batch)

        @block.gpsimd
        def _(pool):
            def batch(b, r, n):
                if not (isinstance(r, int) and r == 0):
                    pool.wait_ge(gathered[n], 16 * NG * r)
                    pool.wait_ge(summed, b - 1)
                pool.sem_inc(passed, 1)
                nc.gpsimd.tensor_copy(stage[:, n, :], slots[:, bass.ds(b * NG, NG)]).then_inc(staged, 1)
                pool.wait_ge(staged, b + 1)
                pool.sem_inc(passed, 1)
                for c in range(NG):
                    nc.gpsimd.indirect_dma_start(
                        got[:, n, c, :], None, dram["ys"], bass.IndirectOffsetOnAxis(ap=stage[:, n, c:c + 1], axis=0)
                    ).then_inc(gathered[n], 16)

            pool.wait_ge(setup_v, 1)
            batches(pool, batch)

        @block.scalar
        def _(act):
            nc.scalar.preload_act_table_set("natural_log_exp_and_others")
            act.wait_ge(setup_v, 2)
            nc.scalar.activation(expd[:, :], diff[:, :], ACT.Exp).then_inc(exp_done, 1)

            def batch(b, r, n):
                act.wait_ge(var_ready, b + 1)
                nc.scalar.activation(lnv[:, n, :], mv[:, n, :, 1], ACT.Ln, bias=eps_ln[:, :]).then_inc(ln_done, 1)
                act.wait_ge(ln_done, b + 1)
                nc.scalar.activation(rr[:, n, :], lnv[:, n, :], ACT.Exp, scale=-0.5).then_inc(rstd_ready, 1)
                act.wait_ge(res_ready, b + 1)
                act.dma_start(rows("out", b), res[:, n, :, :]).then_inc(out_done[n], 16)

            batches(act, batch)
            for n in range(RB):
                act.wait_ge(out_done[n], 16 * (B // RB))

        @block.vector
        def _(dve):
            v = nc.vector
            steps = Steps(dve, setup_v, 0, 0)
            steps.per_batch = 99

            def did(ins):
                steps.did(ins)
                steps.settle()

            did(v.tensor_copy(slots[:, :], slot_f[:, :]))
            t2 = top2[:, :].rearrange("p (t k) -> p t k", k=2)
            did(v.tensor_tensor(diff[:, :], t2[:, :, 1], t2[:, :, 0], ALU.subtract))
            dve.wait_ge(exp_done, 1)
            did(v.tensor_scalar(den[:, :], expd[:, :], 1.0, None, ALU.add))
            did(v.reciprocal(wt[:, :, 0], den[:, :]))
            did(v.tensor_tensor(wt[:, :, 1], expd[:, :], wt[:, :, 0], ALU.mult))
            wflat = wt[:, :, :].rearrange("p t k -> p (t k)")

            def batch(b, r, n):
                s = Steps(dve, chain, 4, b)
                s.did(v.tensor_copy(wts[:, n, :], wflat[:, bass.ds(b * NG, NG)]))
                s.settle()
                dve.wait_ge(gathered[n], 16 * NG * (r + 1))
                for t in range(TT):
                    last = v.tensor_scalar(z[:, n, t, :], got[:, n, 2 * t, :], wts[:, n, 2 * t:2 * t + 1], None, ALU.mult)
                s.did(last)
                s.settle()
                for t in range(TT):
                    last = v.scalar_tensor_tensor(z[:, n, t, :], got[:, n, 2 * t + 1, :], wts[:, n, 2 * t + 1:2 * t + 2],
                                                  z[:, n, t, :], ALU.mult, ALU.add)
                last.then_inc(summed, 1)
                dve.wait_ge(summed, b + 1)
                dve.sem_inc(passed, 1)
                for t in range(TT):
                    last = v.bn_stats(st[:, n, t, :], z[:, n, t, :])
                s.did(last)
                s.settle()
                dve.sem_inc(passed, 1)
                for t in range(TT):
                    last = v.bn_aggr(mv[:, n, t, :], st[:, n, t, :])
                last.then_inc(var_ready, 1)
                dve.wait_ge(rstd_ready, b + 1)
                if not (isinstance(r, int) and r == 0):
                    dve.wait_ge(out_done[n], 16 * r)
                for t in range(TT):
                    last = v.tensor_scalar(res[:, n, t, :], z[:, n, t, :], mv[:, n, t, 0:1], rr[:, n, t:t + 1],
                                           ALU.subtract, ALU.mult)
                s.did(last)
                s.settle()
                dve.wait_ge(x1_in[n], 16 * (r + 1))
                v.tensor_tensor(res[:, n, :, :], res[:, n, :, :], x1[:, n, :, :], ALU.add).then_inc(res_ready, 1)

            batches(dve, batch)


def sandwich(nc, dram, out):
    for name, rows in (("x1", NTOK), ("xs", ROWS), ("ys", NTILES * MT)):
        dram[name] = nc.dram_tensor(name, [rows, D], F32, kind="Internal").ap()
    dram["out"] = out
    with ExitStack() as ctx:
        def sb(name, shape):
            return ctx.enter_context(nc.sbuf_tensor(name, shape, F32))

        A = {"const": sb("const", [P, NCONST]), "eps_ln": sb("eps_ln", [P, 1]), "eps_rms": sb("eps_rms", [P, 1]),
             "counts": sb("counts", [P, E]), "slot_f": sb("slot_f", [P, 2 * TT * B]), "top2": sb("top2", [P, 2 * TT * B]),
             "const_in": ctx.enter_context(nc.semaphore("const_in")),
             "eps_set": ctx.enter_context(nc.semaphore("eps_set"))}
        attend(nc, A, dram)
        experts(nc, A, dram)
        combine(nc, A, dram)


def constants():
    c = np.zeros((P, NCONST), np.float32)

    def put(name, x):
        at, n = CONST[name]
        c[:, at:at + n] = x

    r = np.arange(P)
    put("ident", np.eye(P, dtype=np.float32))
    put("before", (r[:, None] < r[None, :]).astype(np.float32))
    put("ones", 1.0)
    put("mask0", np.where(r[None, :] >= r[:, None], 0.0, NEG))
    d = np.arange(P + WIN)[None, :] - r[:, None]
    put("mask1", np.where((d >= 0) & (d < WIN), 0.0, NEG))
    for l, turn in enumerate((1e6, 1e4)):
        inv = np.float32(1.0) / np.float32(turn) ** (np.arange(0, HD, 2, dtype=np.float32) / np.float32(HD))
        ang = np.arange(S, dtype=np.float32)[:, None] * inv[None, :].astype(np.float32)
        cos, sin = np.cos(ang), np.sin(ang)
        both = np.stack([cos, cos], -1), np.stack([-sin, sin], -1)
        for name, x in zip((f"cos{l}", f"sin{l}"), both):
            put(name, x.reshape(TT, P, HD).transpose(1, 0, 2).reshape(P, TT * HD))
    put("expert", np.arange(E)[None, :])
    put("region", np.arange(E)[None, :] * REG)
    put("tile", np.arange(NTILES + 2)[None, :])
    return c


_ATTN = ["norm1_w", "norm2_w", "g_wq", "g_kv_down", "g_k_up", "g_v_up", "g_wo", "l_wq", "l_wk", "l_wv", "l_wo"]


def kernel(**inputs):
    import numpy as _np
    import concourse.bacc as _bacc
    from concourse.bass_utils import run_bass_kernel_spmd as _run

    arrays = {"x": _np.asarray(inputs["L0_attn_hidden"]).reshape(NTOK, D), "const": constants()}
    for n in _ATTN:
        arrays[n] = _np.asarray(inputs["L0_attn_" + n])
    arrays["gate_w"] = _np.asarray(inputs["L0_ffn_gate_w"])
    for n in ("w1", "w3"):
        arrays[n] = _np.asarray(inputs["L0_ffn_" + n]).reshape(E * D, F)
    arrays["w2"] = _np.asarray(inputs["L0_ffn_w2"]).reshape(E * F, D)
    arrays = {n: _np.ascontiguousarray(a) for n, a in arrays.items()}
    nc = _bacc.Bacc("TRN2", target_bir_lowering=False, num_devices=1)
    dram = {n: nc.dram_tensor(f"in_{n}", a.shape, F32, kind="ExternalInput").ap() for n, a in arrays.items()}
    out = nc.dram_tensor("out_0", (NTOK, D), F32, kind="ExternalOutput").ap()
    sandwich(nc, dram, out)
    r = _run(nc, [{f"in_{n}": a for n, a in arrays.items()}], core_ids=[0])
    return r.results[0]["out_0"].reshape(B, S, D)
```

```python
from contextlib import ExitStack

import concourse.bass as bass
from concourse import mybir
import numpy as np

F32 = mybir.dt.float32
F32R = mybir.dt.float32r
BF16 = mybir.dt.bfloat16
U32 = mybir.dt.uint32
I32 = mybir.dt.int32
ALU = mybir.AluOpType
ACT = mybir.ActivationFunctionType
AX = mybir.AxisListType

P = 128
B, S, D = 8, 512, 256
H, KVH, HD, LAT = 16, 4, 16, 64
WIN = 64
E, F = 8, 1024
TT = S // P
DH = D // P
HPG = H // KVH
NQK = (H + KVH) * HD
NPROJ = NQK + KVH * HD
NTOK = B * S
MT = 256
REG = NTOK + MT
NTILES = 2 * NTOK // MT + E - 1
UNROLL = 3
SPARE = UNROLL + 1
ROWS = E * REG + SPARE * MT
EPS_LN, EPS_RMS = 1e-5, 1e-6
NEG = -1e30
SCALE = HD ** -0.5

CONST = {}
_at = 0
for _name, _n in (("ident", P), ("before", P), ("ones", P), ("mask0", P), ("mask1", P + WIN),
                  ("cos0", TT * HD), ("sin0", TT * HD), ("cos1", TT * HD), ("sin1", TT * HD),
                  ("expert", E), ("region", E), ("tile", NTILES + 2)):
    CONST[_name] = (_at, _n)
    _at += _n
NCONST = _at

CHUNKS = [[(0, 0, 2, 1), (0, 2, 2, 1), (1, 0, 2, 1), (1, 2, 2, 1), (2, 0, 4, 2), (3, 0, 4, 4)],
          [(0, 0, 4, 2), (1, 0, 4, 2), (2, 0, 4, 2), (3, 0, 4, 4)]]


def width(l, kt):
    return S - kt * P if l == 0 else min(S - kt * P, P + WIN)


NCH = [KVH * len(c) for c in CHUNKS]
UNITS = KVH * TT


def chunks_of(l, u):
    g, kt = divmod(u, TT)
    return [(g * len(CHUNKS[l]) + n, c) for n, c in enumerate(CHUNKS[l]) if c[0] == kt]


def unit_of(l, n):
    g, c = divmod(n, len(CHUNKS[l]))
    return g * TT + CHUNKS[l][c][0]


def order(l, b):
    if l == 0:
        return 0 if isinstance(b, int) and b == 0 else 2 * b - 1
    return 2 * B - 1 if isinstance(b, int) and b == B - 1 else 2 * b + 2


def first_chunk(l, b):
    if l == 0:
        return 0 if isinstance(b, int) and b == 0 else (b - 1) * sum(NCH) + NCH[0]
    if isinstance(b, int) and b == B - 1:
        return NCH[0] + (B - 1) * sum(NCH)
    return b * sum(NCH) + 2 * NCH[0]


SURE = -(-2 * NTOK // MT // UNROLL)
NT1 = NTILES + 2
NQ, FC = 4, F // P
HP = F // NQ


def load_quarter(eng, A, dram, e, q):
    c, n = slice(HP * q, HP * (q + 1)), slice(HP // P * q, HP // P * (q + 1))
    for w in ("w1", "w3"):
        eng.dma_start(A["raw_" + w][:, :, c], dram[w][bass.ds(e * D, D), c].rearrange("(a p) n -> p a n", p=P)
                      ).then_inc(A["raw_in"][q], 16)
    eng.dma_start(A["raw_w2"][:, n, :], dram["w2"][bass.ds(e * F + HP * q, HP), :].rearrange("(a p) n -> p a n", p=P)
                  ).then_inc(A["raw_in"][q], 16)


class Steps:

    def __init__(self, eng, sem, per_batch, b):
        self.eng, self.sem, self.per_batch = eng, sem, per_batch
        self.base, self.n = b * per_batch, 0

    def did(self, ins):
        ins.then_inc(self.sem, 1)
        self.n += 1
        assert self.n <= self.per_batch
        return ins

    def settle(self):
        self.eng.wait_ge(self.sem, self.base + self.n)

    def end(self):
        assert self.n == self.per_batch, (self.n, self.per_batch)


def spread(ap, dims):
    return bass.AP(ap.tensor, ap.offset, [list(ap.ap[0])] + dims)


def tile_table(nc, dve, A, sb, done):
    v, NSLOT = nc.vector, 2 * TT * B
    const, counts, slot_f = A["const"], A["counts"], A["slot_f"]
    expert_i, fresh_i, live_i, row_i, round_i = (A[n] for n in ("expert_i", "fresh_i", "live_i", "row_i", "round_i"))
    cnt_i = sb("cnt_i", [P, E], I32)
    nt_i = sb("nt_i", [P, E], I32)
    nt = sb("nt", [P, E])
    ends = sb("ends", [P, E])
    upto = sb("upto", [P, E, E])
    past = sb("past", [P, NT1, E])
    of_past = sb("of_past", [P, NT1, E])
    expert_f = sb("expert_f", [P, NT1])
    first_f = sb("first_f", [P, NT1])
    row_f = sb("row_f", [P, NT1])
    fresh_f = sb("fresh_f", [P, NT1])
    live_f = sb("live_f", [P, NT1])
    round_f = sb("round_f", [P, 1])
    move, step = sb("move", [P, E]), sb("step", [P, E - 1])
    beyond, moved = sb("beyond", [P, NSLOT, E - 1]), sb("moved", [P, NSLOT])
    steps = Steps(dve, done, 99, 0)

    def K(name):
        at, n = CONST[name]
        return const[:, at:at + n]

    def did(ins):
        steps.did(ins)
        steps.settle()

    did(v.tensor_scalar(cnt_i[:, :], counts[:, :], float(MT - 1), None, ALU.add))
    did(v.tensor_scalar(nt_i[:, :], cnt_i[:, :], MT.bit_length() - 1, None, ALU.arith_shift_right))
    did(v.tensor_copy(nt[:, :], nt_i[:, :]))
    no = K("expert")
    did(v.tensor_tensor(upto[:, :, :], spread(no[:, 0:1], [[1, E], [0, E]]), spread(no[:, 0:1], [[0, E], [1, E]]),
                        ALU.is_ge))
    did(v.tensor_tensor(upto[:, :, :], upto[:, :, :], spread(nt[:, 0:1], [[0, E], [1, E]]), ALU.mult))
    did(v.tensor_reduce(ends[:, :], upto[:, :, :], AX.X, ALU.add))
    tile_no = K("tile")
    did(v.tensor_tensor(past[:, :, :], spread(tile_no[:, 0:1], [[1, NT1], [0, E]]),
                        spread(ends[:, 0:1], [[0, NT1], [1, E]]), ALU.is_ge))
    did(v.tensor_tensor(of_past[:, :, :], past[:, :, :], spread(nt[:, 0:1], [[0, NT1], [1, E]]), ALU.mult))
    did(v.tensor_reduce(expert_f[:, :], past[:, :, :], AX.X, ALU.add))
    did(v.tensor_reduce(first_f[:, :], of_past[:, :, :], AX.X, ALU.add))
    did(v.tensor_tensor(row_f[:, :], tile_no[:, 0:NT1], first_f[:, :], ALU.subtract))
    did(v.tensor_scalar(row_f[:, :], row_f[:, :], float(MT), None, ALU.mult))
    did(v.scalar_tensor_tensor(row_f[:, :], expert_f[:, :], float(REG), row_f[:, :], ALU.mult, ALU.add))
    did(v.tensor_copy(row_i[:, :], row_f[:, :]))
    did(v.tensor_scalar(live_f[:, :], expert_f[:, :], float(E), None, ALU.is_lt))
    did(v.tensor_copy(live_i[:, :], live_f[:, :]))
    at = SURE * UNROLL
    did(v.tensor_reduce(round_f[:, :], live_f[:, at:NTILES:UNROLL], AX.X, ALU.add))
    did(v.tensor_scalar(round_f[:, :], round_f[:, :], float(SURE - 1), None, ALU.add))
    did(v.tensor_copy(round_i[:, :], round_f[:, :]))
    did(v.tensor_scalar(expert_f[:, :], expert_f[:, :], float(E - 1), None, ALU.min))
    did(v.tensor_copy(expert_i[:, :], expert_f[:, :]))
    did(v.tensor_tensor(fresh_f[:, 1:NT1], expert_f[:, 1:NT1], expert_f[:, 0:NT1 - 1], ALU.not_equal))
    did(v.tensor_scalar(fresh_f[:, 0:1], expert_f[:, 0:1], 1.0, None, ALU.min))
    did(v.tensor_copy(fresh_i[:, :], fresh_f[:, :]))
    dve.sem_inc(A["table_ready"], 1)
    did(v.tensor_tensor(move[:, :], ends[:, :], nt[:, :], ALU.subtract))
    did(v.tensor_scalar(move[:, :], move[:, :], float(MT), None, ALU.mult))
    did(v.tensor_tensor(move[:, :], move[:, :], K("region"), ALU.subtract))
    did(v.tensor_tensor(step[:, :], move[:, 1:E], move[:, 0:E - 1], ALU.subtract))
    did(v.tensor_tensor(beyond[:, :, :], spread(slot_f[:, 0:1], [[1, NSLOT], [0, E - 1]]),
                        spread(K("region")[:, 1:2], [[0, NSLOT], [1, E - 1]]), ALU.is_ge))
    did(v.tensor_tensor(beyond[:, :, :], beyond[:, :, :], spread(step[:, 0:1], [[0, NSLOT], [1, E - 1]]), ALU.mult))
    did(v.tensor_reduce(moved[:, :], beyond[:, :, :], AX.X, ALU.add))
    did(v.tensor_tensor(slot_f[:, :], slot_f[:, :], moved[:, :], ALU.add))


def attend(nc, A, dram):
    with ExitStack() as ctx:
        def sb(name, shape, dt=F32):
            return ctx.enter_context(nc.sbuf_tensor(name, shape, dt))

        def pb(name, shape, dt=F32):
            return ctx.enter_context(nc.psum_tensor(name, shape, dt))

        def sem(name):
            return ctx.enter_context(nc.semaphore(name))

        const, eps_ln, eps_rms = A["const"], A["eps_ln"], A["eps_rms"]
        counts, slot_f, top2 = A["counts"], A["slot_f"], A["top2"]

        def K(name, rows=P):
            at, n = CONST[name]
            return const[0:rows, at:at + n]

        ident = K("ident")
        ident_b = sb("ident_b", [P, P], BF16)
        before_b = sb("before_b", [P, P], BF16)
        ones_b = sb("ones_b", [P, P], BF16)
        zeros_b = sb("zeros_b", [P, P], BF16)
        mask_b = [sb(f"mask_b{l}", [P, CONST[f"mask{l}"][1]], BF16) for l in range(2)]
        W = [sb(f"W{l}", [P, DH, NPROJ]) for l in range(2)]
        WO = [sb(f"WO{l}", [P, KVH // 2, D]) for l in range(2)]
        gate = sb("gate", [P, DH, E])
        normw = sb("normw", [P, 2, DH])
        down = sb("down", [P, DH, LAT])
        up = sb("up", [LAT, 2 * KVH * HD])
        downT = sb("downT", [LAT, DH, P])

        Xin = sb("Xin", [P, TT, D])
        Hs = sb("Hs", [P, 4 * TT * D])
        xn = sb("xn", [P, TT, D])
        xT = sb("xT", [P, DH, S])
        R = sb("R", [P, TT, NQK])
        T2 = sb("T2", [P, 2, NQK])
        SQ = sb("SQ", [P, 2, NQK])
        SS = sb("SS", [P, TT, H + KVH])
        RL = sb("RL", [P, TT, H + KVH])
        RS = sb("RS", [P, TT, H + KVH])
        hi_q = sb("hi_q", [P, 2, S], F32R)
        lo_q = sb("lo_q", [P, 2, S], F32R)
        hi_k = sb("hi_k", [KVH * HD, S], F32R)
        lo_k = sb("lo_k", [KVH * HD, S], F32R)
        QS = [sb(f"QS{l}", [P, 2, HPG * S], F32R) for l in range(2)]
        KS = [sb(f"KS{l}", [P, KVH, S], F32R) for l in range(2)]
        VA = [sb(f"VA{l}", [P, TT, KVH, 2 * HD]) for l in range(2)]
        VA_own = [sb(f"VA_own{l}", [P, TT, KVH, 2 * HD]) for l in range(2)]
        probs = sb("probs", [P, 4, 1024])
        turned = sb("turned", [P, S])
        both = sb("both", [P, S])
        inv = sb("inv", [P, S // 32])
        OT = [sb(f"OT{l}", [P, KVH // 2, S]) for l in range(2)]
        st = sb("st", [P, TT, 6])
        mv = sb("mv", [P, TT, 2])
        vv = sb("vv", [P, TT])
        lnv = sb("lnv", [P, TT])
        rr = sb("rr", [P, TT])
        Xres = sb("Xres", [P, TT, D])
        Ff = sb("Ff", [P, TT, D])
        FT = sb("FT", [P, DH, S])
        st2 = sb("st2", [P, TT, 6])
        mv2 = sb("mv2", [P, TT, 2])
        lnv2 = sb("lnv2", [P, TT])
        rr2 = sb("rr2", [P, TT])
        lg = sb("lg", [P, TT, E])
        mx = sb("mx", [P, TT, 8])
        ix = sb("ix", [P, TT, 8], U32)
        ixf = sb("ixf", [P, TT, 2])
        oh = sb("oh", [P, 2, TT, E])
        ohb = sb("ohb", [P, TT, E], BF16)
        pos = sb("pos", [P, TT, E])
        slot_u = sb("slot_u", [P, TT * 2], U32)
        zeros = sb("zeros", [P, MT // P, D])
        pad_i = sb("pad_i", [P, E], I32)
        base = sb("base", [P, E])

        SC = [pb(f"SC{n}", [P, 1024]) for n in range(2)]
        OP = pb("OP", [P, 512])
        PR = [pb(f"PR{n}", [P, 512]) for n in range(3)]

        q_stack = [nc.dram_tensor(f"q_stack{l}", [KVH, 2, HD, HPG, S], F32, kind="Internal").ap()
                   for l in range(2)]
        k_stack = [nc.dram_tensor(f"k_stack{l}", [2, KVH * HD, S], F32, kind="Internal").ap()
                   for l in range(2)]

        two = range(2)
        UNSTACK, STACK = 16 * 10, 16 * 3
        wts_in, wo_in = sem("wts_in"), sem("wo_in")
        zeros_set, pads_zeroed, spare_zeroed = sem("zeros_set"), sem("pads_zeroed"), sem("spare_zeroed")
        ups_in = sem("ups_in")
        nw_in = sem("nw_in")
        setup_v = sem("setup_v")
        setup_g = sem("setup_g")
        setup_pe = sem("setup_pe")
        x_in, x_used = sem("x_in"), sem("x_used")
        norm_v = [sem(f"norm_v{l}") for l in two]
        var_ready = [sem(f"var_ready{l}") for l in two]
        ln_done = [sem(f"ln_done{l}") for l in two]
        rstd_ready = [sem(f"rstd_ready{l}") for l in two]
        xn_ready = [sem(f"xn_ready{l}") for l in two]
        xt_psum = [sem(f"xt_psum{l}") for l in two]
        xt_act = [sem(f"xt_act{l}") for l in two]
        xt_dve = [sem(f"xt_dve{l}") for l in two]
        proj_done = [sem(f"proj_done{l}") for l in two]
        roped = [sem(f"roped{l}") for l in two]
        squared = [sem(f"squared{l}") for l in two]
        summed = [sem(f"summed{l}") for l in two]
        rot_ready = [sem(f"rot_ready{l}") for l in two]
        qk_ln = [sem(f"qk_ln{l}") for l in two]
        qk_rstd = [sem(f"qk_rstd{l}") for l in two]
        qk_ready = [sem(f"qk_ready{l}") for l in two]
        qkt_psum = [sem(f"qkt_psum{l}") for l in two]
        hi_done = [sem(f"hi_done{l}") for l in two]
        lo_done = [sem(f"lo_done{l}") for l in two]
        unstacked = [sem(f"unstacked{l}") for l in two]
        stacked = [[sem(f"stacked{l}_{g}") for g in range(KVH)] for l in two]
        scored, exped = sem("scored"), sem("exped")
        pv_done = sem("pv_done")
        op_read, sums_inv, scaled, ot_done = sem("op_read"), sem("sums_inv"), sem("scaled"), sem("ot_done")
        wo_done = [sem(f"wo_done{l}") for l in two]
        resid = [sem(f"resid{l}") for l in two]
        xres_in = sem("xres_in")
        tail_v = sem("tail_v")
        var2_ready, ln2_done, rstd2_ready = sem("var2_ready"), sem("ln2_done"), sem("rstd2_ready")
        x1_ready, x1_out = sem("x1_ready"), sem("x1_out")
        f_ready, ft_psum, ft_act, ft_dve = sem("f_ready"), sem("ft_psum"), sem("ft_act"), sem("ft_dve")
        logits_done, picks_ready, pos_done = sem("logits_done"), sem("picks_ready"), sem("pos_done")
        slots_ready, scattered = sem("slots_ready"), A["scattered"]
        f_free = sem("f_free")
        pads_ready, counts_ready, table_v = sem("pads_ready"), sem("counts_ready"), sem("table_v")
        passed_v, passed_g = sem("passed_v"), sem("passed_g")

        block = ctx.enter_context(nc.Block())

        def alone(eng, passed):
            eng.sem_inc(passed, 1)

        def program(eng, half, finish_only_wo):
            half(att=None, prep=(0, 0), wo=None, tail=None, prev=None)
            half(att=(0, 0), prep=(0, 1), wo=None, tail=None, prev=None)
            finish_only_wo(0, 0)
            half(att=(0, 1), prep=(1, 0), wo=None, tail=None, prev=0)
            half(att=(1, 0), prep=(0, 2), wo=(0, 1), tail=None, prev=0)
            with eng.Fori(2, B - 1) as i:
                half(att=(0, i), prep=(1, i - 1), wo=(1, i - 2), tail=None, prev=1)
                half(att=(1, i - 1), prep=(0, i + 1), wo=(0, i), tail=i - 2, prev=0)
            half(att=(0, B - 1), prep=(1, B - 2), wo=(1, B - 3), tail=None, prev=1)
            finish_only_wo(0, B - 1)
            half(att=(1, B - 2), prep=(1, B - 1), wo=None, tail=B - 3, prev=0)
            finish_only_wo(1, B - 2)
            half(att=(1, B - 1), prep=None, wo=None, tail=B - 2, prev=1)
            finish_only_wo(1, B - 1)
            half(att=None, prep=None, wo=None, tail=B - 1, prev=None)

        def va(l, b):
            own = isinstance(b, int) and b == (B - 1 if l else 0)
            return VA_own[l] if own else VA[l]

        def hs(b, t0=0, n=TT):
            return Hs[:, bass.ds((b % 4) * (TT * D) + t0 * D, n * D)]

        PLACES = [dict(turn=2, project=(4, 5, 6, 7), norm=8, parts=10, out=(12, 15)),
                  dict(turn=3, project=(4, 5, 6, 7), norm=8, parts=10, out=(12, 15),
                       stats=(2, 3, 4, 6, 6), f_turn=(10, 11), logits=12, ranks=14)]

        def places(att):
            return PLACES[1 if att is None else att[0]]

        @block.sync
        def _(sp):
            def load_x(b):
                sp.dma_start(Xin[:, :, :], dram["x"][bass.ds(b * S, S), :].rearrange("(t p) n -> p t n", p=P)
                             ).then_inc(x_in, 16)

            load_x(0)
            sp.dma_start(const[:, :], dram["const"]).then_inc(A["const_in"], 16)
            for l, w in enumerate(("norm1_w", "norm2_w")):
                sp.dma_start(normw[:, l, :], dram[w].rearrange("(a p) -> p a", p=P),
                             allow_slow_non_contiguous=True).then_inc(nw_in, 16)
            sp.dma_start(down[:, :, :], dram["g_kv_down"].rearrange("(a p) n -> p a n", p=P)).then_inc(ups_in, 16)
            sp.dma_start(up[:, 0:KVH * HD], dram["g_k_up"]).then_inc(ups_in, 16)
            sp.dma_start(up[:, KVH * HD:], dram["g_v_up"]).then_inc(ups_in, 16)
            sp.dma_start(W[0][:, :, 0:D], dram["g_wq"].rearrange("(a p) n -> p a n", p=P)).then_inc(wts_in, 16)
            for w, at in (("l_wq", 0), ("l_wk", D), ("l_wv", NQK)):
                v = dram[w].rearrange("(a p) n -> p a n", p=P)
                sp.dma_start(W[1][:, :, at:at + v.shape[2]], v).then_inc(wts_in, 16)
            sp.dma_start(gate[:, :, :], dram["gate_w"].rearrange("(a p) n -> p a n", p=P)).then_inc(wts_in, 16)
            for l, w in enumerate(("g_wo", "l_wo")):
                v = dram[w].rearrange("(m two h d) n -> h two d m n", two=2, h=HPG, d=HD)
                for h in range(HPG):
                    for n in range(2):
                        row = 32 * h + HD * n
                        sp.dma_start(WO[l][row:row + HD, :, :], v[h, n]).then_inc(wo_in, 16)

            def half(att, prep, wo, tail, prev):
                if prep is not None:
                    l, b = prep
                    if l == 1 and not (isinstance(b, int) and b + 2 >= B):
                        sp.wait_ge(x_used, b + 2)
                        load_x(b + 2)
                    elif l == 0 and isinstance(b, int) and b < 2:
                        if b == 1:
                            sp.wait_ge(x_used, 1)
                            load_x(1)
                if tail is not None:
                    sp.wait_ge(x1_out, tail * 16 + 1)
                    sp.wait_ge(f_ready, tail + 1)
                    sp.dma_start(Xres[:, :, :], dram["x"][bass.ds(tail * S, S), :].rearrange("(t p) n -> p t n", p=P)
                                 ).then_inc(xres_in, 16)
                    sp.wait_ge(x1_ready, tail + 1)
                    sp.dma_start(dram["x1"][bass.ds(tail * S, S), :].rearrange("(t p) n -> p t n", p=P),
                                 Xres[:, :, :]).then_inc(x1_out, 16)
                if prep is not None:
                    l, b = prep
                    if not (isinstance(b, int) and b == 0):
                        for g in range(KVH):
                            sp.wait_ge(stacked[l][g], STACK * b)
                    for n in range(3):
                        for part, done, q, k in ((0, hi_done, hi_q, hi_k), (1, lo_done, lo_q, lo_k)):
                            sp.wait_ge(done[l], 3 * b + n + 1)
                            if n == 2:
                                sp.dma_start(k_stack[l][part], k[:, :].bitcast(F32)).then_inc(unstacked[l], 16)
                                continue
                            for g in range(2):
                                sp.dma_start(q_stack[l][2 * n + g, part].rearrange("d h s -> h d s"),
                                             q[64 * g:64 * (g + 1), n, :].bitcast(F32)).then_inc(unstacked[l], 16)
                    sp.wait_ge(unstacked[l], UNSTACK * (b + 1))
                    if not (isinstance(b, int) and b == 0):
                        sp.wait_ge(exped, first_chunk(l, b - 1) + NCH[l])
                    for g in range(KVH):
                        row = 64 * (g % 2)
                        q = q_stack[l][g]
                        sp.dma_start(QS[l][row:row + 64, g // 2, :].bitcast(F32),
                                     bass.AP(q.tensor, q.offset, [[0, 2], [HPG * S, 2 * HD], [1, HPG * S]])
                                     ).then_inc(stacked[l][g], 16)
                        for part in range(2):
                            k = k_stack[l][part, HD * g:HD * (g + 1)]
                            sp.dma_start(KS[l][row + 32 * part:row + 32 * part + 32, g, :].bitcast(F32),
                                         bass.AP(k.tensor, k.offset, [[0, 2], [S, HD], [1, S]])
                                         ).then_inc(stacked[l][g], 16)

            sp.sem_inc(x1_out, 1)
            program(sp, half, lambda l, b: None)
            sp.wait_ge(zeros_set, 1)
            for name, r0, n in (("xs", E * REG, SPARE), ("ys", SURE * UNROLL * MT, NTILES - SURE * UNROLL)):
                for m in range(n):
                    at = r0 + m * MT
                    sp.dma_start(dram[name][at:at + MT, :].rearrange("(m p) n -> p m n", p=P), zeros[:, :, :]
                                 ).then_inc(spare_zeroed, 16)
            for q in range(NQ):
                load_quarter(sp, A, dram, 0, q)
            sp.wait_ge(pads_ready, 1)
            for e in range(E):
                at = sp.value_load(pad_i[0:1, e:e + 1], min_val=0, max_val=ROWS - MT)
                sp.dma_start(dram["xs"][bass.ds(at, MT), :].rearrange("(m p) n -> p m n", p=P), zeros[:, :, :]
                             ).then_inc(pads_zeroed, 16)
            sp.wait_ge(x1_out, 16 * B + 1)
            sp.wait_ge(spare_zeroed, 16 * (SPARE + NTILES - SURE * UNROLL))
            sp.wait_ge(A["table_ready"], 1)
            for q in range(NQ):
                sp.wait_ge(A["raw_in"][q], 48)
                other = sp.value_load(A["fresh_i"][0:1, 0:1], min_val=0, max_val=1)
                with sp.If(other):
                    load_quarter(sp, A, dram, sp.value_load(A["expert_i"][0:1, 0:1], min_val=0, max_val=E - 1), q)
                with sp.Else():
                    sp.sem_inc(A["raw_in"][q], 48)
            sp.wait_ge(pads_zeroed, 16 * E)

        @block.gpsimd
        def _(pool):
            nc.gpsimd.memset(zeros[:, :, :], 0.0).then_inc(zeros_set, 1)
            for l in two:
                nc.gpsimd.memset(VA_own[l][:, :, :, :], 1.0).then_inc(setup_g, 1)
                nc.gpsimd.memset(VA[l][:, :, :, :], 1.0).then_inc(setup_g, 1)
                nc.gpsimd.memset(KS[l][:, :, :].bitcast(F32), 0.0).then_inc(setup_g, 1)

            def half(att, prep, wo, tail, prev):
                if prep is not None:
                    l, b = prep
                    for t in range(TT):
                        pool.wait_ge(roped[l], 4 * b + t + 1)
                        nc.gpsimd.tensor_tensor(R[:, t, :], R[:, t, :], T2[:, t % 2, :], ALU.add
                                                ).then_inc(rot_ready[l], 1)
                if tail is not None:
                    pool.wait_ge(slots_ready, tail + 1)
                    alone(pool, passed_g)
                    for t in range(TT):
                        for k in range(2):
                            c = 2 * t + k
                            nc.gpsimd.indirect_dma_start(
                                dram["xs"], bass.IndirectOffsetOnAxis(ap=slot_u[:, c:c + 1], axis=0),
                                Ff[:, t, :], None).then_inc(scattered, 16)
                    if not (isinstance(tail, int) and tail == B - 1):
                        pool.wait_ge(scattered, 16 * 2 * TT * (tail + 1))
                        pool.sem_inc(f_free, 1)

            pool.sem_inc(f_free, 1)
            program(pool, half, lambda l, b: None)

        @block.tensor
        def _(pe):
            mm, tr = nc.tensor.matmul, nc.tensor.transpose
            pe.wait_ge(A["const_in"], 16)
            pe.wait_ge(ups_in, 48)
            for a in range(DH):
                tr(PR[a][0:LAT, 0:P], down[:, a, :], ident).then_inc(setup_pe, 1)
            pe.wait_ge(setup_v, 1)
            for a in range(DH):
                mm(PR[2][:, P * a:P * (a + 1)], downT[:, a, :], up[:, :], start=True, stop=True
                   ).then_inc(setup_pe, 1)

            def score_unit(l, b, u, chunk0):
                g, kt = divmod(u, TT)
                w = width(l, kt)
                mw = CONST[f"mask{l}"][1] if l == 1 and w > P else P
                if kt == 0 and g % 2 == 0:
                    pe.wait_ge(stacked[l][g], STACK * (b + 1))
                    pe.wait_ge(stacked[l][g + 1], STACK * (b + 1))
                for n, (_, h0, nh, per) in chunks_of(l, u):
                    if not (isinstance(chunk0, int) and chunk0 + n < 2):
                        pe.wait_ge(exped, chunk0 + n - 1)
                    sc = SC[n % 2]
                    for j in range(0, nh, per):
                        out = spread(sc[:, 512 * (j // per):512 * (j // per) + 1], [[w, per], [1, w]])
                        q = QS[l][:, g // 2, (h0 + j) * S + kt * P:(h0 + j) * S + kt * P + 1]
                        mm(out, KS[l][:, g, kt * P:(kt + 1) * P], spread(q, [[S, per], [1, w]]),
                           start=True, stop=False)
                        out = spread(sc[:, 512 * (j // per):512 * (j // per) + 1], [[w, per], [1, mw]])
                        last = mm(out, ident_b[:, :], spread(mask_b[l][:, 0:1], [[0, per], [1, mw]]),
                                  start=False, stop=True)
                    last.then_inc(scored, 1)

            def pv_unit(l, b, a, u, chunk0):
                g, kt = divmod(u, TT)
                w = width(l, kt)
                mine = chunks_of(l, u)
                pe.wait_ge(exped, chunk0 + mine[-1][0] + 1)
                if kt == 0 and not (isinstance(a, int) and a == 0 and g == 0):
                    pe.wait_ge(op_read, 4 * a + g)
                if kt == 0 and l == 1:
                    mm(OP[:, :], zeros_b[:, :], spread(ones_b[:, 0:1], [[0, S]]), start=True, stop=False)
                for n, (_, h0, nh, per) in mine:
                    for j in range(nh):
                        h = h0 + j
                        at = 512 * (j // per) + w * (j % per)
                        last = mm(OP[32 * h:32 * h + 32, kt * P:kt * P + w], va(l, b)[:, kt, g, :],
                                  probs[:, n % 4, at:at + w], start=(kt == 0 and l == 0), stop=(kt == TT - 1),
                                  tile_position=(0, 32 * h))
                last.then_inc(pv_done, 1)

            def project_out(l, b, u):
                if (l, u) == (0, 0) and isinstance(b, int) and b == 0:
                    pe.wait_ge(wo_in, 16 * 4 * HPG)
                pe.wait_ge(ot_done, 2 * (order(l, b) + 1))
                if l == 0 and not (isinstance(b, int) and b < 2):
                    pe.wait_ge(resid[1], 2 * (b - 1))
                if l == 1:
                    pe.wait_ge(resid[0], 2 * min(b + 2, B) if isinstance(b, int) else 2 * (b + 2))
                for j in range(2):
                    for m in range(KVH // 2):
                        last = mm(PR[u][:, D * j:D * (j + 1)], OT[l][:, m, (2 * u + j) * P:(2 * u + j + 1) * P],
                                  WO[l][:, m, :], start=(m == 0), stop=(m == KVH // 2 - 1))
                last.then_inc(wo_done[l], 1)

            def half(att, prep, wo, tail, prev):
                at = places(att)
                for u in range(UNITS):
                    if att is not None:
                        la, ba = att
                        chunk0, a = first_chunk(la, ba), order(la, ba)
                        score_unit(la, ba, u, chunk0)
                        if u > 0:
                            pv_unit(la, ba, a, u - 1, chunk0)
                    if prep is not None:
                        l, b = prep
                        if u == at["turn"]:
                            pe.wait_ge(xn_ready[l], b + 1)
                            for f in range(DH):
                                for t in range(TT):
                                    last = tr(PR[f][:, t * P:(t + 1) * P], xn[:, t, f * P:(f + 1) * P], ident)
                                last.then_inc(xt_psum[l], 1)
                        if u in at["project"]:
                            t = at["project"].index(u)
                            if isinstance(b, int) and b == 0 and t == 0:
                                pe.wait_ge(setup_v, 2)
                            if t == 0:
                                pe.wait_ge(xt_act[l], b + 1)
                                pe.wait_ge(xt_dve[l], b + 1)
                            if t == 3:
                                pe.wait_ge(roped[l], 4 * b + 1)
                            bank = PR[(2, 0, 1, 2)[t]]
                            for f in range(DH):
                                last = mm(bank[:, 0:NPROJ], xT[:, f, t * P:(t + 1) * P], W[l][:, f, :],
                                          start=(f == 0), stop=(f == DH - 1))
                            last.then_inc(proj_done[l], 1)
                        if u == at["parts"]:
                            pe.wait_ge(qk_ready[l], 4 * (b + 1))
                            for n in range(3):
                                m = P if n < 2 else KVH * HD
                                for t in range(TT):
                                    last = tr(PR[n][0:m, t * P:(t + 1) * P], R[:, t, n * P:n * P + m], ident)
                                last.then_inc(qkt_psum[l], 1)
                    if wo is not None and u in at["out"]:
                        n = at["out"].index(u)
                        if prep is not None:
                            pe.wait_ge(lo_done[prep[0]], 3 * prep[1] + n + 1)
                        project_out(*wo, n)
                    if tail is not None:
                        b = tail
                        if u in at["f_turn"]:
                            f = at["f_turn"].index(u)
                            if f == 0:
                                pe.wait_ge(f_ready, b + 2)
                                if prep is not None:
                                    pe.wait_ge(lo_done[prep[0]], 3 * (prep[1] + 1))
                            else:
                                pe.wait_ge(ft_act, b + 1)
                            for t in range(TT):
                                last = tr(PR[2][:, t * P:(t + 1) * P], Ff[:, t, f * P:(f + 1) * P], ident)
                            last.then_inc(ft_psum, 1)
                        if u == at["logits"]:
                            pe.wait_ge(ft_dve, b + 1)
                            for t in range(TT):
                                for f in range(DH):
                                    last = mm(PR[2][:, t * E:(t + 1) * E], FT[:, f, t * P:(t + 1) * P],
                                              gate[:, f, :], start=(f == 0), stop=(f == DH - 1))
                            last.then_inc(logits_done, 1)
                        if u == at["ranks"]:
                            pe.wait_ge(picks_ready, b + 1)
                            for t in range(TT + 1):
                                out = PR[2][:, t * E:(t + 1) * E]
                                for s in range(min(t, TT)):
                                    last = mm(out, ones_b[:, :], ohb[:, s, :], start=(s == 0), stop=(t == TT and s == TT - 1))
                                if t < TT:
                                    last = mm(out, before_b[:, :], ohb[:, t, :], start=(t == 0), stop=True)
                            last.then_inc(pos_done, 1)
                if att is not None:
                    pv_unit(la, ba, a, UNITS - 1, chunk0)

            def finish(l, b):
                if b == 0:
                    pe.wait_ge(lo_done[0], 3 * 2)
                else:
                    pe.wait_ge(lo_done[1], 3 * (B - 1 if l == 0 else B))
                for n in range(2):
                    project_out(l, b, n)

            program(pe, half, finish)

        @block.scalar
        def _(act):
            act.wait_ge(A["eps_set"], 2)
            nc.scalar.preload_act_table_set("natural_log_exp_and_others")

            def exp_unit(l, b, a, u, chunk0, prev):
                for n, (kt, h0, nh, per) in chunks_of(l, u):
                    act.wait_ge(scored, chunk0 + n + 1)
                    if n >= 4:
                        act.wait_ge(pv_done, UNITS * a + unit_of(l, n - 4) + 1)
                    elif prev is not None:
                        act.wait_ge(pv_done, UNITS * (a - 1) + unit_of(prev, NCH[prev] + n - 4) + 1)
                    cols = per * width(l, kt)
                    nb = nh // per
                    nc.scalar.activation(spread(probs[:, n % 4, 0:1], [[512, nb], [1, cols]]),
                                         spread(SC[n % 2][:, 0:1], [[512, nb], [1, cols]]),
                                         ACT.Exp, scale=SCALE).then_inc(exped, 1)

            def rsqrt(out, tmp, in_, eps, scale, wait, waited, mid, midv, done):
                act.wait_ge(wait, waited)
                nc.scalar.activation(tmp, in_, ACT.Ln, bias=eps, scale=scale).then_inc(mid, 1)
                act.wait_ge(mid, midv)
                nc.scalar.activation(out, tmp, ACT.Exp, scale=-0.5).then_inc(done, 1)

            def half(att, prep, wo, tail, prev):
                at = places(att)
                for u in range(UNITS):
                    if att is not None:
                        la, ba = att
                        exp_unit(la, ba, order(la, ba), u, first_chunk(la, ba), prev)
                    if prep is not None:
                        l, b = prep
                        if l == 0 and u < 2:
                            rsqrt(rr[:, :], lnv[:, :], vv[:, :], (eps_ln, eps_rms)[u][:, :], 1.0,
                                  var_ready[0], 2 * b + u + 1, ln_done[0], 2 * b + u + 1, rstd_ready[0])
                        if l == 1 and u == 0:
                            rsqrt(rr[:, :], lnv[:, :], vv[:, :], eps_rms[:, :], 1.0,
                                  var_ready[1], b + 1, ln_done[1], b + 1, rstd_ready[1])
                        if u == at["turn"]:
                            act.wait_ge(xt_psum[l], 2 * b + 1)
                            nc.scalar.activation(xT[:, 0, :], PR[0][:, :], ACT.Copy).then_inc(xt_act[l], 1)
                        if u in at["project"]:
                            t = at["project"].index(u)
                            if isinstance(b, int) and b == 0 and t == 0:
                                act.wait_ge(setup_g, 6)
                            act.wait_ge(proj_done[l], 4 * b + t + 1)
                            nc.scalar.activation(va(l, b)[:, t, :, 0:HD],
                                                 PR[(2, 0, 1, 2)[t]][:, NQK:NPROJ].rearrange("p (g d) -> p g d", g=KVH),
                                                 ACT.Copy)
                            if t >= 2:
                                act.wait_ge(summed[l], 4 * b + t - 1)
                            nc.scalar.activation(SQ[:, t % 2, :], PR[(2, 0, 1, 2)[t]][:, 0:NQK], ACT.Square
                                                 ).then_inc(squared[l], 1)
                        if u == at["norm"]:
                            rsqrt(RS[:, :, :], RL[:, :, :], SS[:, :, :], eps_rms[:, :], 1.0 / HD,
                                  summed[l], 4 * (b + 1), qk_ln[l], b + 1, qk_rstd[l])
                        if u == at["parts"]:
                            if l == 1 and isinstance(b, int) and b == B - 1:
                                act.wait_ge(unstacked[1], UNSTACK * b)
                            elif l == 1:
                                act.wait_ge(unstacked[0], UNSTACK * min(b + 2, B) if isinstance(b, int) else UNSTACK * (b + 2))
                            elif isinstance(b, int) and b <= 1:
                                if b == 1:
                                    act.wait_ge(unstacked[0], UNSTACK)
                            else:
                                act.wait_ge(unstacked[1], UNSTACK * (b - 1))
                            for n in range(3):
                                act.wait_ge(qkt_psum[l], 3 * b + n + 1)
                                o = hi_q[:, n, :] if n < 2 else hi_k[:, :]
                                i = PR[n][:, :] if n < 2 else PR[n][0:KVH * HD, :]
                                nc.scalar.activation(o, i, ACT.Copy).then_inc(hi_done[l], 1)
                    if tail is not None:
                        if u in (at["stats"][1], at["stats"][3]):
                            n = int(u == at["stats"][3])
                            rsqrt(rr2[:, :], lnv2[:, :], mv2[:, :, 1], eps_ln[:, :], 1.0,
                                  var2_ready, 2 * tail + n + 1, ln2_done, 2 * tail + n + 1, rstd2_ready)
                        if u == at["f_turn"][0]:
                            act.wait_ge(ft_psum, 2 * tail + 1)
                            nc.scalar.activation(FT[:, 0, :], PR[2][:, :], ACT.Copy).then_inc(ft_act, 1)

            program(act, half, lambda l, b: None)

        @block.vector
        def _(dve):
            v = nc.vector
            v.memset(eps_ln[:, :], EPS_LN).then_inc(A["eps_set"], 1)
            v.memset(eps_rms[:, :], EPS_RMS).then_inc(A["eps_set"], 1)
            dve.wait_ge(A["const_in"], 16)
            for o, i in ((ident_b, "ident"), (before_b, "before"), (ones_b, "ones"), (mask_b[0], "mask0"), (mask_b[1], "mask1")):
                v.tensor_copy(o[:, :], K(i))
            v.memset(zeros_b[:, :], 0.0)
            v.tensor_copy(base[:, :], K("region"))
            dve.wait_ge(setup_pe, DH)
            v.tensor_copy(downT[:, 0, :], PR[0][0:LAT, 0:P])
            v.tensor_copy(downT[:, 1, :], PR[1][0:LAT, 0:P]).then_inc(setup_v, 1)
            dve.wait_ge(nw_in, 32)
            dve.wait_ge(wts_in, 16 * 5)
            dve.wait_ge(setup_pe, 2 * DH)
            for a in range(DH):
                v.tensor_scalar(W[0][:, a, 0:D], W[0][:, a, 0:D], normw[:, 0, a:a + 1], None, ALU.mult)
                v.tensor_scalar(W[0][:, a, D:NPROJ], PR[2][:, P * a:P * (a + 1)], normw[:, 0, a:a + 1], None, ALU.mult)
            for a in range(DH):
                last = v.tensor_scalar(W[1][:, a, :], W[1][:, a, :], normw[:, 1, a:a + 1], None, ALU.mult)
            last.then_inc(setup_v, 1)

            NORM = [6, 4]

            def norm_stats(l, b, s):
                if l == 0:
                    dve.wait_ge(x_in, 16 * (b + 1))
                    src = Xin[:, :, :]
                else:
                    dve.wait_ge(resid[0], 2 * (b + 1))
                    src = hs(b).rearrange("p (t n) -> p t n", t=TT)
                alone(dve, passed_v)
                for t in range(TT):
                    last = v.bn_stats(st[:, t, :], src[:, t, :])
                s.did(last)
                s.settle()
                alone(dve, passed_v)
                for t in range(TT):
                    last = v.bn_aggr(mv[:, t, :], st[:, t, :])
                s.did(last)
                s.settle()
                if l == 0:
                    v.tensor_copy(vv[:, :], mv[:, :, 1]).then_inc(var_ready[0], 1)
                else:
                    s.did(v.tensor_tensor(vv[:, :], mv[:, :, 0], mv[:, :, 0], ALU.mult))
                    s.settle()
                    v.tensor_tensor(vv[:, :], vv[:, :], mv[:, :, 1], ALU.add).then_inc(var_ready[1], 1)

            def layer_norm_h(b, s):
                dve.wait_ge(rstd_ready[0], 2 * b + 1)
                s.did(v.tensor_tensor(vv[:, :], mv[:, :, 1], rr[:, :], ALU.mult))
                s.settle()
                s.did(v.tensor_tensor(vv[:, :], vv[:, :], rr[:, :], ALU.mult))
                for t in range(TT):
                    last = v.tensor_scalar(hs(b, t, 1), Xin[:, t, :], mv[:, t, 0:1], rr[:, t:t + 1],
                                           ALU.subtract, ALU.mult)
                s.did(last)
                s.settle()
                dve.sem_inc(x_used, 1)
                dve.sem_inc(var_ready[0], 1)

            def rms_x(l, b, s):
                dve.wait_ge(rstd_ready[l], 2 * b + 2 if l == 0 else b + 1)
                for t in range(TT):
                    last = v.tensor_scalar(xn[:, t, :], hs(b, t, 1), rr[:, t:t + 1], None, ALU.mult)
                s.did(last)
                s.settle()
                dve.sem_inc(xn_ready[l], 1)

            def rope(l, b, t):
                dve.wait_ge(squared[l], 4 * b + t + 1)
                if t >= 2:
                    dve.wait_ge(rot_ready[l], 4 * b + t - 1)
                qk = PR[(2, 0, 1, 2)[t]][:, 0:NQK]
                tab = [CONST[f"{n}{l}"][0] + t * HD for n in ("cos", "sin")]
                heads = [[HD, H + KVH], [2, HD // 2], [1, 2]]
                over = [[0, H + KVH], [2, HD // 2], [1, 2]]
                v.tensor_tensor(R[:, t, :].rearrange("p (h i two) -> p h i two", i=HD // 2, two=2),
                                spread(qk, heads), spread(const[:, tab[0]:tab[0] + 1], over), ALU.mult)
                swapped = spread(PR[(2, 0, 1, 2)[t]][:, 1:2], [[HD, H + KVH], [2, HD // 2], [-1, 2]])
                v.tensor_tensor(T2[:, t % 2, :].rearrange("p (h i two) -> p h i two", i=HD // 2, two=2),
                                swapped, spread(const[:, tab[1]:tab[1] + 1], over), ALU.mult
                                ).then_inc(roped[l], 1)
                v.tensor_reduce(SS[:, t, :], SQ[:, t % 2, :].rearrange("p (h d) -> p h d", d=HD), AX.X, ALU.add
                                ).then_inc(summed[l], 1)

            def qk_norm(l, b):
                dve.wait_ge(qk_rstd[l], b + 1)
                for t in range(TT):
                    dve.wait_ge(rot_ready[l], 4 * b + t + 1)
                    r = R[:, t, :].rearrange("p (h d) -> p h d", d=HD)
                    v.tensor_tensor(r, r, spread(RS[:, t, 0:1], [[1, H + KVH], [0, HD]]), ALU.mult
                                    ).then_inc(qk_ready[l], 1)

            def low_parts(l, b):
                if l == 1 and isinstance(b, int) and b == B - 1:
                    dve.wait_ge(unstacked[1], UNSTACK * b)
                elif l == 1:
                    dve.wait_ge(unstacked[0], UNSTACK * min(b + 2, B) if isinstance(b, int) else UNSTACK * (b + 2))
                elif isinstance(b, int) and b <= 1:
                    if b == 1:
                        dve.wait_ge(unstacked[0], UNSTACK)
                else:
                    dve.wait_ge(unstacked[1], UNSTACK * (b - 1))
                for n in range(3):
                    dve.wait_ge(hi_done[l], 3 * b + n + 1)
                    o, h = (lo_q[:, n, :], hi_q[:, n, :]) if n < 2 else (lo_k[:, :], hi_k[:, :])
                    i = PR[n][:, :] if n < 2 else PR[n][0:KVH * HD, :]
                    v.tensor_tensor(o, i, h.bitcast(F32), ALU.subtract).then_inc(lo_done[l], 1)

            def normalise(l, a, g):
                first = isinstance(a, int) and 4 * a + g == 0
                if not first:
                    dve.wait_ge(scaled, 4 * a + g)
                dve.wait_ge(pv_done, UNITS * a + TT * (g + 1))
                v.transpose(turned[:, :], OP[:, :]).then_inc(op_read, 1)
                dve.wait_ge(op_read, 4 * a + g + 1)
                blocks = turned[:, :].rearrange("p (q i) -> p q i", i=32)
                filled = both[:, :].rearrange("p (q i) -> p q i", i=32)[:, :, HD * (g % 2):HD * (g % 2 + 1)]
                v.reciprocal(inv[:, :], blocks[:, :, HD]).then_inc(sums_inv, 1)
                dve.wait_ge(sums_inv, 4 * a + g + 1)
                if g % 2 == 0 and not first:
                    dve.wait_ge(ot_done, 2 * a + g // 2)
                v.tensor_tensor(filled, blocks[:, :, 0:HD], spread(inv[:, 0:1], [[1, S // 32], [0, HD]]),
                                ALU.mult).then_inc(scaled, 1)
                if g % 2:
                    dve.wait_ge(scaled, 4 * a + g + 1)
                    v.transpose(OT[l][:, g // 2, :], both[:, :]).then_inc(ot_done, 1)

            def residual(l, b, u):
                dve.wait_ge(wo_done[l], 2 * b + u + 1)
                h = hs(b, 2 * u, 2)
                v.tensor_tensor(h, h, PR[u][:, :], ALU.add).then_inc(resid[l], 1)

            TAIL = 13

            def stats2(b, src, s):
                alone(dve, passed_v)
                for t in range(TT):
                    last = v.bn_stats(st2[:, t, :], src[:, t, :])
                s.did(last)
                s.settle()
                alone(dve, passed_v)
                for t in range(TT):
                    last = v.bn_aggr(mv2[:, t, :], st2[:, t, :])
                last.then_inc(var2_ready, 1)

            def tail_1(b, s):
                dve.wait_ge(resid[1], 2 * (b + 1))
                stats2(b, hs(b).rearrange("p (t n) -> p t n", t=TT), s)

            def tail_2(b, s):
                dve.wait_ge(rstd2_ready, 2 * b + 1)
                dve.wait_ge(xres_in, 16 * (b + 1))
                dve.wait_ge(f_free, b + 1)
                for t in range(TT):
                    last = v.tensor_scalar(Ff[:, t, :], hs(b, t, 1), mv2[:, t, 0:1], rr2[:, t:t + 1],
                                           ALU.subtract, ALU.mult)
                s.did(last)
                s.settle()
                s.did(v.tensor_tensor(Xres[:, :, :], Xres[:, :, :], Ff[:, :, :], ALU.add))
                s.settle()
                dve.sem_inc(x1_ready, 1)
                stats2(b, Xres[:, :, :], s)

            def tail_3(b, s):
                dve.wait_ge(rstd2_ready, 2 * b + 2)
                for t in range(TT):
                    last = v.tensor_scalar(Ff[:, t, :], Xres[:, t, :], mv2[:, t, 0:1], rr2[:, t:t + 1],
                                           ALU.subtract, ALU.mult)
                last.then_inc(f_ready, 1)

            def tail_4(b, s):
                dve.wait_ge(ft_psum, 2 * b + 2)
                v.tensor_copy(FT[:, 1, :], PR[2][:, :]).then_inc(ft_dve, 1)

            def tail_5(b, s):
                dve.wait_ge(logits_done, b + 1)
                s.did(v.tensor_copy(lg[:, :, :], PR[2][:, 0:TT * E].rearrange("p (t e) -> p t e", t=TT)))
                s.settle()
                alone(dve, passed_v)
                for t in range(TT):
                    last = v.max(mx[:, t, :], lg[:, t, :])
                s.did(last)
                s.settle()
                alone(dve, passed_v)
                for t in range(TT):
                    last = v.max_index(ix[:, t, :], mx[:, t, :], lg[:, t, :])
                s.did(last)
                s.settle()
                alone(dve, passed_v)
                v.tensor_copy(top2[:, bass.ds(b * (2 * TT), 2 * TT)].rearrange("p (t k) -> p t k", k=2), mx[:, :, 0:2])
                s.did(v.tensor_copy(ixf[:, :, :], ix[:, :, 0:2]))
                s.settle()
                for k in range(2):
                    last = v.tensor_tensor(oh[:, k, :, :], spread(K("expert"), [[0, TT], [1, E]]),
                                           spread(ixf[:, 0, k:k + 1], [[2, TT], [0, E]]), ALU.is_equal)
                s.did(last)
                s.settle()
                v.tensor_tensor(ohb[:, :, :], oh[:, 0, :, :], oh[:, 1, :, :], ALU.add).then_inc(picks_ready, 1)

            def tail_6(b, s):
                dve.wait_ge(pos_done, b + 1)
                s.did(v.tensor_tensor(pos[:, :, :], PR[2][:, 0:TT * E].rearrange("p (t e) -> p t e", t=TT),
                                      spread(base[:, 0:1], [[0, TT], [1, E]]), ALU.add))
                s.settle()
                s.did(v.tensor_tensor(base[:, :], base[:, :], PR[2][:, TT * E:(TT + 1) * E], ALU.add))
                for k in range(2):
                    last = v.tensor_tensor(oh[:, k, :, :], oh[:, k, :, :], pos[:, :, :], ALU.mult)
                s.did(last)
                s.settle()
                rows = slot_f[:, bass.ds(b * (2 * TT), 2 * TT)].rearrange("p (t k) -> p t k", k=2)
                for k in range(2):
                    last = v.tensor_reduce(rows[:, :, k], oh[:, k, :, :], AX.X, ALU.add)
                s.did(last)
                s.settle()
                alone(dve, passed_v)
                v.tensor_copy(slot_u[:, :], slot_f[:, bass.ds(b * (2 * TT), 2 * TT)]).then_inc(slots_ready, 1)

            def half(att, prep, wo, tail, prev):
                at = places(att)
                if att is not None:
                    la, a = att[0], order(*att)
                if prep is not None:
                    l, b = prep
                    s = Steps(dve, norm_v[l], NORM[l], b)
                    norm_stats(l, b, s)
                if tail is not None:
                    ts = Steps(dve, tail_v, TAIL, tail)
                for u in range(UNITS):
                    if att is not None and u % TT == 0 and u > 0:
                        normalise(la, a, u // TT - 1)
                    if prep is not None:
                        if u == 0 and l == 0:
                            layer_norm_h(b, s)
                        if u == 1:
                            rms_x(l, b, s)
                            s.end()
                        if u == at["turn"]:
                            dve.wait_ge(xt_psum[l], 2 * b + 2)
                            v.tensor_copy(xT[:, 1, :], PR[1][:, :]).then_inc(xt_dve[l], 1)
                        if u in at["project"]:
                            rope(l, b, at["project"].index(u))
                        if u == at["norm"]:
                            qk_norm(l, b)
                        if u == at["parts"]:
                            low_parts(l, b)
                    if tail is not None:
                        if u == at["stats"][0]:
                            tail_1(tail, ts)
                        if u == at["stats"][2]:
                            tail_2(tail, ts)
                        if u == at["stats"][4]:
                            tail_3(tail, ts)
                        if u == at["f_turn"][1]:
                            tail_4(tail, ts)
                        if u == at["logits"]:
                            tail_5(tail, ts)
                    if wo is not None and u in at["out"]:
                        residual(*wo, at["out"].index(u))
                    if tail is not None and u == at["ranks"]:
                        tail_6(tail, ts)
                        ts.end()
                if att is not None:
                    normalise(la, a, KVH - 1)

            def finish(l, b):
                for u in range(2):
                    residual(l, b, u)

            dve.sem_inc(f_ready, 1)
            program(dve, half, finish)
            v.tensor_copy(pad_i[:, :], base[:, :]).then_inc(pads_ready, 1)
            v.tensor_tensor(counts[:, :], base[:, :], K("region"), ALU.subtract).then_inc(counts_ready, 1)
            dve.wait_ge(counts_ready, 1)
            tile_table(nc, dve, A, sb, table_v)


LP, RING = 3, 4


def experts(nc, A, dram):
    with ExitStack() as ctx:
        def sb(name, shape, dt=F32):
            return ctx.enter_context(nc.sbuf_tensor(name, shape, dt))

        def pb(name, shape, dt=F32):
            return ctx.enter_context(nc.psum_tensor(name, shape, dt))

        def sem(name):
            return ctx.enter_context(nc.semaphore(name))

        const = A["const"]

        def K(name):
            at, n = CONST[name]
            return const[:, at:at + n]

        ident = K("ident")
        expert_i, fresh_i, live_i, row_i, round_i = (A[n] for n in ("expert_i", "fresh_i", "live_i", "row_i", "round_i"))
        raw1, raw2, raw3 = A["raw_w1"], A["raw_w2"], A["raw_w3"]
        hi1, lo1 = sb("hi1", [P, DH, F], F32R), sb("lo1", [P, DH, F], F32R)
        hi3, lo3 = sb("hi3", [P, DH, F], F32R), sb("lo3", [P, DH, F], F32R)
        hi2, lo2 = sb("hi2", [P, FC, D], F32R), sb("lo2", [P, FC, D], F32R)
        xg = sb("xg", [P, UNROLL, MT // P, D])
        hx, lx = sb("hx", [P, UNROLL, DH, MT], F32R), sb("lx", [P, UNROLL, DH, MT], F32R)
        gate_s = sb("gate_s", [P, RING, MT])
        prod = sb("prod", [P, RING, MT])
        hh, lh = sb("hh", [P, RING, MT], F32R), sb("lh", [P, RING, MT], F32R)
        ys = sb("ysb", [P, UNROLL, MT // P, D])

        HB = [pb(f"HB{n}", [P, 2 * MT]) for n in range(RING)]
        XB = pb("XB", [P, DH * MT])
        YB = [pb(f"YB{n}", [P, MT // P, D]) for n in range(UNROLL)]

        x_in = [sem(f"xg_in{n}") for n in range(UNROLL)]
        y_out = [sem(f"y_out{n}") for n in range(UNROLL)]
        raw_in = A["raw_in"]
        x_psum, x_hi, x_lo = sem("x_psum"), sem("x_hi"), sem("x_lo")
        w_hi, w_lo = sem("w_hi"), sem("w_lo")
        h_psum, silu_done, gated, h_hi, h_lo = (sem("h_psum"), sem("silu_done"), sem("gated"), sem("h_hi"), sem("h_lo"))
        l2_done, y_read = sem("l2_done"), sem("y_read")
        passed = sem("epassed")

        block = ctx.enter_context(nc.Block())

        def tiles(eng, tile):
            for s in range(UNROLL):
                tile(s, 0, s)
            with eng.Fori(1, SURE) as r:
                for s in range(UNROLL):
                    tile(r * UNROLL + s, r, s)
            with eng.Fori(SURE, NTILES // UNROLL) as r:
                live = eng.value_load(live_i[0:1, bass.ds(r * UNROLL, 1)], min_val=0, max_val=1)
                with eng.If(live):
                    for s in range(UNROLL):
                        tile(r * UNROLL + s, r, s)
            r = eng.value_load(round_i[0:1, 0:1], min_val=SURE - 1, max_val=NTILES // UNROLL - 1)
            return r * UNROLL + UNROLL - 1, r

        def where_fresh(eng, j, work, otherwise):
            fresh = eng.value_load(fresh_i[0:1, bass.ds(j, 1)], min_val=0, max_val=1)
            with eng.If(fresh):
                work()
            with eng.Else():
                otherwise()

        def quarter(q):
            c, n = slice(HP * q, HP * (q + 1)), slice(HP // P * q, HP // P * (q + 1))
            return ((raw1[:, :, c], hi1[:, :, c], lo1[:, :, c]), (raw3[:, :, c], hi3[:, :, c], lo3[:, :, c]),
                    (raw2[:, n, :], hi2[:, n, :], lo2[:, n, :]))

        @block.sync
        def _(sp):
            def load_weights(j):
                for q in range(NQ):
                    sp.wait_ge(w_lo, NQ * (j - 1) + q + 1)
                    sp.sem_inc(passed, 1)

                    def load():
                        e = sp.value_load(expert_i[0:1, bass.ds(j, 1)], min_val=0, max_val=E - 1)
                        load_quarter(sp, A, dram, e, q)

                    where_fresh(sp, j, load, lambda: sp.sem_inc(raw_in[q], 48))

            def load_x(j, r, s):
                if not (isinstance(r, int) and r == 0):
                    sp.wait_ge(x_psum, j - UNROLL + 1)
                sp.sem_inc(passed, 1)
                at = sp.value_load(row_i[0:1, bass.ds(j, 1)], min_val=0, max_val=ROWS - MT)
                sp.dma_start(xg[:, s, :, :], dram["xs"][bass.ds(at, MT), :].rearrange("(m p) n -> p m n", p=P)
                             ).then_inc(x_in[s], 16)

            def store_y(j, r, s):
                sp.wait_ge(y_read, j + 1)
                sp.dma_start(dram["ys"][bass.ds(j * MT, MT), :].rearrange("(m p) n -> p m n", p=P), ys[:, s, :, :]
                             ).then_inc(y_out[s], 16)

            sp.wait_ge(A["scattered"], 16 * 2 * TT * B)
            load_x(0, 0, 0)
            load_x(1, 0, 1)

            def tile(j, r, s):
                ahead = (s + 2) % UNROLL
                load_x(j + 2, r if s == 0 else r + 1, ahead)
                load_weights(j + 1)
                if not (isinstance(j, int) and j == 0):
                    store_y(j - 1, r if s else r - 1, (s - 1) % UNROLL)

            j, r = tiles(sp, tile)
            store_y(j, r, UNROLL - 1)
            for s in range(UNROLL):
                sp.wait_ge(y_out[s], 16 * (r + 1))
            for s in range(2):
                sp.wait_ge(x_in[s], 16 * (r + 2))
            for q in range(NQ):
                sp.wait_ge(raw_in[q], 48 * (j + 3))
            sp.sem_inc(passed, 1)

        @block.tensor
        def _(pe):
            mm = nc.tensor.matmul

            def turn_x(j, r, s):
                pe.wait_ge(x_in[s], 16 * (r + 1))
                if not (isinstance(j, int) and j == 0):
                    pe.wait_ge(x_lo, j)
                for m in range(MT // P):
                    for a in range(DH):
                        last = nc.tensor.transpose(XB[:, a * MT + m * P:a * MT + (m + 1) * P],
                                                   xg[:, s, m, a * P:(a + 1) * P], ident)
                last.then_inc(x_psum, 1)

            def first(j, s, f):
                n, k, c = FC * j + f, f % RING, slice(f * P, (f + 1) * P)
                if f % 2 == 0:
                    pe.wait_ge(w_lo, NQ * j + f // 2 + 1)
                if f == 0:
                    pe.wait_ge(x_lo, j + 1)
                if not (isinstance(n, int) and n < RING):
                    pe.wait_ge(gated, n - RING + 1)
                for i, (hi, lo) in enumerate(((hi1, lo1), (hi3, lo3))):
                    out = HB[k][:, i * MT:(i + 1) * MT]
                    for a in range(DH):
                        for p, (w, x) in enumerate(((hi, hx), (hi, lx), (lo, hx))):
                            last = mm(out, w[:, a, c], x[:, s, a, :], start=(a == 0 and p == 0),
                                      stop=(a == DH - 1 and p == 2))
                last.then_inc(h_psum, 1)

            def second(j, s, f):
                n, k = FC * j + f, f % RING
                pe.wait_ge(h_lo, n + 1)
                for m in range(MT // P):
                    for p, (h, w) in enumerate(((hh, hi2), (hh, lo2), (lh, hi2))):
                        last = mm(YB[s][:, m, :], h[:, k, m * P:(m + 1) * P], w[:, f, :],
                                  start=(f == 0 and m == 0 and p == 0),
                                  stop=(f == FC - 1 and m == MT // P - 1 and p == 2))
                last.then_inc(l2_done, 1)

            turn_x(0, 0, 0)

            def tile(j, r, s):
                for f in range(FC):
                    first(j, s, f)
                    if f >= LP:
                        if f == LP and not (isinstance(r, int) and r == 0):
                            pe.wait_ge(y_read, j - UNROLL + 1)
                        second(j, s, f - LP)
                    elif not (isinstance(j, int) and j == 0):
                        second(j - 1, (s - 1) % UNROLL, FC - LP + f)
                    if f == 4:
                        nxt = (s + 1) % UNROLL
                        turn_x(j + 1, r if nxt else r + 1, nxt)

            j, _ = tiles(pe, tile)
            for f in range(FC - LP, FC):
                second(j, UNROLL - 1, f)

        SPLIT = {4: (0, 1), 6: (1, 1), 0: (2, 0), 2: (3, 0)}

        @block.scalar
        def _(act):
            nc.scalar.preload_act_table(ACT.Silu)

            def split(j, q):
                def high():
                    act.wait_ge(raw_in[q], 48 * (j + 2))
                    if not (isinstance(j, int) and j == 0):
                        act.wait_ge(l2_done, FC * (j - 1) + 2 * q + 2)
                    for raw, hi, _ in quarter(q):
                        last = nc.scalar.activation(hi, raw, ACT.Copy)
                    last.then_inc(w_hi, 1)

                def otherwise():
                    act.wait_ge(w_hi, NQ * j + q)
                    act.sem_inc(w_hi, 1)

                if isinstance(j, int) and j == 0:
                    high()
                else:
                    where_fresh(act, j, high, otherwise)

            def x_high(j, s):
                act.wait_ge(x_psum, j + 1)
                nc.scalar.activation(hx[:, s, :, :], XB[:, :].rearrange("p (a n) -> p a n", a=DH), ACT.Copy
                                     ).then_inc(x_hi, 1)

            def evacuate(j, r, s):
                act.wait_ge(l2_done, FC * (j + 1))
                if not (isinstance(r, int) and r == 0):
                    act.wait_ge(y_out[s], 16 * r)
                nc.scalar.activation(ys[:, s, :, :], YB[s][:, :, :], ACT.Copy).then_inc(y_read, 1)

            split(0, 0)
            split(0, 1)
            x_high(0, 0)

            def tile(j, r, s):
                for f in range(FC):
                    n, k = FC * j + f, f % RING
                    if f in SPLIT:
                        q, ahead = SPLIT[f]
                        split(j + ahead, q)
                    act.wait_ge(h_psum, n + 1)
                    if not (isinstance(n, int) and n < RING):
                        act.wait_ge(gated, n - RING + 1)
                    nc.scalar.activation(gate_s[:, k, :], HB[k][:, 0:MT], ACT.Silu).then_inc(silu_done, 1)
                    if f == LP and not (isinstance(j, int) and j == 0):
                        evacuate(j - 1, r if s else r - 1, (s - 1) % UNROLL)
                    if f == 4:
                        x_high(j + 1, (s + 1) % UNROLL)

            j, r = tiles(act, tile)
            evacuate(j, r, UNROLL - 1)

        @block.vector
        def _(dve):
            v = nc.vector

            def split(j, q):
                def low():
                    dve.wait_ge(w_hi, NQ * j + q + 1)
                    for raw, hi, lo in quarter(q):
                        last = v.tensor_tensor(lo, raw, hi.bitcast(F32), ALU.subtract)
                    last.then_inc(w_lo, 1)

                def otherwise():
                    dve.wait_ge(w_lo, NQ * j + q)
                    dve.sem_inc(w_lo, 1)

                if isinstance(j, int) and j == 0:
                    low()
                else:
                    where_fresh(dve, j, low, otherwise)

            def x_low(j, s):
                dve.wait_ge(x_hi, j + 1)
                v.tensor_tensor(lx[:, s, :, :], XB[:, :].rearrange("p (a n) -> p a n", a=DH),
                                hx[:, s, :, :].bitcast(F32), ALU.subtract).then_inc(x_lo, 1)

            split(0, 0)
            split(0, 1)
            x_low(0, 0)

            def tile(j, r, s):
                for f in range(FC):
                    n, k = FC * j + f, f % RING
                    if f in SPLIT:
                        q, ahead = SPLIT[f]
                        split(j + ahead, q)
                    dve.wait_ge(silu_done, n + 1)
                    if not (isinstance(n, int) and n < RING):
                        dve.wait_ge(l2_done, n - RING + 1)
                    v.tensor_tensor(prod[:, k, :], gate_s[:, k, :], HB[k][:, MT:2 * MT], ALU.mult).then_inc(gated, 1)
                    dve.wait_ge(gated, n + 1)
                    v.tensor_copy(hh[:, k, :], prod[:, k, :]).then_inc(h_hi, 1)
                    dve.wait_ge(h_hi, n + 1)
                    v.tensor_tensor(lh[:, k, :], prod[:, k, :], hh[:, k, :].bitcast(F32), ALU.subtract
                                    ).then_inc(h_lo, 1)
                    if f == 4:
                        x_low(j + 1, (s + 1) % UNROLL)

            tiles(dve, tile)


def combine(nc, A, dram):
    with ExitStack() as ctx:
        def sb(name, shape, dt=F32):
            return ctx.enter_context(nc.sbuf_tensor(name, shape, dt))

        def sem(name):
            return ctx.enter_context(nc.semaphore(name))

        slot_f, top2, eps_ln = A["slot_f"], A["top2"], A["eps_ln"]
        RB = 2
        NG = 2 * TT
        slots = sb("slots", [P, B * NG], U32)
        stage = sb("stage", [P, RB, NG], U32)
        diff = sb("diff", [P, B * TT])
        expd = sb("expd", [P, B * TT])
        den = sb("den", [P, B * TT])
        wt = sb("wt", [P, B * TT, 2])
        got = sb("got", [P, RB, NG, D])
        x1 = sb("x1s", [P, RB, TT, D])
        z = sb("z", [P, RB, TT, D])
        res = sb("res", [P, RB, TT, D])
        wts = sb("wts", [P, RB, NG])
        st = sb("cst", [P, RB, TT, 6])
        mv = sb("cmv", [P, RB, TT, 2])
        lnv = sb("clnv", [P, RB, TT])
        rr = sb("crr", [P, RB, TT])

        setup_v, exp_done = sem("csetup_v"), sem("cexp_done")
        staged = sem("staged")
        gathered = [sem(f"gathered{n}") for n in range(RB)]
        x1_in = [sem(f"x1_in{n}") for n in range(RB)]
        out_done = [sem(f"out_done{n}") for n in range(RB)]
        summed, var_ready, ln_done, rstd_ready, res_ready = (
            sem("csummed"), sem("cvar_ready"), sem("cln_done"), sem("crstd_ready"), sem("res_ready"))
        chain, passed = sem("cchain"), sem("cpassed")

        block = ctx.enter_context(nc.Block())

        def batches(eng, batch):
            for n in range(RB):
                batch(n, 0, n)
            with eng.Fori(1, B // RB) as r:
                for n in range(RB):
                    batch(r * RB + n, r, n)

        def rows(name, b):
            return dram[name][bass.ds(b * S, S), :].rearrange("(t p) n -> p t n", p=P)

        @block.sync
        def _(sp):
            def batch(b, r, n):
                if not (isinstance(r, int) and r == 0):
                    sp.wait_ge(res_ready, b - 1)
                sp.dma_start(x1[:, n, :, :], rows("x1", b)).then_inc(x1_in[n], 16)

            batches(sp, batch)

        @block.gpsimd
        def _(pool):
            def batch(b, r, n):
                if not (isinstance(r, int) and r == 0):
                    pool.wait_ge(gathered[n], 16 * NG * r)
                    pool.wait_ge(summed, b - 1)
                pool.sem_inc(passed, 1)
                nc.gpsimd.tensor_copy(stage[:, n, :], slots[:, bass.ds(b * NG, NG)]).then_inc(staged, 1)
                pool.wait_ge(staged, b + 1)
                pool.sem_inc(passed, 1)
                for c in range(NG):
                    nc.gpsimd.indirect_dma_start(
                        got[:, n, c, :], None, dram["ys"], bass.IndirectOffsetOnAxis(ap=stage[:, n, c:c + 1], axis=0)
                    ).then_inc(gathered[n], 16)

            pool.wait_ge(setup_v, 1)
            batches(pool, batch)

        @block.scalar
        def _(act):
            nc.scalar.preload_act_table_set("natural_log_exp_and_others")
            act.wait_ge(setup_v, 2)
            nc.scalar.activation(expd[:, :], diff[:, :], ACT.Exp).then_inc(exp_done, 1)

            def batch(b, r, n):
                act.wait_ge(var_ready, b + 1)
                nc.scalar.activation(lnv[:, n, :], mv[:, n, :, 1], ACT.Ln, bias=eps_ln[:, :]).then_inc(ln_done, 1)
                act.wait_ge(ln_done, b + 1)
                nc.scalar.activation(rr[:, n, :], lnv[:, n, :], ACT.Exp, scale=-0.5).then_inc(rstd_ready, 1)
                act.wait_ge(res_ready, b + 1)
                act.dma_start(rows("out", b), res[:, n, :, :]).then_inc(out_done[n], 16)

            batches(act, batch)
            for n in range(RB):
                act.wait_ge(out_done[n], 16 * (B // RB))

        @block.vector
        def _(dve):
            v = nc.vector
            steps = Steps(dve, setup_v, 0, 0)
            steps.per_batch = 99

            def did(ins):
                steps.did(ins)
                steps.settle()

            did(v.tensor_copy(slots[:, :], slot_f[:, :]))
            t2 = top2[:, :].rearrange("p (t k) -> p t k", k=2)
            did(v.tensor_tensor(diff[:, :], t2[:, :, 1], t2[:, :, 0], ALU.subtract))
            dve.wait_ge(exp_done, 1)
            did(v.tensor_scalar(den[:, :], expd[:, :], 1.0, None, ALU.add))
            did(v.reciprocal(wt[:, :, 0], den[:, :]))
            did(v.tensor_tensor(wt[:, :, 1], expd[:, :], wt[:, :, 0], ALU.mult))
            wflat = wt[:, :, :].rearrange("p t k -> p (t k)")

            def batch(b, r, n):
                s = Steps(dve, chain, 4, b)
                s.did(v.tensor_copy(wts[:, n, :], wflat[:, bass.ds(b * NG, NG)]))
                s.settle()
                dve.wait_ge(gathered[n], 16 * NG * (r + 1))
                for t in range(TT):
                    last = v.tensor_scalar(z[:, n, t, :], got[:, n, 2 * t, :], wts[:, n, 2 * t:2 * t + 1], None, ALU.mult)
                s.did(last)
                s.settle()
                for t in range(TT):
                    last = v.scalar_tensor_tensor(z[:, n, t, :], got[:, n, 2 * t + 1, :], wts[:, n, 2 * t + 1:2 * t + 2],
                                                  z[:, n, t, :], ALU.mult, ALU.add)
                last.then_inc(summed, 1)
                dve.wait_ge(summed, b + 1)
                dve.sem_inc(passed, 1)
                for t in range(TT):
                    last = v.bn_stats(st[:, n, t, :], z[:, n, t, :])
                s.did(last)
                s.settle()
                dve.sem_inc(passed, 1)
                for t in range(TT):
                    last = v.bn_aggr(mv[:, n, t, :], st[:, n, t, :])
                last.then_inc(var_ready, 1)
                dve.wait_ge(rstd_ready, b + 1)
                if not (isinstance(r, int) and r == 0):
                    dve.wait_ge(out_done[n], 16 * r)
                for t in range(TT):
                    last = v.tensor_scalar(res[:, n, t, :], z[:, n, t, :], mv[:, n, t, 0:1], rr[:, n, t:t + 1],
                                           ALU.subtract, ALU.mult)
                s.did(last)
                s.settle()
                dve.wait_ge(x1_in[n], 16 * (r + 1))
                v.tensor_tensor(res[:, n, :, :], res[:, n, :, :], x1[:, n, :, :], ALU.add).then_inc(res_ready, 1)

            batches(dve, batch)


def sandwich(nc, dram, out):
    for name, rows in (("x1", NTOK), ("xs", ROWS), ("ys", NTILES * MT)):
        dram[name] = nc.dram_tensor(name, [rows, D], F32, kind="Internal").ap()
    dram["out"] = out
    with ExitStack() as ctx:
        def sb(name, shape, dt=F32):
            return ctx.enter_context(nc.sbuf_tensor(name, shape, dt))

        A = {"const": sb("const", [P, NCONST]), "eps_ln": sb("eps_ln", [P, 1]), "eps_rms": sb("eps_rms", [P, 1]),
             "counts": sb("counts", [P, E]), "slot_f": sb("slot_f", [P, 2 * TT * B]), "top2": sb("top2", [P, 2 * TT * B]),
             "row_i": sb("row_i", [P, NT1], I32),
             "expert_i": sb("expert_i", [P, NT1], I32),
             "fresh_i": sb("fresh_i", [P, NT1], I32),
             "live_i": sb("live_i", [P, NT1], I32),
             "round_i": sb("round_i", [P, 1], I32),
             "table_ready": ctx.enter_context(nc.semaphore("table_ready")),
             "raw_w1": sb("raw_w1", [P, DH, F]), "raw_w3": sb("raw_w3", [P, DH, F]), "raw_w2": sb("raw_w2", [P, FC, D]),
             "raw_in": [ctx.enter_context(nc.semaphore(f"raw_in{q}")) for q in range(NQ)],
             "scattered": ctx.enter_context(nc.semaphore("scattered")),
             "const_in": ctx.enter_context(nc.semaphore("const_in")),
             "eps_set": ctx.enter_context(nc.semaphore("eps_set"))}
        attend(nc, A, dram)
        experts(nc, A, dram)
        combine(nc, A, dram)


def constants():
    c = np.zeros((P, NCONST), np.float32)

    def put(name, x):
        at, n = CONST[name]
        c[:, at:at + n] = x

    r = np.arange(P)
    put("ident", np.eye(P, dtype=np.float32))
    put("before", (r[:, None] < r[None, :]).astype(np.float32))
    put("ones", 1.0)
    put("mask0", np.where(r[None, :] >= r[:, None], 0.0, NEG))
    d = np.arange(P + WIN)[None, :] - r[:, None]
    put("mask1", np.where((d >= 0) & (d < WIN), 0.0, NEG))
    for l, turn in enumerate((1e6, 1e4)):
        inv = np.float32(1.0) / np.float32(turn) ** (np.arange(0, HD, 2, dtype=np.float32) / np.float32(HD))
        ang = np.arange(S, dtype=np.float32)[:, None] * inv[None, :].astype(np.float32)
        cos, sin = np.cos(ang), np.sin(ang)
        both = np.stack([cos, cos], -1), np.stack([-sin, sin], -1)
        for name, x in zip((f"cos{l}", f"sin{l}"), both):
            put(name, x.reshape(TT, P, HD).transpose(1, 0, 2).reshape(P, TT * HD))
    put("expert", np.arange(E)[None, :])
    put("region", np.arange(E)[None, :] * REG)
    put("tile", np.arange(NTILES + 2)[None, :])
    return c


_ATTN = ["norm1_w", "norm2_w", "g_wq", "g_kv_down", "g_k_up", "g_v_up", "g_wo", "l_wq", "l_wk", "l_wv", "l_wo"]


def kernel(**inputs):
    import numpy as _np
    import concourse.bacc as _bacc
    from concourse.bass_utils import run_bass_kernel_spmd as _run

    arrays = {"x": _np.asarray(inputs["L0_attn_hidden"]).reshape(NTOK, D), "const": constants()}
    for n in _ATTN:
        arrays[n] = _np.asarray(inputs["L0_attn_" + n])
    arrays["gate_w"] = _np.asarray(inputs["L0_ffn_gate_w"])
    for n in ("w1", "w3"):
        arrays[n] = _np.asarray(inputs["L0_ffn_" + n]).reshape(E * D, F)
    arrays["w2"] = _np.asarray(inputs["L0_ffn_w2"]).reshape(E * F, D)
    arrays = {n: _np.ascontiguousarray(a) for n, a in arrays.items()}
    nc = _bacc.Bacc("TRN2", target_bir_lowering=False, num_devices=1)
    dram = {n: nc.dram_tensor(f"in_{n}", a.shape, F32, kind="ExternalInput").ap() for n, a in arrays.items()}
    out = nc.dram_tensor("out_0", (NTOK, D), F32, kind="ExternalOutput").ap()
    sandwich(nc, dram, out)
    r = _run(nc, [{f"in_{n}": a for n, a in arrays.items()}], core_ids=[0])
    return r.results[0]["out_0"].reshape(B, S, D)
```

```python
from contextlib import ExitStack

import concourse.bass as bass
from concourse import mybir
import numpy as np

F32 = mybir.dt.float32
F32R = mybir.dt.float32r
BF16 = mybir.dt.bfloat16
U32 = mybir.dt.uint32
I32 = mybir.dt.int32
ALU = mybir.AluOpType
ACT = mybir.ActivationFunctionType
AX = mybir.AxisListType

P = 128
B, S, D = 8, 512, 256
H, KVH, HD, LAT = 16, 4, 16, 64
WIN = 64
E, F = 8, 1024
TT = S // P
DH = D // P
HPG = H // KVH
NQK = (H + KVH) * HD
NPROJ = NQK + KVH * HD
NTOK = B * S
MT = 256
REG = NTOK + MT
NTILES = 2 * NTOK // MT + E - 1
UNROLL = 3
SPARE = UNROLL + 1
ROWS = E * REG + SPARE * MT
XW = D + 2
DUMP = 2 * NTOK
EPS_LN, EPS_RMS = 1e-5, 1e-6
NEG = -1e30
SCALE = HD ** -0.5

CONST = {}
_at = 0
for _name, _n in (("ident", P), ("before", P), ("ones", P), ("mask0", P), ("mask1", P + WIN),
                  ("cos0", TT * HD), ("sin0", TT * HD), ("cos1", TT * HD), ("sin1", TT * HD),
                  ("expert", E), ("region", E), ("tile", NTILES + 2), ("place", TT), ("lane", MT // P), ("dump", MT // P)):
    CONST[_name] = (_at, _n)
    _at += _n
NCONST = _at

CHUNKS = [[(0, 0, 2, 1), (0, 2, 2, 1), (1, 0, 2, 1), (1, 2, 2, 1), (2, 0, 4, 2), (3, 0, 4, 4)],
          [(0, 0, 4, 2), (1, 0, 4, 2), (2, 0, 4, 2), (3, 0, 4, 4)]]


def width(l, kt):
    return S - kt * P if l == 0 else min(S - kt * P, P + WIN)


NCH = [KVH * len(c) for c in CHUNKS]
UNITS = KVH * TT


def chunks_of(l, u):
    g, kt = divmod(u, TT)
    return [(g * len(CHUNKS[l]) + n, c) for n, c in enumerate(CHUNKS[l]) if c[0] == kt]


def unit_of(l, n):
    g, c = divmod(n, len(CHUNKS[l]))
    return g * TT + CHUNKS[l][c][0]


def order(l, b):
    if l == 0:
        return 0 if isinstance(b, int) and b == 0 else 2 * b - 1
    return 2 * B - 1 if isinstance(b, int) and b == B - 1 else 2 * b + 2


def first_chunk(l, b):
    if l == 0:
        return 0 if isinstance(b, int) and b == 0 else (b - 1) * sum(NCH) + NCH[0]
    if isinstance(b, int) and b == B - 1:
        return NCH[0] + (B - 1) * sum(NCH)
    return b * sum(NCH) + 2 * NCH[0]


SURE = -(-2 * NTOK // MT // UNROLL)
NT1 = NTILES + 2
NQ, FC = 4, F // P
HP = F // NQ


def load_quarter(eng, A, dram, e, q):
    c, n = slice(HP * q, HP * (q + 1)), slice(HP // P * q, HP // P * (q + 1))
    for w in ("w1", "w3"):
        eng.dma_start(A["raw_" + w][:, :, c], dram[w][bass.ds(e * D, D), c].rearrange("(a p) n -> p a n", p=P)
                      ).then_inc(A["raw_in"][q], 16)
    eng.dma_start(A["raw_w2"][:, n, :], dram["w2"][bass.ds(e * F + HP * q, HP), :].rearrange("(a p) n -> p a n", p=P)
                  ).then_inc(A["raw_in"][q], 16)


class Steps:

    def __init__(self, eng, sem, per_batch, b):
        self.eng, self.sem, self.per_batch = eng, sem, per_batch
        self.base, self.n = b * per_batch, 0

    def did(self, ins):
        ins.then_inc(self.sem, 1)
        self.n += 1
        assert self.n <= self.per_batch
        return ins

    def settle(self):
        self.eng.wait_ge(self.sem, self.base + self.n)

    def end(self):
        assert self.n == self.per_batch, (self.n, self.per_batch)


def spread(ap, dims):
    return bass.AP(ap.tensor, ap.offset, [list(ap.ap[0])] + dims)


def tile_table(nc, dve, A, sb, done):
    v = nc.vector
    const, counts, own_f = A["const"], A["counts"], A["own_f"]
    expert_i, fresh_i, live_i, row_i, round_i = (A[n] for n in ("expert_i", "fresh_i", "live_i", "row_i", "round_i"))
    cnt_i = sb("cnt_i", [P, E], I32)
    nt_i = sb("nt_i", [P, E], I32)
    nt = sb("nt", [P, E])
    ends = sb("ends", [P, E])
    upto = sb("upto", [P, E, E])
    past = sb("past", [P, NT1, E])
    of_past = sb("of_past", [P, NT1, E])
    expert_f = sb("expert_f", [P, NT1])
    first_f = sb("first_f", [P, NT1])
    row_f = sb("row_f", [P, NT1])
    fresh_f = sb("fresh_f", [P, NT1])
    live_f = sb("live_f", [P, NT1])
    round_f = sb("round_f", [P, 1])
    steps = Steps(dve, done, 99, 0)

    def K(name):
        at, n = CONST[name]
        return const[:, at:at + n]

    def did(ins):
        steps.did(ins)
        steps.settle()

    did(v.tensor_scalar(cnt_i[:, :], counts[:, :], float(MT - 1), None, ALU.add))
    did(v.tensor_scalar(nt_i[:, :], cnt_i[:, :], MT.bit_length() - 1, None, ALU.arith_shift_right))
    did(v.tensor_copy(nt[:, :], nt_i[:, :]))
    no = K("expert")
    did(v.tensor_tensor(upto[:, :, :], spread(no[:, 0:1], [[1, E], [0, E]]), spread(no[:, 0:1], [[0, E], [1, E]]),
                        ALU.is_ge))
    did(v.tensor_tensor(upto[:, :, :], upto[:, :, :], spread(nt[:, 0:1], [[0, E], [1, E]]), ALU.mult))
    did(v.tensor_reduce(ends[:, :], upto[:, :, :], AX.X, ALU.add))
    tile_no = K("tile")
    did(v.tensor_tensor(past[:, :, :], spread(tile_no[:, 0:1], [[1, NT1], [0, E]]),
                        spread(ends[:, 0:1], [[0, NT1], [1, E]]), ALU.is_ge))
    did(v.tensor_tensor(of_past[:, :, :], past[:, :, :], spread(nt[:, 0:1], [[0, NT1], [1, E]]), ALU.mult))
    did(v.tensor_reduce(expert_f[:, :], past[:, :, :], AX.X, ALU.add))
    did(v.tensor_reduce(first_f[:, :], of_past[:, :, :], AX.X, ALU.add))
    did(v.tensor_tensor(row_f[:, :], tile_no[:, 0:NT1], first_f[:, :], ALU.subtract))
    did(v.tensor_scalar(row_f[:, :], row_f[:, :], float(MT), None, ALU.mult))
    did(v.scalar_tensor_tensor(row_f[:, :], expert_f[:, :], float(REG), row_f[:, :], ALU.mult, ALU.add))
    did(v.tensor_copy(row_i[:, :], row_f[:, :]))
    did(v.tensor_tensor(own_f[:, :, :], spread(row_f[:, 0:1], [[1, NT1], [0, MT // P]]),
                        spread(K("lane")[:, 0:1], [[0, NT1], [1, MT // P]]), ALU.add))
    did(v.tensor_scalar(live_f[:, :], expert_f[:, :], float(E), None, ALU.is_lt))
    did(v.tensor_copy(live_i[:, :], live_f[:, :]))
    at = SURE * UNROLL
    did(v.tensor_reduce(round_f[:, :], live_f[:, at:NTILES:UNROLL], AX.X, ALU.add))
    did(v.tensor_scalar(round_f[:, :], round_f[:, :], float(SURE - 1), None, ALU.add))
    did(v.tensor_copy(round_i[:, :], round_f[:, :]))
    did(v.tensor_scalar(expert_f[:, :], expert_f[:, :], float(E - 1), None, ALU.min))
    did(v.tensor_copy(expert_i[:, :], expert_f[:, :]))
    did(v.tensor_tensor(fresh_f[:, 1:NT1], expert_f[:, 1:NT1], expert_f[:, 0:NT1 - 1], ALU.not_equal))
    did(v.tensor_scalar(fresh_f[:, 0:1], expert_f[:, 0:1], 1.0, None, ALU.min))
    did(v.tensor_copy(fresh_i[:, :], fresh_f[:, :]))
    dve.sem_inc(A["table_ready"], 1)


def attend(nc, A, dram):
    with ExitStack() as ctx:
        def sb(name, shape, dt=F32):
            return ctx.enter_context(nc.sbuf_tensor(name, shape, dt))

        def pb(name, shape, dt=F32):
            return ctx.enter_context(nc.psum_tensor(name, shape, dt))

        def sem(name):
            return ctx.enter_context(nc.semaphore(name))

        const, eps_ln, eps_rms = A["const"], A["eps_ln"], A["eps_rms"]
        counts, top2 = A["counts"], A["top2"]

        def K(name, rows=P):
            at, n = CONST[name]
            return const[0:rows, at:at + n]

        ident = K("ident")
        ident_b = sb("ident_b", [P, P], BF16)
        before_b = sb("before_b", [P, P], BF16)
        ones_b = sb("ones_b", [P, P], BF16)
        zeros_b = sb("zeros_b", [P, P], BF16)
        mask_b = [sb(f"mask_b{l}", [P, CONST[f"mask{l}"][1]], BF16) for l in range(2)]
        W = [sb(f"W{l}", [P, DH, NPROJ]) for l in range(2)]
        WO = [sb(f"WO{l}", [P, KVH // 2, D]) for l in range(2)]
        gate = sb("gate", [P, DH, E])
        normw = sb("normw", [P, 2, DH])
        down = sb("down", [P, DH, LAT])
        up = sb("up", [LAT, 2 * KVH * HD])
        downT = sb("downT", [LAT, DH, P])

        Xin = sb("Xin", [P, TT, D])
        Hs = sb("Hs", [P, 4 * TT * D])
        xn = sb("xn", [P, TT, D])
        xT = sb("xT", [P, DH, S])
        R = sb("R", [P, TT, NQK])
        T2 = sb("T2", [P, 2, NQK])
        SQ = sb("SQ", [P, 2, NQK])
        SS = sb("SS", [P, TT, H + KVH])
        RL = sb("RL", [P, TT, H + KVH])
        RS = sb("RS", [P, TT, H + KVH])
        hi_q = sb("hi_q", [P, 2, S], F32R)
        lo_q = sb("lo_q", [P, 2, S], F32R)
        hi_k = sb("hi_k", [KVH * HD, S], F32R)
        lo_k = sb("lo_k", [KVH * HD, S], F32R)
        QS = [sb(f"QS{l}", [P, 2, HPG * S], F32R) for l in range(2)]
        KS = [sb(f"KS{l}", [P, KVH, S], F32R) for l in range(2)]
        VA = [sb(f"VA{l}", [P, TT, KVH, 2 * HD]) for l in range(2)]
        VA_own = [sb(f"VA_own{l}", [P, TT, KVH, 2 * HD]) for l in range(2)]
        probs = sb("probs", [P, 4, 1024])
        turned = sb("turned", [P, S])
        both = sb("both", [P, S])
        inv = sb("inv", [P, S // 32])
        OT = [sb(f"OT{l}", [P, KVH // 2, S]) for l in range(2)]
        st = sb("st", [P, TT, 6])
        mv = sb("mv", [P, TT, 2])
        vv = sb("vv", [P, TT])
        lnv = sb("lnv", [P, TT])
        rr = sb("rr", [P, TT])
        Xres = sb("Xres", [P, TT, D])
        Ff = sb("Ff", [P, TT, XW])
        FT = sb("FT", [P, DH, S])
        st2 = sb("st2", [P, TT, 6])
        mv2 = sb("mv2", [P, TT, 2])
        lnv2 = sb("lnv2", [P, TT])
        rr2 = sb("rr2", [P, TT])
        lg = sb("lg", [P, TT, E])
        mx = sb("mx", [P, TT, 8])
        ix = sb("ix", [P, TT, 8], U32)
        ixf = sb("ixf", [P, TT, 2])
        oh = sb("oh", [P, 2, TT, E])
        ohb = sb("ohb", [P, TT, E], BF16)
        pos = sb("pos", [P, TT, E])
        slot_u = sb("slot_u", [P, TT * 2], U32)
        pads = sb("pads", [P, MT // P, XW])
        diff, expd, den = (sb(n, [P, B * TT]) for n in ("diff", "expd", "den"))
        token2 = sb("token2", [P, TT])
        slot_f = sb("slot_f", [P, TT, 2])
        pad_i = sb("pad_i", [P, E], I32)
        base = sb("base", [P, E])

        SC = [pb(f"SC{n}", [P, 1024]) for n in range(2)]
        OP = pb("OP", [P, 512])
        PR = [pb(f"PR{n}", [P, 512]) for n in range(3)]

        q_stack = [nc.dram_tensor(f"q_stack{l}", [2, 2, HD, 2 * HPG, S], F32, kind="Internal").ap()
                   for l in range(2)]
        k_stack = [nc.dram_tensor(f"k_stack{l}", [KVH, 2, 2, HD, S], F32, kind="Internal").ap()
                   for l in range(2)]

        two = range(2)
        UNSTACK = (32, 32, 64)
        PARTS = (2, 0, 1)
        wts_in, wo_in = sem("wts_in"), sem("wo_in")
        pads_set, pads_filled, spare_filled = sem("pads_set"), sem("pads_filled"), sem("spare_filled")
        ups_in = sem("ups_in")
        nw_in = sem("nw_in")
        setup_v = sem("setup_v")
        setup_g = sem("setup_g")
        setup_pe = sem("setup_pe")
        x_in, x_used = sem("x_in"), sem("x_used")
        norm_v = [sem(f"norm_v{l}") for l in two]
        var_ready = [sem(f"var_ready{l}") for l in two]
        ln_done = [sem(f"ln_done{l}") for l in two]
        rstd_ready = [sem(f"rstd_ready{l}") for l in two]
        xn_ready = [sem(f"xn_ready{l}") for l in two]
        xt_psum = [sem(f"xt_psum{l}") for l in two]
        xt_act = [sem(f"xt_act{l}") for l in two]
        xt_dve = [sem(f"xt_dve{l}") for l in two]
        proj_done = [sem(f"proj_done{l}") for l in two]
        roped = [sem(f"roped{l}") for l in two]
        squared = [sem(f"squared{l}") for l in two]
        summed = [sem(f"summed{l}") for l in two]
        rot_ready = [sem(f"rot_ready{l}") for l in two]
        qk_ln = [sem(f"qk_ln{l}") for l in two]
        qk_rstd = [sem(f"qk_rstd{l}") for l in two]
        qk_ready = [sem(f"qk_ready{l}") for l in two]
        qkt_psum = [sem(f"qkt_psum{l}") for l in two]
        hi_done = [sem(f"hi_done{l}") for l in two]
        lo_done = [sem(f"lo_done{l}") for l in two]
        unstacked = [[sem(f"unstacked{l}_{n}") for n in range(3)] for l in two]
        k_stacked = [[sem(f"k_stacked{l}_{n}") for n in two] for l in two]
        q_stacked = [[sem(f"q_stacked{l}_{g}") for g in range(KVH)] for l in two]
        scored, exped = sem("scored"), sem("exped")
        pv_done = sem("pv_done")
        op_read, sums_inv, scaled, ot_done = sem("op_read"), sem("sums_inv"), sem("scaled"), sem("ot_done")
        wo_done = [sem(f"wo_done{l}") for l in two]
        resid = [sem(f"resid{l}") for l in two]
        xres_in = sem("xres_in")
        tail_v = sem("tail_v")
        var2_ready, ln2_done, rstd2_ready = sem("var2_ready"), sem("ln2_done"), sem("rstd2_ready")
        x1_ready, x1_out = sem("x1_ready"), sem("x1_out")
        f_ready, ft_psum, ft_act, ft_dve = sem("f_ready"), sem("ft_psum"), sem("ft_act"), sem("ft_dve")
        logits_done, picks_ready, pos_done = sem("logits_done"), sem("picks_ready"), sem("pos_done")
        slots_ready, scattered = sem("slots_ready"), A["scattered"]
        f_free = sem("f_free")
        weights_v, weights_exp = sem("weights_v"), sem("weights_exp")
        pads_ready, counts_ready, table_v = sem("pads_ready"), sem("counts_ready"), sem("table_v")
        passed_s, passed_p, passed_v, passed_g = (sem(f"passed_{e}") for e in "spvg")

        block = ctx.enter_context(nc.Block())

        def alone(eng, passed):
            eng.sem_inc(passed, 1)

        def program(eng, half, finish_only_wo):
            half(att=None, prep=(0, 0), wo=None, tail=None, prev=None)
            half(att=(0, 0), prep=(0, 1), wo=None, tail=None, prev=None)
            finish_only_wo(0, 0)
            half(att=(0, 1), prep=(1, 0), wo=None, tail=None, prev=0)
            half(att=(1, 0), prep=(0, 2), wo=(0, 1), tail=None, prev=0)
            with eng.Fori(2, B - 1) as i:
                half(att=(0, i), prep=(1, i - 1), wo=(1, i - 2), tail=None, prev=1)
                half(att=(1, i - 1), prep=(0, i + 1), wo=(0, i), tail=i - 2, prev=0)
            half(att=(0, B - 1), prep=(1, B - 2), wo=(1, B - 3), tail=None, prev=1)
            finish_only_wo(0, B - 1)
            half(att=(1, B - 2), prep=(1, B - 1), wo=None, tail=B - 3, prev=0)
            finish_only_wo(1, B - 2)
            half(att=(1, B - 1), prep=None, wo=None, tail=B - 2, prev=1)
            finish_only_wo(1, B - 1)
            half(att=None, prep=None, wo=None, tail=B - 1, prev=None)

        def va(l, b):
            own = isinstance(b, int) and b == (B - 1 if l else 0)
            return VA_own[l] if own else VA[l]

        def wait_unstacked(eng, l, b, n):
            if l == 1 and isinstance(b, int) and b == B - 1:
                eng.wait_ge(unstacked[1][n], UNSTACK[n] * b)
            elif l == 1:
                eng.wait_ge(unstacked[0][n], UNSTACK[n] * min(b + 2, B) if isinstance(b, int) else UNSTACK[n] * (b + 2))
            elif isinstance(b, int) and b <= 1:
                if b == 1:
                    eng.wait_ge(unstacked[0][n], UNSTACK[n])
            else:
                eng.wait_ge(unstacked[1][n], UNSTACK[n] * (b - 1))

        def hs(b, t0=0, n=TT):
            return Hs[:, bass.ds((b % 4) * (TT * D) + t0 * D, n * D)]

        PLACES = [dict(norms=(1, 2), turn=3, project=(4, 5, 6, 7), norm=8, parts=10, out=(12, 14)),
                  dict(norms=(0, 1), turn=3, project=(4, 5, 6, 7), norm=8, parts=10, out=(11, 14),
                       stats=(2, 3, 4, 6, 6), f_turn=(10, 11), logits=12, ranks=14)]

        def places(att):
            return PLACES[1 if att is None else att[0]]

        @block.sync
        def _(sp):
            def load_x(b):
                sp.dma_start(Xin[:, :, :], dram["x"][bass.ds(b * S, S), :].rearrange("(t p) n -> p t n", p=P)
                             ).then_inc(x_in, 16)

            load_x(0)
            sp.dma_start(const[:, :], dram["const"]).then_inc(A["const_in"], 16)
            for l, w in enumerate(("norm1_w", "norm2_w")):
                sp.dma_start(normw[:, l, :], dram[w].rearrange("(a p) -> p a", p=P),
                             allow_slow_non_contiguous=True).then_inc(nw_in, 16)
            sp.dma_start(down[:, :, :], dram["g_kv_down"].rearrange("(a p) n -> p a n", p=P)).then_inc(ups_in, 16)
            sp.dma_start(up[:, 0:KVH * HD], dram["g_k_up"]).then_inc(ups_in, 16)
            sp.dma_start(up[:, KVH * HD:], dram["g_v_up"]).then_inc(ups_in, 16)
            sp.dma_start(W[0][:, :, 0:D], dram["g_wq"].rearrange("(a p) n -> p a n", p=P)).then_inc(wts_in, 16)
            for w, at in (("l_wq", 0), ("l_wk", D), ("l_wv", NQK)):
                v = dram[w].rearrange("(a p) n -> p a n", p=P)
                sp.dma_start(W[1][:, :, at:at + v.shape[2]], v).then_inc(wts_in, 16)
            sp.dma_start(gate[:, :, :], dram["gate_w"].rearrange("(a p) n -> p a n", p=P)).then_inc(wts_in, 16)
            for l, w in enumerate(("g_wo", "l_wo")):
                v = dram[w].rearrange("(m two h d) n -> h two d m n", two=2, h=HPG, d=HD)
                for h in range(HPG):
                    for n in range(2):
                        row = 32 * h + HD * n
                        sp.dma_start(WO[l][row:row + HD, :, :], v[h, n]).then_inc(wo_in, 16)

            def half(att, prep, wo, tail, prev):
                if prep is not None:
                    l, b = prep
                    if l == 1 and not (isinstance(b, int) and b + 2 >= B):
                        sp.wait_ge(x_used, b + 2)
                        load_x(b + 2)
                    elif l == 0 and isinstance(b, int) and b < 2:
                        if b == 1:
                            sp.wait_ge(x_used, 1)
                            load_x(1)
                if tail is not None:
                    sp.wait_ge(x1_out, tail * 16 + 1)
                    sp.wait_ge(f_ready, tail + 1)
                    sp.dma_start(Xres[:, :, :], dram["x"][bass.ds(tail * S, S), :].rearrange("(t p) n -> p t n", p=P)
                                 ).then_inc(xres_in, 16)
                    sp.wait_ge(x1_ready, tail + 1)
                    sp.dma_start(dram["x1"][bass.ds(tail * S, S), :].rearrange("(t p) n -> p t n", p=P),
                                 Xres[:, :, :]).then_inc(x1_out, 16)
                if prep is not None:
                    l, b = prep
                    if not (isinstance(b, int) and b == 0):
                        for n in two:
                            sp.wait_ge(k_stacked[l][n], 16 * b)
                        for g in range(KVH):
                            sp.wait_ge(q_stacked[l][g], 16 * b)
                    for i, n in enumerate(PARTS):
                        for part, done, q, k in ((0, hi_done, hi_q, hi_k), (1, lo_done, lo_q, lo_k)):
                            sp.wait_ge(done[l], 3 * b + i + 1)
                            if n < 2:
                                sp.dma_start(q_stack[l][n, part].rearrange("d h s -> h d s"), q[:, n, :].bitcast(F32)
                                             ).then_inc(unstacked[l][n], 16)
                                continue
                            for twin in range(2):
                                sp.dma_start(k_stack[l][:, part, twin], k[:, :].bitcast(F32)
                                             ).then_inc(unstacked[l][n], 16)
                    if not (isinstance(b, int) and b == 0):
                        sp.wait_ge(exped, first_chunk(l, b - 1) + NCH[l])
                        alone(sp, passed_s)
                    sp.wait_ge(unstacked[l][2], UNSTACK[2] * (b + 1))
                    for n in two:
                        k = k_stack[l][n]
                        sp.dma_start(KS[l][64 * n:64 * (n + 1), n::2, :].bitcast(F32),
                                     bass.AP(k.tensor, k.offset, [[S, 4 * HD], [2 * 4 * HD * S, 2], [1, S]])
                                     ).then_inc(k_stacked[l][n], 16)
                    for g in range(KVH):
                        if g % 2 == 0:
                            sp.wait_ge(unstacked[l][g // 2], UNSTACK[g // 2] * (b + 1))
                        row = 64 * (g % 2)
                        q = q_stack[l][g // 2, 0, 0, HPG * (g % 2)]
                        sp.dma_start(QS[l][row:row + 64, g // 2, :].bitcast(F32),
                                     bass.AP(q.tensor, q.offset, [[0, 2], [2 * HPG * S, 2 * HD], [1, HPG * S]])
                                     ).then_inc(q_stacked[l][g], 16)

            sp.sem_inc(x1_out, 1)
            program(sp, half, lambda l, b: None)
            sp.wait_ge(pads_set, 3)
            for m in range(SPARE):
                at = E * REG + m * MT
                sp.dma_start(dram["xs"][at:at + MT, :].rearrange("(m p) n -> p m n", p=P), pads[:, :, :]
                             ).then_inc(spare_filled, 16)
            for q in range(NQ):
                load_quarter(sp, A, dram, 0, q)
            sp.wait_ge(pads_ready, 1)
            for e in range(E):
                at = sp.value_load(pad_i[0:1, e:e + 1], min_val=0, max_val=ROWS - MT)
                sp.dma_start(dram["xs"][bass.ds(at, MT), :].rearrange("(m p) n -> p m n", p=P), pads[:, :, :]
                             ).then_inc(pads_filled, 16)
            sp.wait_ge(x1_out, 16 * B + 1)
            sp.wait_ge(spare_filled, 16 * SPARE)
            sp.wait_ge(A["table_ready"], 1)
            for q in range(NQ):
                sp.wait_ge(A["raw_in"][q], 48)
                other = sp.value_load(A["fresh_i"][0:1, 0:1], min_val=0, max_val=1)
                with sp.If(other):
                    load_quarter(sp, A, dram, sp.value_load(A["expert_i"][0:1, 0:1], min_val=0, max_val=E - 1), q)
                with sp.Else():
                    sp.sem_inc(A["raw_in"][q], 48)
            sp.wait_ge(pads_filled, 16 * E)

        @block.gpsimd
        def _(pool):
            nc.gpsimd.memset(pads[:, :, 0:D], 0.0).then_inc(pads_set, 1)
            nc.gpsimd.memset(pads[:, :, D + 1], -1.0).then_inc(pads_set, 1)
            pool.wait_ge(A["const_in"], 16)
            nc.gpsimd.tensor_copy(pads[:, :, D], K("dump")).then_inc(pads_set, 1)
            for l in two:
                nc.gpsimd.memset(VA_own[l][:, :, :, :], 1.0).then_inc(setup_g, 1)
                nc.gpsimd.memset(VA[l][:, :, :, :], 1.0).then_inc(setup_g, 1)
                nc.gpsimd.memset(KS[l][:, :, :].bitcast(F32), 0.0).then_inc(setup_g, 1)

            def half(att, prep, wo, tail, prev):
                if prep is not None:
                    l, b = prep
                    for t in range(TT):
                        pool.wait_ge(roped[l], 4 * b + t + 1)
                        nc.gpsimd.tensor_tensor(R[:, t, :], R[:, t, :], T2[:, t % 2, :], ALU.add
                                                ).then_inc(rot_ready[l], 1)
                if tail is not None:
                    pool.wait_ge(slots_ready, tail + 1)
                    alone(pool, passed_g)
                    for t in range(TT):
                        for k in range(2):
                            c = 2 * t + k
                            nc.gpsimd.indirect_dma_start(
                                dram["xs"], bass.IndirectOffsetOnAxis(ap=slot_u[:, c:c + 1], axis=0),
                                Ff[:, t, :], None).then_inc(scattered, 16)
                    if not (isinstance(tail, int) and tail == B - 1):
                        pool.wait_ge(scattered, 16 * 2 * TT * (tail + 1))
                        pool.sem_inc(f_free, 1)

            pool.sem_inc(f_free, 1)
            program(pool, half, lambda l, b: None)

        @block.tensor
        def _(pe):
            mm, tr = nc.tensor.matmul, nc.tensor.transpose
            pe.wait_ge(A["const_in"], 16)
            pe.wait_ge(ups_in, 48)
            for a in range(DH):
                tr(PR[a][0:LAT, 0:P], down[:, a, :], ident).then_inc(setup_pe, 1)
            pe.wait_ge(setup_v, 1)
            for a in range(DH):
                mm(PR[2][:, P * a:P * (a + 1)], downT[:, a, :], up[:, :], start=True, stop=True
                   ).then_inc(setup_pe, 1)

            def score_unit(l, b, u, chunk0):
                g, kt = divmod(u, TT)
                w = width(l, kt)
                mw = CONST[f"mask{l}"][1] if l == 1 and w > P else P
                if kt == 0 and g % 2 == 0:
                    for n in two:
                        if g == 0:
                            pe.wait_ge(k_stacked[l][n], 16 * (b + 1))
                        pe.wait_ge(q_stacked[l][g + n], 16 * (b + 1))
                for n, (_, h0, nh, per) in chunks_of(l, u):
                    if not (isinstance(chunk0, int) and chunk0 + n < 2):
                        pe.wait_ge(exped, chunk0 + n - 1)
                    sc = SC[n % 2]
                    for j in range(0, nh, per):
                        out = spread(sc[:, 512 * (j // per):512 * (j // per) + 1], [[w, per], [1, w]])
                        q = QS[l][:, g // 2, (h0 + j) * S + kt * P:(h0 + j) * S + kt * P + 1]
                        mm(out, KS[l][:, g, kt * P:(kt + 1) * P], spread(q, [[S, per], [1, w]]),
                           start=True, stop=False)
                        out = spread(sc[:, 512 * (j // per):512 * (j // per) + 1], [[w, per], [1, mw]])
                        last = mm(out, ident_b[:, :], spread(mask_b[l][:, 0:1], [[0, per], [1, mw]]),
                                  start=False, stop=True)
                    last.then_inc(scored, 1)

            def pv_unit(l, b, a, u, chunk0):
                g, kt = divmod(u, TT)
                w = width(l, kt)
                mine = chunks_of(l, u)
                pe.wait_ge(exped, chunk0 + mine[-1][0] + 1)
                if kt == 0 and not (isinstance(a, int) and a == 0 and g == 0):
                    pe.wait_ge(op_read, 4 * a + g)
                if kt == 0 and l == 1:
                    mm(OP[:, :], zeros_b[:, :], spread(ones_b[:, 0:1], [[0, S]]), start=True, stop=False)
                for n, (_, h0, nh, per) in mine:
                    for j in range(nh):
                        h = h0 + j
                        at = 512 * (j // per) + w * (j % per)
                        last = mm(OP[32 * h:32 * h + 32, kt * P:kt * P + w], va(l, b)[:, kt, g, :],
                                  probs[:, n % 4, at:at + w], start=(kt == 0 and l == 0), stop=(kt == TT - 1),
                                  tile_position=(0, 32 * h))
                last.then_inc(pv_done, 1)

            def project_out(l, b, u):
                if (l, u) == (0, 0) and isinstance(b, int) and b == 0:
                    pe.wait_ge(wo_in, 16 * 4 * HPG)
                pe.wait_ge(ot_done, 2 * (order(l, b) + 1))
                if l == 0 and not (isinstance(b, int) and b < 2):
                    pe.wait_ge(resid[1], 2 * (b - 1))
                if l == 1:
                    pe.wait_ge(resid[0], 2 * min(b + 2, B) if isinstance(b, int) else 2 * (b + 2))
                for j in range(2):
                    for m in range(KVH // 2):
                        last = mm(PR[u][:, D * j:D * (j + 1)], OT[l][:, m, (2 * u + j) * P:(2 * u + j + 1) * P],
                                  WO[l][:, m, :], start=(m == 0), stop=(m == KVH // 2 - 1))
                last.then_inc(wo_done[l], 1)

            def half(att, prep, wo, tail, prev):
                at = places(att)
                for u in range(UNITS):
                    if att is not None:
                        la, ba = att
                        chunk0, a = first_chunk(la, ba), order(la, ba)
                        score_unit(la, ba, u, chunk0)
                        if u > 0:
                            pv_unit(la, ba, a, u - 1, chunk0)
                    if prep is not None:
                        l, b = prep
                        if u == at["turn"]:
                            pe.wait_ge(xn_ready[l], b + 1)
                            for f in range(DH):
                                for t in range(TT):
                                    last = tr(PR[f][:, t * P:(t + 1) * P], xn[:, t, f * P:(f + 1) * P], ident)
                                last.then_inc(xt_psum[l], 1)
                        if u in at["project"]:
                            t = at["project"].index(u)
                            if isinstance(b, int) and b == 0 and t == 0:
                                pe.wait_ge(setup_v, 2)
                            if t == 0:
                                pe.wait_ge(xt_act[l], b + 1)
                                pe.wait_ge(xt_dve[l], b + 1)
                            if t == 3:
                                pe.wait_ge(roped[l], 4 * b + 1)
                            bank = PR[(2, 0, 1, 2)[t]]
                            for f in range(DH):
                                last = mm(bank[:, 0:NPROJ], xT[:, f, t * P:(t + 1) * P], W[l][:, f, :],
                                          start=(f == 0), stop=(f == DH - 1))
                            last.then_inc(proj_done[l], 1)
                        if u == at["parts"]:
                            pe.wait_ge(qk_ready[l], 4 * (b + 1))
                            alone(pe, passed_p)
                            for n in PARTS:
                                m = P if n < 2 else KVH * HD
                                for t in range(TT):
                                    last = tr(PR[n][0:m, t * P:(t + 1) * P], R[:, t, n * P:n * P + m], ident)
                                last.then_inc(qkt_psum[l], 1)
                    if wo is not None and u in at["out"]:
                        n = at["out"].index(u)
                        if prep is not None:
                            pe.wait_ge(lo_done[prep[0]], 3 * prep[1] + n + 2)
                        project_out(*wo, n)
                    if tail is not None:
                        b = tail
                        if u in at["f_turn"]:
                            f = at["f_turn"].index(u)
                            if f == 0:
                                pe.wait_ge(f_ready, b + 2)
                                if prep is not None:
                                    pe.wait_ge(lo_done[prep[0]], 3 * prep[1] + 1)
                            else:
                                pe.wait_ge(ft_act, b + 1)
                            for t in range(TT):
                                last = tr(PR[2][:, t * P:(t + 1) * P], Ff[:, t, f * P:(f + 1) * P], ident)
                            last.then_inc(ft_psum, 1)
                        if u == at["logits"]:
                            pe.wait_ge(ft_dve, b + 1)
                            for t in range(TT):
                                for f in range(DH):
                                    last = mm(PR[2][:, t * E:(t + 1) * E], FT[:, f, t * P:(t + 1) * P],
                                              gate[:, f, :], start=(f == 0), stop=(f == DH - 1))
                            last.then_inc(logits_done, 1)
                        if u == at["ranks"]:
                            pe.wait_ge(picks_ready, b + 1)
                            for t in range(TT + 1):
                                out = PR[2][:, t * E:(t + 1) * E]
                                for s in range(min(t, TT)):
                                    last = mm(out, ones_b[:, :], ohb[:, s, :], start=(s == 0), stop=(t == TT and s == TT - 1))
                                if t < TT:
                                    last = mm(out, before_b[:, :], ohb[:, t, :], start=(t == 0), stop=True)
                            last.then_inc(pos_done, 1)
                if att is not None:
                    pv_unit(la, ba, a, UNITS - 1, chunk0)

            def finish(l, b):
                if b == 0:
                    pe.wait_ge(lo_done[0], 3 * 2)
                else:
                    pe.wait_ge(lo_done[1], 3 * (B - 1 if l == 0 else B))
                for n in range(2):
                    project_out(l, b, n)

            program(pe, half, finish)

        @block.scalar
        def _(act):
            act.wait_ge(A["eps_set"], 2)
            nc.scalar.preload_act_table_set("natural_log_exp_and_others")

            def exp_unit(l, b, a, u, chunk0, prev):
                for n, (kt, h0, nh, per) in chunks_of(l, u):
                    act.wait_ge(scored, chunk0 + n + 1)
                    if n >= 4:
                        act.wait_ge(pv_done, UNITS * a + unit_of(l, n - 4) + 1)
                    elif prev is not None:
                        act.wait_ge(pv_done, UNITS * (a - 1) + unit_of(prev, NCH[prev] + n - 4) + 1)
                    cols = per * width(l, kt)
                    nb = nh // per
                    nc.scalar.activation(spread(probs[:, n % 4, 0:1], [[512, nb], [1, cols]]),
                                         spread(SC[n % 2][:, 0:1], [[512, nb], [1, cols]]),
                                         ACT.Exp, scale=SCALE).then_inc(exped, 1)

            def rsqrt(out, tmp, in_, eps, scale, wait, waited, mid, midv, done):
                act.wait_ge(wait, waited)
                nc.scalar.activation(tmp, in_, ACT.Ln, bias=eps, scale=scale).then_inc(mid, 1)
                act.wait_ge(mid, midv)
                nc.scalar.activation(out, tmp, ACT.Exp, scale=-0.5).then_inc(done, 1)

            def half(att, prep, wo, tail, prev):
                at = places(att)
                for u in range(UNITS):
                    if att is not None:
                        la, ba = att
                        exp_unit(la, ba, order(la, ba), u, first_chunk(la, ba), prev)
                    if prep is not None:
                        l, b = prep
                        if l == 0 and u in at["norms"]:
                            n = at["norms"].index(u)
                            rsqrt(rr[:, :], lnv[:, :], vv[:, :], (eps_ln, eps_rms)[n][:, :], 1.0,
                                  var_ready[0], 2 * b + n + 1, ln_done[0], 2 * b + n + 1, rstd_ready[0])
                        if l == 1 and u == at["norms"][0]:
                            rsqrt(rr[:, :], lnv[:, :], vv[:, :], eps_rms[:, :], 1.0,
                                  var_ready[1], b + 1, ln_done[1], b + 1, rstd_ready[1])
                        if u == at["turn"]:
                            act.wait_ge(xt_psum[l], 2 * b + 1)
                            nc.scalar.activation(xT[:, 0, :], PR[0][:, :], ACT.Copy).then_inc(xt_act[l], 1)
                        if u in at["project"]:
                            t = at["project"].index(u)
                            if isinstance(b, int) and b == 0 and t == 0:
                                act.wait_ge(setup_g, 6)
                            act.wait_ge(proj_done[l], 4 * b + t + 1)
                            nc.scalar.activation(va(l, b)[:, t, :, 0:HD],
                                                 PR[(2, 0, 1, 2)[t]][:, NQK:NPROJ].rearrange("p (g d) -> p g d", g=KVH),
                                                 ACT.Copy)
                            if t >= 2:
                                act.wait_ge(summed[l], 4 * b + t - 1)
                            nc.scalar.activation(SQ[:, t % 2, :], PR[(2, 0, 1, 2)[t]][:, 0:NQK], ACT.Square
                                                 ).then_inc(squared[l], 1)
                        if u == at["norm"]:
                            rsqrt(RS[:, :, :], RL[:, :, :], SS[:, :, :], eps_rms[:, :], 1.0 / HD,
                                  summed[l], 4 * (b + 1), qk_ln[l], b + 1, qk_rstd[l])
                        if u == at["parts"]:
                            for i, n in enumerate(PARTS):
                                wait_unstacked(act, l, b, n)
                                act.wait_ge(qkt_psum[l], 3 * b + i + 1)
                                o = hi_q[:, n, :] if n < 2 else hi_k[:, :]
                                i = PR[n][:, :] if n < 2 else PR[n][0:KVH * HD, :]
                                nc.scalar.activation(o, i, ACT.Copy).then_inc(hi_done[l], 1)
                    if tail is not None:
                        if u in (at["stats"][1], at["stats"][3]):
                            n = int(u == at["stats"][3])
                            rsqrt(rr2[:, :], lnv2[:, :], mv2[:, :, 1], eps_ln[:, :], 1.0,
                                  var2_ready, 2 * tail + n + 1, ln2_done, 2 * tail + n + 1, rstd2_ready)
                        if u == at["f_turn"][0]:
                            act.wait_ge(ft_psum, 2 * tail + 1)
                            nc.scalar.activation(FT[:, 0, :], PR[2][:, :], ACT.Copy).then_inc(ft_act, 1)

            program(act, half, lambda l, b: None)
            act.wait_ge(weights_v, 1)
            nc.scalar.activation(expd[:, :], diff[:, :], ACT.Exp).then_inc(weights_exp, 1)

        @block.vector
        def _(dve):
            v = nc.vector
            v.memset(eps_ln[:, :], EPS_LN).then_inc(A["eps_set"], 1)
            v.memset(eps_rms[:, :], EPS_RMS).then_inc(A["eps_set"], 1)
            dve.wait_ge(A["const_in"], 16)
            for o, i in ((ident_b, "ident"), (before_b, "before"), (ones_b, "ones"), (mask_b[0], "mask0"), (mask_b[1], "mask1")):
                v.tensor_copy(o[:, :], K(i))
            v.memset(zeros_b[:, :], 0.0)
            v.tensor_copy(base[:, :], K("region"))
            v.tensor_copy(token2[:, :], K("place"))
            dve.wait_ge(setup_pe, DH)
            v.tensor_copy(downT[:, 0, :], PR[0][0:LAT, 0:P])
            v.tensor_copy(downT[:, 1, :], PR[1][0:LAT, 0:P]).then_inc(setup_v, 1)
            dve.wait_ge(nw_in, 32)
            dve.wait_ge(wts_in, 16 * 5)
            dve.wait_ge(setup_pe, 2 * DH)
            for a in range(DH):
                v.tensor_scalar(W[0][:, a, 0:D], W[0][:, a, 0:D], normw[:, 0, a:a + 1], None, ALU.mult)
                v.tensor_scalar(W[0][:, a, D:NPROJ], PR[2][:, P * a:P * (a + 1)], normw[:, 0, a:a + 1], None, ALU.mult)
            for a in range(DH):
                last = v.tensor_scalar(W[1][:, a, :], W[1][:, a, :], normw[:, 1, a:a + 1], None, ALU.mult)
            last.then_inc(setup_v, 1)

            NORM = [6, 4]

            def norm_stats(l, b, s):
                if l == 0:
                    dve.wait_ge(x_in, 16 * (b + 1))
                    src = Xin[:, :, :]
                else:
                    dve.wait_ge(resid[0], 2 * (b + 1))
                    src = hs(b).rearrange("p (t n) -> p t n", t=TT)
                alone(dve, passed_v)
                for t in range(TT):
                    last = v.bn_stats(st[:, t, :], src[:, t, :])
                s.did(last)
                s.settle()
                alone(dve, passed_v)
                for t in range(TT):
                    last = v.bn_aggr(mv[:, t, :], st[:, t, :])
                s.did(last)
                s.settle()
                if l == 0:
                    v.tensor_copy(vv[:, :], mv[:, :, 1]).then_inc(var_ready[0], 1)
                else:
                    s.did(v.tensor_tensor(vv[:, :], mv[:, :, 0], mv[:, :, 0], ALU.mult))
                    s.settle()
                    v.tensor_tensor(vv[:, :], vv[:, :], mv[:, :, 1], ALU.add).then_inc(var_ready[1], 1)

            def layer_norm_h(b, s):
                dve.wait_ge(rstd_ready[0], 2 * b + 1)
                s.did(v.tensor_tensor(vv[:, :], mv[:, :, 1], rr[:, :], ALU.mult))
                s.settle()
                s.did(v.tensor_tensor(vv[:, :], vv[:, :], rr[:, :], ALU.mult))
                for t in range(TT):
                    last = v.tensor_scalar(hs(b, t, 1), Xin[:, t, :], mv[:, t, 0:1], rr[:, t:t + 1],
                                           ALU.subtract, ALU.mult)
                s.did(last)
                s.settle()
                dve.sem_inc(x_used, 1)
                dve.sem_inc(var_ready[0], 1)

            def rms_x(l, b, s):
                dve.wait_ge(rstd_ready[l], 2 * b + 2 if l == 0 else b + 1)
                for t in range(TT):
                    last = v.tensor_scalar(xn[:, t, :], hs(b, t, 1), rr[:, t:t + 1], None, ALU.mult)
                s.did(last)
                s.settle()
                dve.sem_inc(xn_ready[l], 1)

            def rope(l, b, t):
                dve.wait_ge(squared[l], 4 * b + t + 1)
                if t >= 2:
                    dve.wait_ge(rot_ready[l], 4 * b + t - 1)
                qk = PR[(2, 0, 1, 2)[t]][:, 0:NQK]
                tab = [CONST[f"{n}{l}"][0] + t * HD for n in ("cos", "sin")]
                heads = [[HD, H + KVH], [2, HD // 2], [1, 2]]
                over = [[0, H + KVH], [2, HD // 2], [1, 2]]
                v.tensor_tensor(R[:, t, :].rearrange("p (h i two) -> p h i two", i=HD // 2, two=2),
                                spread(qk, heads), spread(const[:, tab[0]:tab[0] + 1], over), ALU.mult)
                swapped = spread(PR[(2, 0, 1, 2)[t]][:, 1:2], [[HD, H + KVH], [2, HD // 2], [-1, 2]])
                v.tensor_tensor(T2[:, t % 2, :].rearrange("p (h i two) -> p h i two", i=HD // 2, two=2),
                                swapped, spread(const[:, tab[1]:tab[1] + 1], over), ALU.mult
                                ).then_inc(roped[l], 1)
                v.tensor_reduce(SS[:, t, :], SQ[:, t % 2, :].rearrange("p (h d) -> p h d", d=HD), AX.X, ALU.add
                                ).then_inc(summed[l], 1)

            def qk_norm(l, b):
                dve.wait_ge(qk_rstd[l], b + 1)
                for t in range(TT):
                    dve.wait_ge(rot_ready[l], 4 * b + t + 1)
                    r = R[:, t, :].rearrange("p (h d) -> p h d", d=HD)
                    v.tensor_tensor(r, r, spread(RS[:, t, 0:1], [[1, H + KVH], [0, HD]]), ALU.mult
                                    ).then_inc(qk_ready[l], 1)

            def low_parts(l, b):
                for i, n in enumerate(PARTS):
                    wait_unstacked(dve, l, b, n)
                    dve.wait_ge(hi_done[l], 3 * b + i + 1)
                    o, h = (lo_q[:, n, :], hi_q[:, n, :]) if n < 2 else (lo_k[:, :], hi_k[:, :])
                    i = PR[n][:, :] if n < 2 else PR[n][0:KVH * HD, :]
                    v.tensor_tensor(o, i, h.bitcast(F32), ALU.subtract).then_inc(lo_done[l], 1)

            def normalise(l, a, g):
                first = isinstance(a, int) and 4 * a + g == 0
                if not first:
                    dve.wait_ge(scaled, 4 * a + g)
                dve.wait_ge(pv_done, UNITS * a + TT * (g + 1))
                v.transpose(turned[:, :], OP[:, :]).then_inc(op_read, 1)
                dve.wait_ge(op_read, 4 * a + g + 1)
                blocks = turned[:, :].rearrange("p (q i) -> p q i", i=32)
                filled = both[:, :].rearrange("p (q i) -> p q i", i=32)[:, :, HD * (g % 2):HD * (g % 2 + 1)]
                v.reciprocal(inv[:, :], blocks[:, :, HD]).then_inc(sums_inv, 1)
                dve.wait_ge(sums_inv, 4 * a + g + 1)
                if g % 2 == 0 and not first:
                    dve.wait_ge(ot_done, 2 * a + g // 2)
                v.tensor_tensor(filled, blocks[:, :, 0:HD], spread(inv[:, 0:1], [[1, S // 32], [0, HD]]),
                                ALU.mult).then_inc(scaled, 1)
                if g % 2:
                    dve.wait_ge(scaled, 4 * a + g + 1)
                    v.transpose(OT[l][:, g // 2, :], both[:, :]).then_inc(ot_done, 1)

            def residual(l, b, u):
                dve.wait_ge(wo_done[l], 2 * b + u + 1)
                h = hs(b, 2 * u, 2)
                v.tensor_tensor(h, h, PR[u][:, :], ALU.add).then_inc(resid[l], 1)

            TAIL = 15

            def stats2(b, src, s):
                alone(dve, passed_v)
                for t in range(TT):
                    last = v.bn_stats(st2[:, t, :], src[:, t, :])
                s.did(last)
                s.settle()
                alone(dve, passed_v)
                for t in range(TT):
                    last = v.bn_aggr(mv2[:, t, :], st2[:, t, :])
                last.then_inc(var2_ready, 1)

            def tail_1(b, s):
                dve.wait_ge(resid[1], 2 * (b + 1))
                stats2(b, hs(b).rearrange("p (t n) -> p t n", t=TT), s)

            def tail_2(b, s):
                dve.wait_ge(rstd2_ready, 2 * b + 1)
                dve.wait_ge(xres_in, 16 * (b + 1))
                dve.wait_ge(f_free, b + 1)
                for t in range(TT):
                    last = v.tensor_scalar(Ff[:, t, 0:D], hs(b, t, 1), mv2[:, t, 0:1], rr2[:, t:t + 1],
                                           ALU.subtract, ALU.mult)
                s.did(last)
                s.settle()
                s.did(v.tensor_tensor(Xres[:, :, :], Xres[:, :, :], Ff[:, :, 0:D], ALU.add))
                s.settle()
                dve.sem_inc(x1_ready, 1)
                stats2(b, Xres[:, :, :], s)

            def tail_3(b, s):
                dve.wait_ge(rstd2_ready, 2 * b + 2)
                for t in range(TT):
                    last = v.tensor_scalar(Ff[:, t, 0:D], Xres[:, t, :], mv2[:, t, 0:1], rr2[:, t:t + 1],
                                           ALU.subtract, ALU.mult)
                last.then_inc(f_ready, 1)

            def tail_4(b, s):
                dve.wait_ge(ft_psum, 2 * b + 2)
                v.tensor_copy(FT[:, 1, :], PR[2][:, :]).then_inc(ft_dve, 1)

            def tail_5(b, s):
                dve.wait_ge(logits_done, b + 1)
                s.did(v.tensor_copy(lg[:, :, :], PR[2][:, 0:TT * E].rearrange("p (t e) -> p t e", t=TT)))
                s.settle()
                alone(dve, passed_v)
                for t in range(TT):
                    last = v.max(mx[:, t, :], lg[:, t, :])
                s.did(last)
                s.settle()
                alone(dve, passed_v)
                for t in range(TT):
                    last = v.max_index(ix[:, t, :], mx[:, t, :], lg[:, t, :])
                s.did(last)
                s.settle()
                alone(dve, passed_v)
                v.tensor_copy(top2[:, bass.ds(b * (2 * TT), 2 * TT)].rearrange("p (t k) -> p t k", k=2), mx[:, :, 0:2])
                s.did(v.tensor_copy(ixf[:, :, :], ix[:, :, 0:2]))
                s.settle()
                for k in range(2):
                    last = v.tensor_tensor(oh[:, k, :, :], spread(K("expert"), [[0, TT], [1, E]]),
                                           spread(ixf[:, 0, k:k + 1], [[2, TT], [0, E]]), ALU.is_equal)
                s.did(last)
                s.settle()
                v.tensor_tensor(ohb[:, :, :], oh[:, 0, :, :], oh[:, 1, :, :], ALU.add).then_inc(picks_ready, 1)

            def tail_6(b, s):
                dve.wait_ge(pos_done, b + 1)
                s.did(v.tensor_tensor(pos[:, :, :], PR[2][:, 0:TT * E].rearrange("p (t e) -> p t e", t=TT),
                                      spread(base[:, 0:1], [[0, TT], [1, E]]), ALU.add))
                s.settle()
                s.did(v.tensor_tensor(base[:, :], base[:, :], PR[2][:, TT * E:(TT + 1) * E], ALU.add))
                for k in range(2):
                    last = v.tensor_tensor(oh[:, k, :, :], oh[:, k, :, :], pos[:, :, :], ALU.mult)
                s.did(last)
                s.settle()
                for k in range(2):
                    last = v.tensor_reduce(slot_f[:, :, k], oh[:, k, :, :], AX.X, ALU.add)
                s.did(last)
                s.settle()
                v.tensor_copy(Ff[:, :, D], token2[:, :])
                s.did(v.tensor_copy(Ff[:, :, D + 1], slot_f[:, :, 1]))
                s.settle()
                s.did(v.tensor_scalar(token2[:, :], token2[:, :], float(2 * S), None, ALU.add))
                v.tensor_copy(slot_u[:, :], slot_f[:, :, :].rearrange("p t k -> p (t k)")).then_inc(slots_ready, 1)

            def half(att, prep, wo, tail, prev):
                at = places(att)
                if att is not None:
                    la, a = att[0], order(*att)
                if prep is not None:
                    l, b = prep
                    s = Steps(dve, norm_v[l], NORM[l], b)
                    norm_stats(l, b, s)
                if tail is not None:
                    ts = Steps(dve, tail_v, TAIL, tail)
                for u in range(UNITS):
                    if att is not None and u % TT == 0 and u > 0:
                        normalise(la, a, u // TT - 1)
                    if prep is not None:
                        if l == 0 and u == at["norms"][0]:
                            layer_norm_h(b, s)
                        if u == at["norms"][1 - l]:
                            rms_x(l, b, s)
                            s.end()
                        if u == at["turn"]:
                            dve.wait_ge(xt_psum[l], 2 * b + 2)
                            v.tensor_copy(xT[:, 1, :], PR[1][:, :]).then_inc(xt_dve[l], 1)
                        if u in at["project"]:
                            rope(l, b, at["project"].index(u))
                        if u == at["norm"]:
                            qk_norm(l, b)
                        if u == at["parts"]:
                            low_parts(l, b)
                    if tail is not None:
                        if u == at["stats"][0]:
                            tail_1(tail, ts)
                        if u == at["stats"][2]:
                            tail_2(tail, ts)
                        if u == at["stats"][4]:
                            tail_3(tail, ts)
                        if u == at["f_turn"][1]:
                            tail_4(tail, ts)
                        if u == at["logits"]:
                            tail_5(tail, ts)
                    if wo is not None and u in at["out"]:
                        residual(*wo, at["out"].index(u))
                    if tail is not None and u == at["ranks"]:
                        tail_6(tail, ts)
                        ts.end()
                if att is not None:
                    normalise(la, a, KVH - 1)

            def finish(l, b):
                for u in range(2):
                    residual(l, b, u)

            dve.sem_inc(f_ready, 1)
            program(dve, half, finish)
            v.tensor_copy(pad_i[:, :], base[:, :]).then_inc(pads_ready, 1)
            v.tensor_tensor(counts[:, :], base[:, :], K("region"), ALU.subtract).then_inc(counts_ready, 1)
            dve.wait_ge(counts_ready, 1)
            tile_table(nc, dve, A, sb, table_v)
            s = Steps(dve, weights_v, 3, 0)
            wt, t2 = A["wt"], top2[:, :].rearrange("p (t k) -> p t k", k=2)
            s.did(v.tensor_tensor(diff[:, :], t2[:, :, 1], t2[:, :, 0], ALU.subtract))
            dve.wait_ge(weights_exp, 1)
            s.did(v.tensor_scalar(den[:, :], expd[:, :], 1.0, None, ALU.add))
            s.settle()
            s.did(v.reciprocal(wt[:, :, 0], den[:, :]))
            s.settle()
            v.tensor_tensor(wt[:, :, 1], expd[:, :], wt[:, :, 0], ALU.mult)


LP, RING = 3, 4


def experts(nc, A, dram):
    with ExitStack() as ctx:
        def sb(name, shape, dt=F32):
            return ctx.enter_context(nc.sbuf_tensor(name, shape, dt))

        def pb(name, shape, dt=F32):
            return ctx.enter_context(nc.psum_tensor(name, shape, dt))

        def sem(name):
            return ctx.enter_context(nc.semaphore(name))

        const = A["const"]

        def K(name):
            at, n = CONST[name]
            return const[:, at:at + n]

        ident = K("ident")
        expert_i, fresh_i, live_i, row_i, round_i, own_f = (
            A[n] for n in ("expert_i", "fresh_i", "live_i", "row_i", "round_i", "own_f"))
        raw1, raw2, raw3 = A["raw_w1"], A["raw_w2"], A["raw_w3"]
        hi1, lo1 = sb("hi1", [P, DH, F], F32R), sb("lo1", [P, DH, F], F32R)
        hi3, lo3 = sb("hi3", [P, DH, F], F32R), sb("lo3", [P, DH, F], F32R)
        hi2, lo2 = sb("hi2", [P, FC, D], F32R), sb("lo2", [P, FC, D], F32R)
        xg = sb("xg", [P, UNROLL, MT // P, XW])
        second_f = sb("second_f", [P, MT // P])
        dest_f = sb("dest_f", [P, MT // P])
        dest_u = sb("dest_u", [P, UNROLL, MT // P], U32)
        hx, lx = sb("hx", [P, UNROLL, DH, MT], F32R), sb("lx", [P, UNROLL, DH, MT], F32R)
        gate_s = sb("gate_s", [P, RING, MT])
        prod = sb("prod", [P, RING, MT])
        hh, lh = sb("hh", [P, RING, MT], F32R), sb("lh", [P, RING, MT], F32R)
        ys = sb("ysb", [P, UNROLL, MT // P, D])

        HB = [pb(f"HB{n}", [P, 2 * MT]) for n in range(RING)]
        XB = pb("XB", [P, DH * MT])
        YB = [pb(f"YB{n}", [P, MT // P, D]) for n in range(UNROLL)]

        x_in = [sem(f"xg_in{n}") for n in range(UNROLL)]
        y_out = [sem(f"y_out{n}") for n in range(UNROLL)]
        raw_in = A["raw_in"]
        x_psum, x_hi, x_lo = sem("x_psum"), sem("x_hi"), sem("x_lo")
        w_hi, w_lo = sem("w_hi"), sem("w_lo")
        h_psum, silu_done, gated, h_hi, h_lo = (sem("h_psum"), sem("silu_done"), sem("gated"), sem("h_hi"), sem("h_lo"))
        dest_v, dest_ready, x1_in = sem("dest_v"), sem("dest_ready"), A["x1_in"]
        l2_done, y_read = sem("l2_done"), sem("y_read")
        STORE = 16 * MT // P
        passed_g, passed = sem("epassed_g"), sem("epassed")

        block = ctx.enter_context(nc.Block())

        def tiles(eng, tile):
            for s in range(UNROLL):
                tile(s, 0, s)
            with eng.Fori(1, SURE) as r:
                for s in range(UNROLL):
                    tile(r * UNROLL + s, r, s)
            with eng.Fori(SURE, NTILES // UNROLL) as r:
                live = eng.value_load(live_i[0:1, bass.ds(r * UNROLL, 1)], min_val=0, max_val=1)
                with eng.If(live):
                    for s in range(UNROLL):
                        tile(r * UNROLL + s, r, s)
            r = eng.value_load(round_i[0:1, 0:1], min_val=SURE - 1, max_val=NTILES // UNROLL - 1)
            return r * UNROLL + UNROLL - 1, r

        def where_fresh(eng, j, work, otherwise):
            fresh = eng.value_load(fresh_i[0:1, bass.ds(j, 1)], min_val=0, max_val=1)
            with eng.If(fresh):
                work()
            with eng.Else():
                otherwise()

        def quarter(q):
            c, n = slice(HP * q, HP * (q + 1)), slice(HP // P * q, HP // P * (q + 1))
            return ((raw1[:, :, c], hi1[:, :, c], lo1[:, :, c]), (raw3[:, :, c], hi3[:, :, c], lo3[:, :, c]),
                    (raw2[:, n, :], hi2[:, n, :], lo2[:, n, :]))

        @block.sync
        def _(sp):
            def load_weights(j):
                for q in range(NQ):
                    sp.wait_ge(w_lo, NQ * (j - 1) + q + 1)
                    sp.sem_inc(passed, 1)

                    def load():
                        e = sp.value_load(expert_i[0:1, bass.ds(j, 1)], min_val=0, max_val=E - 1)
                        load_quarter(sp, A, dram, e, q)

                    where_fresh(sp, j, load, lambda: sp.sem_inc(raw_in[q], 48))

            def load_x(j, r, s):
                if not (isinstance(r, int) and r == 0):
                    sp.wait_ge(x_psum, j - UNROLL + 1)
                    sp.wait_ge(dest_ready, j - UNROLL + 1)
                sp.sem_inc(passed, 1)
                at = sp.value_load(row_i[0:1, bass.ds(j, 1)], min_val=0, max_val=ROWS - MT)
                sp.dma_start(xg[:, s, :, :], dram["xs"][bass.ds(at, MT), :].rearrange("(m p) n -> p m n", p=P)
                             ).then_inc(x_in[s], 16)

            sp.wait_ge(A["scattered"], 16 * 2 * TT * B)
            load_x(0, 0, 0)
            load_x(1, 0, 1)
            sp.dma_start(A["x1"][:, :, :], dram["x1"].rearrange("(t p) n -> p t n", p=P)).then_inc(x1_in, 16)

            def tile(j, r, s):
                ahead = (s + 2) % UNROLL
                load_x(j + 2, r if s == 0 else r + 1, ahead)
                load_weights(j + 1)

            j, r = tiles(sp, tile)
            for s in range(2):
                sp.wait_ge(x_in[s], 16 * (r + 2))
            for q in range(NQ):
                sp.wait_ge(raw_in[q], 48 * (j + 3))
            sp.sem_inc(passed, 1)

        @block.gpsimd
        def _(pool):
            def tile(j, r, s):
                pool.wait_ge(dest_ready, j + 1)
                pool.wait_ge(y_read, j + 1)
                if not (isinstance(j, int) and j == 0):
                    pool.wait_ge(y_out[(s - 1) % UNROLL], STORE * (r + 1 if s else r))
                pool.sem_inc(passed_g, 1)
                for m in range(MT // P):
                    nc.gpsimd.indirect_dma_start(
                        dram["ys"], bass.IndirectOffsetOnAxis(ap=dest_u[:, s, m:m + 1], axis=0), ys[:, s, m, :], None
                    ).then_inc(y_out[s], 16)

            _, r = tiles(pool, tile)
            for s in range(UNROLL):
                pool.wait_ge(y_out[s], STORE * (r + 1))
            pool.sem_inc(passed_g, 1)

        @block.tensor
        def _(pe):
            mm = nc.tensor.matmul

            def turn_x(j, r, s):
                pe.wait_ge(x_in[s], 16 * (r + 1))
                if not (isinstance(j, int) and j == 0):
                    pe.wait_ge(x_lo, j)
                for m in range(MT // P):
                    for a in range(DH):
                        last = nc.tensor.transpose(XB[:, a * MT + m * P:a * MT + (m + 1) * P],
                                                   xg[:, s, m, a * P:(a + 1) * P], ident)
                last.then_inc(x_psum, 1)

            def first(j, s, f):
                n, k, c = FC * j + f, f % RING, slice(f * P, (f + 1) * P)
                if f % 2 == 0:
                    pe.wait_ge(w_lo, NQ * j + f // 2 + 1)
                if f == 0:
                    pe.wait_ge(x_lo, j + 1)
                if not (isinstance(n, int) and n < RING):
                    pe.wait_ge(gated, n - RING + 1)
                for i, (hi, lo) in enumerate(((hi1, lo1), (hi3, lo3))):
                    out = HB[k][:, i * MT:(i + 1) * MT]
                    for a in range(DH):
                        for p, (w, x) in enumerate(((hi, hx), (hi, lx), (lo, hx))):
                            last = mm(out, w[:, a, c], x[:, s, a, :], start=(a == 0 and p == 0),
                                      stop=(a == DH - 1 and p == 2))
                last.then_inc(h_psum, 1)

            def second(j, s, f):
                n, k = FC * j + f, f % RING
                pe.wait_ge(h_lo, n + 1)
                for m in range(MT // P):
                    for p, (h, w) in enumerate(((hh, hi2), (hh, lo2), (lh, hi2))):
                        last = mm(YB[s][:, m, :], h[:, k, m * P:(m + 1) * P], w[:, f, :],
                                  start=(f == 0 and m == 0 and p == 0),
                                  stop=(f == FC - 1 and m == MT // P - 1 and p == 2))
                last.then_inc(l2_done, 1)

            turn_x(0, 0, 0)

            def tile(j, r, s):
                for f in range(FC):
                    first(j, s, f)
                    if f >= LP:
                        if f == LP and not (isinstance(r, int) and r == 0):
                            pe.wait_ge(y_read, j - UNROLL + 1)
                        second(j, s, f - LP)
                    elif not (isinstance(j, int) and j == 0):
                        second(j - 1, (s - 1) % UNROLL, FC - LP + f)
                    if f == 4:
                        nxt = (s + 1) % UNROLL
                        turn_x(j + 1, r if nxt else r + 1, nxt)

            j, _ = tiles(pe, tile)
            for f in range(FC - LP, FC):
                second(j, UNROLL - 1, f)

        SPLIT = {4: (0, 1), 6: (1, 1), 0: (2, 0), 2: (3, 0)}

        @block.scalar
        def _(act):
            nc.scalar.preload_act_table(ACT.Silu)

            def split(j, q):
                def high():
                    act.wait_ge(raw_in[q], 48 * (j + 2))
                    if not (isinstance(j, int) and j == 0):
                        act.wait_ge(l2_done, FC * (j - 1) + 2 * q + 2)
                    for raw, hi, _ in quarter(q):
                        last = nc.scalar.activation(hi, raw, ACT.Copy)
                    last.then_inc(w_hi, 1)

                def otherwise():
                    act.wait_ge(w_hi, NQ * j + q)
                    act.sem_inc(w_hi, 1)

                if isinstance(j, int) and j == 0:
                    high()
                else:
                    where_fresh(act, j, high, otherwise)

            def x_high(j, s):
                act.wait_ge(x_psum, j + 1)
                nc.scalar.activation(hx[:, s, :, :], XB[:, :].rearrange("p (a n) -> p a n", a=DH), ACT.Copy
                                     ).then_inc(x_hi, 1)

            def evacuate(j, r, s):
                act.wait_ge(l2_done, FC * (j + 1))
                if not (isinstance(r, int) and r == 0):
                    act.wait_ge(y_out[s], STORE * r)
                nc.scalar.activation(ys[:, s, :, :], YB[s][:, :, :], ACT.Copy).then_inc(y_read, 1)

            split(0, 0)
            split(0, 1)
            x_high(0, 0)

            def tile(j, r, s):
                for f in range(FC):
                    n, k = FC * j + f, f % RING
                    if f in SPLIT:
                        q, ahead = SPLIT[f]
                        split(j + ahead, q)
                    act.wait_ge(h_psum, n + 1)
                    if not (isinstance(n, int) and n < RING):
                        act.wait_ge(gated, n - RING + 1)
                    nc.scalar.activation(gate_s[:, k, :], HB[k][:, 0:MT], ACT.Silu).then_inc(silu_done, 1)
                    if f == LP and not (isinstance(j, int) and j == 0):
                        evacuate(j - 1, r if s else r - 1, (s - 1) % UNROLL)
                    if f == 4:
                        x_high(j + 1, (s + 1) % UNROLL)

            j, r = tiles(act, tile)
            evacuate(j, r, UNROLL - 1)

        @block.vector
        def _(dve):
            v = nc.vector

            def split(j, q):
                def low():
                    dve.wait_ge(w_hi, NQ * j + q + 1)
                    for raw, hi, lo in quarter(q):
                        last = v.tensor_tensor(lo, raw, hi.bitcast(F32), ALU.subtract)
                    last.then_inc(w_lo, 1)

                def otherwise():
                    dve.wait_ge(w_lo, NQ * j + q)
                    dve.sem_inc(w_lo, 1)

                if isinstance(j, int) and j == 0:
                    low()
                else:
                    where_fresh(dve, j, low, otherwise)

            def x_low(j, s):
                dve.wait_ge(x_hi, j + 1)
                v.tensor_tensor(lx[:, s, :, :], XB[:, :].rearrange("p (a n) -> p a n", a=DH),
                                hx[:, s, :, :].bitcast(F32), ALU.subtract).then_inc(x_lo, 1)

            def places(j, r, s):
                dve.wait_ge(x_in[s], 16 * (r + 1))
                if not (isinstance(r, int) and r == 0):
                    dve.wait_ge(y_out[s], STORE * r)
                steps = Steps(dve, dest_v, 2, j)
                own = own_f[:, bass.ds(j, 1), :].rearrange("p one m -> p (one m)")
                steps.did(v.tensor_tensor(second_f[:, :], own, xg[:, s, :, D + 1], ALU.is_equal))
                steps.settle()
                steps.did(v.tensor_tensor(dest_f[:, :], second_f[:, :], xg[:, s, :, D], ALU.add))
                steps.settle()
                v.tensor_copy(dest_u[:, s, :], dest_f[:, :]).then_inc(dest_ready, 1)

            split(0, 0)
            split(0, 1)
            x_low(0, 0)
            places(0, 0, 0)

            def tile(j, r, s):
                for f in range(FC):
                    n, k = FC * j + f, f % RING
                    if f in SPLIT:
                        q, ahead = SPLIT[f]
                        split(j + ahead, q)
                    dve.wait_ge(silu_done, n + 1)
                    if not (isinstance(n, int) and n < RING):
                        dve.wait_ge(l2_done, n - RING + 1)
                    v.tensor_tensor(prod[:, k, :], gate_s[:, k, :], HB[k][:, MT:2 * MT], ALU.mult).then_inc(gated, 1)
                    dve.wait_ge(gated, n + 1)
                    v.tensor_copy(hh[:, k, :], prod[:, k, :]).then_inc(h_hi, 1)
                    dve.wait_ge(h_hi, n + 1)
                    v.tensor_tensor(lh[:, k, :], prod[:, k, :], hh[:, k, :].bitcast(F32), ALU.subtract
                                    ).then_inc(h_lo, 1)
                    if f == 4:
                        x_low(j + 1, (s + 1) % UNROLL)
                        places(j + 1, r if s < UNROLL - 1 else r + 1, (s + 1) % UNROLL)

            tiles(dve, tile)


def combine(nc, A, dram):
    with ExitStack() as ctx:
        def sb(name, shape, dt=F32):
            return ctx.enter_context(nc.sbuf_tensor(name, shape, dt))

        def sem(name):
            return ctx.enter_context(nc.semaphore(name))

        wt, eps_ln, x1 = A["wt"], A["eps_ln"], A["x1"]
        RB = 4
        both = sb("got", [P, RB, TT, 2 * D])
        z1 = sb("z1", [P, RB, TT, D])
        z = sb("z", [P, RB, TT, D])
        res = sb("res", [P, RB, TT, D])
        st = sb("cst", [P, RB, TT, 6])
        mv = sb("cmv", [P, RB, TT, 2])
        lnv = sb("clnv", [P, RB, TT])
        rr = sb("crr", [P, RB, TT])
        shift = sb("shift", [P, RB, TT])

        both_in = [sem(f"both_in{n}") for n in range(RB)]
        out_done = [sem(f"out_done{n}") for n in range(RB)]
        first_ready, summed, var_ready, ln_done, rstd_ready, shifted, normed, res_ready = (
            sem(n) for n in ("first_ready", "csummed", "cvar_ready", "cln_done", "crstd_ready", "shifted", "normed", "res_ready"))
        chain, passed = sem("cchain"), sem("cpassed")

        block = ctx.enter_context(nc.Block())

        def batches(eng, batch):
            for n in range(RB):
                batch(n, 0, n)
            with eng.Fori(1, B // RB) as r:
                for n in range(RB):
                    batch(r * RB + n, r, n)

        @block.sync
        def _(sp):
            def batch(b, r, n):
                if not (isinstance(r, int) and r == 0):
                    sp.wait_ge(summed, b - RB + 1)
                sp.dma_start(both[:, n, :, :], dram["ys"][bass.ds(b * 2 * S, 2 * S), :]
                             .rearrange("(t p k) n -> p t (k n)", p=P, k=2)).then_inc(both_in[n], 16)

            batches(sp, batch)

        @block.gpsimd
        def _(pool):
            def batch(b, r, n):
                pool.wait_ge(normed, b + 1)
                nc.gpsimd.tensor_tensor(res[:, n, :, :], res[:, n, :, :], x1[:, bass.ds(b * TT, TT), :], ALU.add
                                        ).then_inc(res_ready, 1)

            pool.wait_ge(A["x1_in"], 16)
            batches(pool, batch)

        @block.scalar
        def _(act):
            nc.scalar.preload_act_table_set("natural_log_exp_and_others")

            def first(b, r, n):
                act.wait_ge(both_in[n], 16 * (r + 1))
                if not (isinstance(r, int) and r == 0):
                    act.wait_ge(summed, b - RB + 1)
                act.sem_inc(passed, 1)
                for t in range(TT):
                    last = nc.scalar.activation(z1[:, n, t, :], both[:, n, t, 0:D], ACT.Copy,
                                                scale=wt[:, bass.ds(b * TT + t, 1), 0])
                last.then_inc(first_ready, 1)

            def rstd(b, n):
                act.wait_ge(var_ready, b + 1)
                nc.scalar.activation(lnv[:, n, :], mv[:, n, :, 1], ACT.Ln, bias=eps_ln[:, :]).then_inc(ln_done, 1)
                act.wait_ge(ln_done, b + 1)
                nc.scalar.activation(rr[:, n, :], lnv[:, n, :], ACT.Exp, scale=-0.5).then_inc(rstd_ready, 1)

            def norm(b, r, n):
                act.wait_ge(shifted, b + 1)
                if not (isinstance(r, int) and r == 0):
                    act.wait_ge(out_done[n], 16 * r)
                for t in range(TT):
                    last = nc.scalar.activation(res[:, n, t, :], z[:, n, t, :], ACT.Identity,
                                                scale=rr[:, n, t:t + 1], bias=shift[:, n, t:t + 1])
                last.then_inc(normed, 1)

            def store(b, n):
                act.wait_ge(res_ready, b + 1)
                act.dma_start(dram["out"][bass.ds(b * S, S), :].rearrange("(t p) n -> p t n", p=P), res[:, n, :, :]
                              ).then_inc(out_done[n], 16)

            def batch(b, r, n):
                first(b, r, n)
                if not (isinstance(b, int) and b < 1):
                    rstd(b - 1, (n - 1) % RB)
                if not (isinstance(b, int) and b < 2):
                    norm(b - 2, r if n > 1 else r - 1, (n - 2) % RB)
                if not (isinstance(b, int) and b < 3):
                    store(b - 3, (n - 3) % RB)

            batches(act, batch)
            rstd(B - 1, RB - 1)
            for b in (B - 2, B - 1):
                norm(b, b // RB, b % RB)
                store(b - 1, (b - 1) % RB)
            store(B - 1, RB - 1)
            for n in range(RB):
                act.wait_ge(out_done[n], 16 * (B // RB))

        @block.vector
        def _(dve):
            v = nc.vector

            def batch(b, r, n):
                s = Steps(dve, chain, 1, b)
                dve.wait_ge(first_ready, b + 1)
                for t in range(TT):
                    last = v.scalar_tensor_tensor(z[:, n, t, :], both[:, n, t, D:2 * D], wt[:, bass.ds(b * TT + t, 1), 1],
                                                  z1[:, n, t, :], ALU.mult, ALU.add)
                last.then_inc(summed, 1)
                dve.wait_ge(summed, b + 1)
                dve.sem_inc(passed, 1)
                for t in range(TT):
                    last = v.bn_stats(st[:, n, t, :], z[:, n, t, :])
                s.did(last)
                s.settle()
                dve.sem_inc(passed, 1)
                for t in range(TT):
                    last = v.bn_aggr(mv[:, n, t, :], st[:, n, t, :])
                last.then_inc(var_ready, 1)
                if not (isinstance(b, int) and b == 0):
                    shifts(b - 1, (n - 1) % RB)

            def shifts(b, n):
                dve.wait_ge(rstd_ready, b + 1)
                if not (isinstance(b, int) and b < RB):
                    dve.wait_ge(normed, b - RB + 1)
                v.scalar_tensor_tensor(shift[:, n, :], mv[:, n, :, 0], -1.0, rr[:, n, :], ALU.mult, ALU.mult
                                       ).then_inc(shifted, 1)

            batches(dve, batch)
            shifts(B - 1, RB - 1)


def sandwich(nc, dram, out):
    for name, rows, cols in (("x1", NTOK, D), ("xs", ROWS, XW), ("ys", DUMP + MT, D)):
        dram[name] = nc.dram_tensor(name, [rows, cols], F32, kind="Internal").ap()
    dram["out"] = out
    with ExitStack() as ctx:
        def sb(name, shape, dt=F32):
            return ctx.enter_context(nc.sbuf_tensor(name, shape, dt))

        A = {"const": sb("const", [P, NCONST]), "eps_ln": sb("eps_ln", [P, 1]), "eps_rms": sb("eps_rms", [P, 1]),
             "counts": sb("counts", [P, E]), "own_f": sb("own_f", [P, NT1, MT // P]), "top2": sb("top2", [P, 2 * TT * B]),
             "wt": sb("wt", [P, B * TT, 2]),
             "row_i": sb("row_i", [P, NT1], I32),
             "expert_i": sb("expert_i", [P, NT1], I32),
             "fresh_i": sb("fresh_i", [P, NT1], I32),
             "live_i": sb("live_i", [P, NT1], I32),
             "round_i": sb("round_i", [P, 1], I32),
             "table_ready": ctx.enter_context(nc.semaphore("table_ready")),
             "raw_w1": sb("raw_w1", [P, DH, F]), "raw_w3": sb("raw_w3", [P, DH, F]), "raw_w2": sb("raw_w2", [P, FC, D]),
             "raw_in": [ctx.enter_context(nc.semaphore(f"raw_in{q}")) for q in range(NQ)],
             "scattered": ctx.enter_context(nc.semaphore("scattered")),
             "const_in": ctx.enter_context(nc.semaphore("const_in")),
             "eps_set": ctx.enter_context(nc.semaphore("eps_set"))}
        attend(nc, A, dram)
        A["x1"], A["x1_in"] = sb("x1s", [P, B * TT, D]), ctx.enter_context(nc.semaphore("x1_in"))
        experts(nc, A, dram)
        combine(nc, A, dram)


def constants():
    c = np.zeros((P, NCONST), np.float32)

    def put(name, x):
        at, n = CONST[name]
        c[:, at:at + n] = x

    r = np.arange(P)
    put("ident", np.eye(P, dtype=np.float32))
    put("before", (r[:, None] < r[None, :]).astype(np.float32))
    put("ones", 1.0)
    put("mask0", np.where(r[None, :] >= r[:, None], 0.0, NEG))
    d = np.arange(P + WIN)[None, :] - r[:, None]
    put("mask1", np.where((d >= 0) & (d < WIN), 0.0, NEG))
    for l, turn in enumerate((1e6, 1e4)):
        inv = np.float32(1.0) / np.float32(turn) ** (np.arange(0, HD, 2, dtype=np.float32) / np.float32(HD))
        ang = np.arange(S, dtype=np.float32)[:, None] * inv[None, :].astype(np.float32)
        cos, sin = np.cos(ang), np.sin(ang)
        both = np.stack([cos, cos], -1), np.stack([-sin, sin], -1)
        for name, x in zip((f"cos{l}", f"sin{l}"), both):
            put(name, x.reshape(TT, P, HD).transpose(1, 0, 2).reshape(P, TT * HD))
    put("expert", np.arange(E)[None, :])
    put("region", np.arange(E)[None, :] * REG)
    put("tile", np.arange(NTILES + 2)[None, :])
    put("place", 2 * (np.arange(TT)[None, :] * P + r[:, None]))
    put("lane", np.arange(MT // P)[None, :] * P + r[:, None])
    put("dump", DUMP + np.arange(MT // P)[None, :] * P + r[:, None])
    return c


_ATTN = ["norm1_w", "norm2_w", "g_wq", "g_kv_down", "g_k_up", "g_v_up", "g_wo", "l_wq", "l_wk", "l_wv", "l_wo"]


def kernel(**inputs):
    import numpy as _np
    import concourse.bacc as _bacc
    from concourse.bass_utils import run_bass_kernel_spmd as _run

    arrays = {"x": _np.asarray(inputs["L0_attn_hidden"]).reshape(NTOK, D), "const": constants()}
    for n in _ATTN:
        arrays[n] = _np.asarray(inputs["L0_attn_" + n])
    arrays["gate_w"] = _np.asarray(inputs["L0_ffn_gate_w"])
    for n in ("w1", "w3"):
        arrays[n] = _np.asarray(inputs["L0_ffn_" + n]).reshape(E * D, F)
    arrays["w2"] = _np.asarray(inputs["L0_ffn_w2"]).reshape(E * F, D)
    arrays = {n: _np.ascontiguousarray(a) for n, a in arrays.items()}
    nc = _bacc.Bacc("TRN2", target_bir_lowering=False, num_devices=1)
    dram = {n: nc.dram_tensor(f"in_{n}", a.shape, F32, kind="ExternalInput").ap() for n, a in arrays.items()}
    out = nc.dram_tensor("out_0", (NTOK, D), F32, kind="ExternalOutput").ap()
    sandwich(nc, dram, out)
    r = _run(nc, [{f"in_{n}": a for n, a in arrays.items()}], core_ids=[0])
    return r.results[0]["out_0"].reshape(B, S, D)
```
